# Optimizing a Trainium2 kernel written in Bass

```python
import numpy as np
import jax
import jax.numpy as jnp

def _softmax(x, axis=-1):
    return jax.nn.softmax(x, axis=axis)

def _gelu(x):
    return jax.nn.gelu(x, approximate=True)

def _silu(x):
    return jax.nn.silu(x)

def _sigmoid(x):
    return jax.nn.sigmoid(x)

def _layernorm(x, axis=-1, eps=1e-05):
    m = jnp.mean(x, axis=axis, keepdims=True)
    v = jnp.var(x, axis=axis, keepdims=True)
    return (x - m) / jnp.sqrt(v + eps)

def _scatter_add(tgt, idx, src, axis=0):
    return tgt.at[idx].add(src)

def _segment_sum(src, seg, n):
    return jax.ops.segment_sum(src, seg, n)
kernel_name = 'mk_recurrent_d1_jaxref_r8_9545c3'

def setup_inputs(seed: int=0):
    np.random.seed(seed)
    _w = jnp.asarray

    def _L0_attn_setup():
        import jax, jax.numpy as jnp
        import numpy as np
        D_MODEL = 256
        NUM_HEADS = 16
        D_HEAD = D_MODEL // NUM_HEADS
        SCALE = 1.0 / np.sqrt(D_HEAD)
        key = jax.random.key(seed)
        ks = jax.random.split(key, 5)
        B, S = (4, 256)
        qkv = jax.random.normal(ks[0], (B, S, D_MODEL), dtype=jnp.float32)
        in_proj = jax.random.normal(ks[1], (3 * D_MODEL, D_MODEL), dtype=jnp.float32) * (1.0 / np.sqrt(D_MODEL))
        in_proj_bias = jnp.zeros((3 * D_MODEL,), dtype=jnp.float32)
        out_w = jax.random.normal(ks[2], (D_MODEL, D_MODEL), dtype=jnp.float32) * (1.0 / np.sqrt(D_MODEL))
        out_b = jnp.zeros((D_MODEL,), dtype=jnp.float32)
        alibi_slopes = (2.0 ** (-jnp.linspace(1.0, 8.0, NUM_HEADS))).astype(jnp.float32)
        return {'qkv': qkv, 'in_proj': in_proj, 'in_proj_bias': in_proj_bias, 'out_w': out_w, 'out_b': out_b, 'alibi_slopes': alibi_slopes}
    _L0_attn_in = _L0_attn_setup()

    def _L0_ffn_setup():
        import jax, jax.numpy as jnp
        import numpy as np
        B, S, H = (2, 256, 256)
        E, K, F = (32, 4, 176)
        FS = 704
        EPS = 1e-06
        CAP = 128
        key = jax.random.key(seed)
        ks = jax.random.split(key, 10)
        s = 0.02
        return {'hidden_states': jax.random.normal(ks[0], (B, S, H), jnp.float32), 'w_norm': 1.0 + 0.02 * jax.random.normal(ks[1], (H,), jnp.float32), 'w_router': s * jax.random.normal(ks[2], (H, E), jnp.float32), 'w_gate': s * jax.random.normal(ks[3], (E, H, F), jnp.float32), 'w_up': s * jax.random.normal(ks[4], (E, H, F), jnp.float32), 'w_down': s * jax.random.normal(ks[5], (E, F, H), jnp.float32), 'sw_gate': s * jax.random.normal(ks[6], (H, FS), jnp.float32), 'sw_up': s * jax.random.normal(ks[7], (H, FS), jnp.float32), 'sw_down': s * jax.random.normal(ks[8], (FS, H), jnp.float32), 'w_shared_gate': s * jax.random.normal(ks[9], (H, 1), jnp.float32)}
    _L0_ffn_in = _L0_ffn_setup()
    _d = {'L0_attn_qkv': _L0_attn_in['qkv'], 'L0_attn_in_proj': _L0_attn_in['in_proj'], 'L0_attn_in_proj_bias': _L0_attn_in['in_proj_bias'], 'L0_attn_out_w': _L0_attn_in['out_w'], 'L0_attn_out_b': _L0_attn_in['out_b'], 'L0_attn_alibi_slopes': _L0_attn_in['alibi_slopes'], 'L0_ffn_w_norm': _L0_ffn_in['w_norm'], 'L0_ffn_w_router': _L0_ffn_in['w_router'], 'L0_ffn_w_gate': _L0_ffn_in['w_gate'], 'L0_ffn_w_up': _L0_ffn_in['w_up'], 'L0_ffn_w_down': _L0_ffn_in['w_down'], 'L0_ffn_sw_gate': _L0_ffn_in['sw_gate'], 'L0_ffn_sw_up': _L0_ffn_in['sw_up'], 'L0_ffn_sw_down': _L0_ffn_in['sw_down'], 'L0_ffn_w_shared_gate': _L0_ffn_in['w_shared_gate']}
    _x0 = _d['L0_attn_qkv']
    _d['L0_attn_qkv'] = jax.random.normal(jax.random.fold_in(jax.random.key(seed), 1), (2, 1024, 256), dtype=_x0.dtype)
    del _x0
    return _d

def reference(L0_attn_qkv, L0_attn_in_proj, L0_attn_in_proj_bias, L0_attn_out_w, L0_attn_out_b, L0_attn_alibi_slopes, L0_ffn_w_norm, L0_ffn_w_router, L0_ffn_w_gate, L0_ffn_w_up, L0_ffn_w_down, L0_ffn_sw_gate, L0_ffn_sw_up, L0_ffn_sw_down, L0_ffn_w_shared_gate):

    def _L0_attn_ref(qkv, in_proj, in_proj_bias, out_w, out_b, alibi_slopes):
        import jax, jax.numpy as jnp
        import numpy as np
        D_MODEL = 256
        NUM_HEADS = 16
        D_HEAD = D_MODEL // NUM_HEADS
        SCALE = 1.0 / np.sqrt(D_HEAD)
        B, S, D = qkv.shape
        H, Dh = (NUM_HEADS, D_HEAD)
        proj = qkv @ in_proj.T + in_proj_bias
        q, k, v = jnp.split(proj, 3, axis=-1)
        q = q.reshape(B, S, H, Dh).transpose(0, 2, 1, 3)
        k = k.reshape(B, S, H, Dh).transpose(0, 2, 1, 3)
        v = v.reshape(B, S, H, Dh).transpose(0, 2, 1, 3)
        scores = jnp.einsum('bhqd,bhkd->bhqk', q, k) * SCALE
        pos = jnp.arange(S)
        rel = (pos[None, :] - pos[:, None]).astype(scores.dtype)
        scores = scores + rel[None, None] * alibi_slopes[None, :, None, None]
        causal_mask = pos[None, :] > pos[:, None]
        scores = jnp.where(causal_mask[None, None], -jnp.inf, scores)
        attn = jnp.maximum(jax.nn.softmax(scores, axis=-1), 1e-10)
        attended = jnp.einsum('bhqk,bhkd->bhqd', attn, v)
        attended = attended.transpose(0, 2, 1, 3).reshape(B, S, D)
        return attended @ out_w.T + out_b

    def _L0_ffn_ref(hidden_states, w_norm, w_router, w_gate, w_up, w_down, sw_gate, sw_up, sw_down, w_shared_gate):
        import jax, jax.numpy as jnp
        import numpy as np
        B, S, H = (2, 256, 256)
        E, K, F = (32, 4, 176)
        FS = 704
        EPS = 1e-06
        CAP = 128
        inp = hidden_states
        xf = inp.astype(jnp.float32)
        var = jnp.mean(xf * xf, axis=-1, keepdims=True)
        x = (w_norm * (xf * jax.lax.rsqrt(var + EPS))).astype(inp.dtype)
        Bq, Sq, Hq = x.shape
        x = x.reshape(-1, Hq)
        T = Bq * Sq
        logits = x @ w_router
        probs = jax.nn.softmax(logits.astype(jnp.float32), axis=-1)
        w_topk, sel = jax.lax.top_k(probs, K)
        w_topk = w_topk.astype(x.dtype)
        flat_e = sel.reshape(-1)
        order = jnp.argsort(flat_e)
        sorted_e = flat_e[order]
        counts = jnp.zeros((E,), jnp.int32).at[flat_e].add(1)
        starts = jnp.cumsum(counts) - counts
        pos = jnp.arange(T * K) - starts[sorted_e]
        tok = order // K
        valid = pos < CAP
        dest = jnp.where(valid, pos, CAP)
        buf = jnp.zeros((E, CAP + 1, Hq), x.dtype).at[sorted_e, dest].set(x[tok])
        buf = buf[:, :CAP]
        g = jnp.einsum('ech,ehf->ecf', buf, w_gate)
        u = jnp.einsum('ech,ehf->ecf', buf, w_up)
        y = jnp.einsum('ecf,efh->ech', jax.nn.silu(g) * u, w_down)
        wv = w_topk.reshape(-1)[order] * valid.astype(x.dtype)
        gath = y[sorted_e, jnp.minimum(pos, CAP - 1)]
        out = jnp.zeros((T, Hq), x.dtype).at[tok].add(gath * wv[:, None])
        sh = jax.nn.silu(x @ sw_gate) * (x @ sw_up) @ sw_down
        sh = jax.nn.sigmoid(x @ w_shared_gate) * sh
        out = out + sh
        return inp + out.reshape(Bq, Sq, Hq)
    x = L0_attn_qkv
    xn = _layernorm(x, axis=-1)
    s = _L0_attn_ref(xn, L0_attn_in_proj, L0_attn_in_proj_bias, L0_attn_out_w, L0_attn_out_b, L0_attn_alibi_slopes)
    g = _silu(_L0_ffn_ref(xn, L0_ffn_w_norm, L0_ffn_w_router, L0_ffn_w_gate, L0_ffn_w_up, L0_ffn_w_down, L0_ffn_sw_gate, L0_ffn_sw_up, L0_ffn_sw_down, L0_ffn_w_shared_gate))
    x = x + s * g
    return x

_drawn_inputs = setup_inputs


def setup_inputs(seed=0):
    import zlib

    import numpy as np

    out = dict(_drawn_inputs(seed))
    spreads = {'L0_attn_in_proj_bias': (0.0, 0.1), 'L0_attn_out_b': (0.0, 0.1)}
    factors = {'L0_ffn_w_norm': 8.0,
     'L0_ffn_w_router': 8.0,
     'L0_ffn_w_gate': 8.0,
     'L0_ffn_w_up': 8.0,
     'L0_ffn_w_down': 8.0,
     'L0_ffn_sw_gate': 8.0,
     'L0_ffn_sw_up': 8.0,
     'L0_ffn_sw_down': 8.0,
     'L0_ffn_w_shared_gate': 8.0}
    for name, (base, spread) in spreads.items():
        noise = np.random.default_rng([zlib.crc32(name.encode()), seed]).standard_normal(out[name].shape)
        drawn = base * np.exp(spread * noise) if base else spread * noise
        out[name] = jnp.asarray(drawn.astype(out[name].dtype))
    for name, factor in factors.items():
        out[name] = (out[name] * factor).astype(out[name].dtype)
    return out
```

```python
from contextlib import ExitStack

import concourse.bass as bass
from concourse import mybir

F32 = mybir.dt.float32
BF16 = mybir.dt.bfloat16
I32 = mybir.dt.int32
U32 = mybir.dt.uint32
ALU = mybir.AluOpType
ACT = mybir.ActivationFunctionType
AX_X = mybir.AxisListType.X

P = 128
B, S, D = 2, 1024, 256
T = B * S
NT = T // P
NQ = S // P
KC = D // P
H = 16
DH = D // H
E, TOPK, F, CAP = 32, 4, 176, 128
FE = F // 2
FS = 704
NF = -(-FS // P)
FSZ = [min(P, FS - P * c) for c in range(NF)]
SCALE = float(DH) ** -0.5
FLOOR = 1e-10
MASK = -1e30
LEAST = -80.0
LN_EPS, RMS_EPS = 1e-5, 1e-6
UNITS = B * H
SLOTS = 4
SPLIT_ROWS = 6 * DH
SHIFT = SPLIT_ROWS
ROWS = SHIFT + 3 + 12
BLK = 256
O_BANK, AUX = 5, 6
PAD = 16

CB, TR, SA, GU, CA, SB, DN = range(7)
AUX_TASKS = 7
W0, XN0, XF0, R0, QK0, POS0, QK1, V0, U0 = 0, 4, 12, 20, 22, 30, 31, 39, 47
PRO_TASKS = 48


def step_tile(s):
    return NQ - 1 - s


P1_BANK = [0, 2, 0, 2, 0, 1, 0, 2]
P2_BANK = [4, 4, 4, 4, 3, 3, 3, 3]


def prob_offset(s):
    return s * (s + 1) // 2 * P


def build(nc, x, in_proj, in_b, out_w, out_b, slopes, w_norm, w_router, w_gate, w_up, w_down,
          sw_gate, sw_up, sw_down, w_sg, out):
    ctx = ExitStack()
    with ctx:
        def sb(name, shape, dt=F32):
            return ctx.enter_context(nc.sbuf_tensor(name, shape, dt))

        def sem(name):
            return ctx.enter_context(nc.semaphore(name))

        def dram(name, shape, dt=F32):
            return nc.dram_tensor(name, shape, dt, kind="Internal").ap()

        xf_rows = dram("xf_rows", (T, D))
        moe_rows = dram("moe_rows", (T + CAP, D))
        slot_table = dram("slot_table", (CAP * E, 4), I32)
        q_parts = dram("q_parts", (3, B * D, S), BF16)
        k_parts = dram("k_parts", (3, B * D, S), BF16)
        q_alibi = dram("q_alibi", (UNITS, 15, S), BF16)
        k_alibi = dram("k_alibi", (UNITS, 15, S), BF16)
        att_rows = dram("att_rows", (B * D, S))

        XN = sb("XN", [P, NT, D])
        STACKS = sb("STACKS", [P, 2 * SLOTS, S], BF16)
        stf = STACKS[:, :, :].rearrange("p a s -> p (a s)").bitcast(F32)
        XF = stf.rearrange("p (t d) -> p t d", d=D)
        XNT = sb("XNT", [P, KC, T])
        XFT = sb("XFT", [P, KC, T])
        SH = XNT[:, :, :].rearrange("p a (t d) -> p (a t) d", d=D)
        ATTS = stf.rearrange("p (b a s) -> p b a s", b=B, a=KC)
        VS = sb("VS", [P, UNITS, NQ * DH])
        PB = sb("PB", [P, 2, 36 * P])
        pbf = PB[:, :, :].rearrange("p a n -> p (a n)")
        OH = pbf[:, 0:2048].rearrange("p (t k e) -> p t k e", t=NT, k=TOPK)
        PROD = pbf[:, 2048:4096].rearrange("p (t k e) -> p t k e", t=NT, k=TOPK)
        X = pbf[:, 0:T * D // P].rearrange("p (t d) -> p t d", d=D)
        INW = pbf[:, 0:1536].rearrange("p (a d) -> p a d", a=6)
        OW = pbf[:, 2048:2560].rearrange("p (a d) -> p a d", a=2)
        QV = [pbf[:, 4096 + 512 * r:4096 + 512 * (r + 1)] for r in range(3)]
        SPL = [pbf[:, 5632 + 768 * r:5632 + 768 * (r + 1)].bitcast(BF16).rearrange("p (a t) -> p a t", a=3)
               for r in range(3)]
        QS = [STACKS[:, r, :] for r in range(SLOTS)]
        KS = [STACKS[:, SLOTS + r, :] for r in range(SLOTS)]
        WG = [sb(f"WG{r}", [P, KC, F]) for r in range(SLOTS)]
        WU = [sb(f"WU{r}", [P, KC, F]) for r in range(SLOTS)]
        WD = [sb(f"WD{r}", [FE, 2, D]) for r in range(SLOTS)]
        SWG = sb("SWG", [P, KC, FS])
        SWU = sb("SWU", [P, KC, FS])
        SWD = sb("SWD", [P, NF, D])
        WIT = sb("WIT", [P, KC, 3 * D + PAD])
        OWT = sb("OWT", [P, KC, D])
        RW = sb("RW", [P, KC, E + 1])
        WN = sb("WN", [P, D])
        BV = sb("BV", [P, D])
        OB = sb("OB", [P, D])
        BQK = sb("BQK", [P, 4])
        BQS = sb("BQS", [P, 4])
        BVR = sb("BVR", [1, D + PAD])
        CNT = sb("CNT", [1, B, NQ])
        IDF = sb("IDF", [P, P])
        IDB = sb("IDB", [P, P], BF16)
        MQ = sb("MQ", [P, P], BF16)
        MK = sb("MK", [P, P], BF16)
        LT = sb("LT", [P, P], BF16)
        ONEB = sb("ONEB", [P, P], BF16)
        SL = sb("SL", [H, 1])
        SLR = sb("SLR", [H, 2])
        SLB = sb("SLB", [H, 3], BF16)
        SLP = sb("SLP", [H, 3])
        vsb = VS[0:H, :, :].rearrange("p u n -> p (u n)").bitcast(BF16).rearrange("p (a s) -> p a s", s=S)
        SROW, IROW, ONER = vsb[:, 0:3, :], vsb[:, 3:7, :], vsb[:, 7, :]
        BNS = sb("BNS", [P, NT, 6])
        MV = sb("MV", [P, NT, 2])
        SS = sb("SS", [P, NT])
        ET = sb("ET", [P, 2, BLK])
        SQJ = ET
        NRM = sb("NRM", [P, 6, NT])
        NR2 = sb("NR2", [P, 6, NT])
        LG = sb("LG", [P, NT, E + 1])
        V8 = sb("V8", [P, NT, 8])
        I8 = sb("I8", [P, NT, 8], U32)
        LS0 = pbf[:, 7936:8448].rearrange("p (t e) -> p t e", e=E)
        LE = pbf[:, 8448:8960].rearrange("p (t e) -> p t e", e=E)
        W4 = sb("W4", [P, NT, TOPK])
        W4E = sb("W4E", [P, NT, TOPK])
        ZS = sb("ZS", [P, NT])
        ZR = sb("ZR", [P, NT])
        SGE = sb("SGE", [P, NT])
        SG1 = sb("SG1", [P, NT])
        SG = sb("SG", [P, NT])
        IO32 = sb("IO32", [P, E])
        IDXF = sb("IDXF", [P, NT, TOPK])
        MB = sb("MB", [P, NT, E], BF16)
        MC = sb("MC", [P, NT, E], BF16)
        PK = sb("PK", [P, NT, TOPK])
        BAD = sb("BAD", [P, NT, TOPK])
        DST = sb("DST", [P, NT, TOPK])
        DST2 = sb("DST2", [P, NT, TOPK])
        DI = sb("DI", [P, TOPK, NT], I32)
        RWS = sb("RWS", [P, NT, TOPK, 4], I32)
        TI = sb("TI", [P, E, 4], I32)
        TABS = sb("TABS", [P, E * 4], I32)
        TS = sb("TS", [P, KC, NT])
        XS = sb("XS", [P, KC, B, NQ])
        XS2 = sb("XS2", [P, KC, B, NQ])
        UL = sb("UL", [P, UNITS, 2])
        NEGM = sb("NEGM", [P, 2, NQ])
        LSUM = sb("LSUM", [P, 2, NQ])
        LNL = sb("LNL", [P, 2, 4])
        CC = sb("CC", [P, 2, 4])
        CR = sb("CR", [P, 2, 2, 4])
        C3 = sb("C3", [P, 2, 4, 3], BF16)
        VH = sb("VH", [P, 2, NQ, 2 * DH])
        OEV = sb("OEV", [P, SLOTS, 2, P])
        XE = sb("XE", [P, 2, D])
        XET = sb("XET", [P, KC, P])
        IDX = sb("IDX", [P, SLOTS, 4], I32)
        RT = sb("RT", [P, 3, BLK])
        HE = sb("HE", [FE, 2, CAP])
        HS = sb("HS", [P, NF, BLK])
        YE = sb("YE", [P, 2, D])
        ZROW = HS[0:H, 0:2, :].rearrange("p a n -> p (a n)").bitcast(BF16)
        XFB = sb("XFB", [P, KC, BLK])
        SGB = sb("SGB", [P, 2])

        PSB = ctx.enter_context(nc.psum_tensor("PSB", [P, 8, 512], F32))
        psf = PSB[:, :, :].rearrange("p a n -> p (a n)")

        x_loaded = [sem(f"x_loaded{g}") for g in range(4)]
        w_loaded = sem("w_loaded")
        rw_loaded = sem("rw_loaded")
        row_loaded = sem("row_loaded")
        sw_loaded = sem("sw_loaded")
        slope_loaded = sem("slope_loaded")
        const_ready = sem("const_ready")
        mask_ready = sem("mask_ready")
        pool_self = sem("pool_self")
        dve_self = sem("dve_self")
        xn_ready = sem("xn_ready")
        xf_ready = sem("xf_ready")
        stat_ready = sem("stat_ready")
        ss_ready = sem("ss_ready")
        sqrt_ready = sem("sqrt_ready")
        pro_ready = [sem(f"pro_ready{b}") for b in range(8)]
        pro_free = [sem(f"pro_free{b}") for b in range(8)]
        qv_ready = sem("qv_ready")
        split_ready = sem("split_ready")
        split_stored = [sem(f"split_stored{r}") for r in range(3)]
        alibi_ready = sem("alibi_ready")
        slope_rows_ready = sem("slope_rows_ready")
        int_rows_ready = sem("int_rows_ready")
        alibi_stored = sem("alibi_stored")
        router_shifted = sem("router_shifted")
        router_exp = sem("router_exp")
        onehot_ready = sem("onehot_ready")
        dest_ready = sem("dest_ready")
        table_tile = sem("table_tile")
        table_cleared = sem("table_cleared")
        token_ids = sem("token_ids")
        scattered = sem("scattered")
        table_loaded = sem("table_loaded")
        xf_stored = sem("xf_stored")
        moe_started = sem("moe_started")
        tsum_ready = sem("tsum_ready")
        held = sem("held")
        stack_loaded = [sem(f"stack_loaded{r}") for r in range(SLOTS)]
        expert_loaded = [sem(f"expert_loaded{r}") for r in range(SLOTS)]
        p1_ready = sem("p1_ready")
        max_ready = sem("max_ready")
        exp1_done = sem("exp1_done")
        p2_ready = sem("p2_ready")
        exp2_done = sem("exp2_done")
        clamp_done = sem("clamp_done")
        pv_done = sem("pv_done")
        v_ready = sem("v_ready")
        o_evacuated = sem("o_evacuated")
        o_stored = [sem(f"o_stored{r}") for r in range(SLOTS)]
        ln_ready = sem("ln_ready")
        c_chain = sem("c_chain")
        c_parts_ready = sem("c_parts_ready")
        c_rows_ready = sem("c_rows_ready")
        aux_ready = [sem(f"aux_ready{b}") for b in range(2)]
        shared_out = sem("shared_out")
        gate_ready = sem("gate_ready")
        exp3_ready = sem("exp3_ready")
        silu_chain = sem("silu_chain")
        silu_done = sem("silu_done")
        block_ready = sem("block_ready")
        idx_ready = sem("idx_ready")
        xe_loaded = [sem(f"xe_loaded{r}") for r in range(2)]
        xet_ready = sem("xet_ready")
        ye_ready = sem("ye_ready")
        moe_added = sem("moe_added")
        ye_free = sem("ye_free")
        fin_loaded = sem("fin_loaded")
        fin_mm = sem("fin_mm")
        fin_z = sem("fin_z")
        fin_e = sem("fin_e")
        fin_chain = sem("fin_chain")
        fin_out = sem("fin_out")
        stored = sem("stored")

        def bank(n):
            return PSB[:, n % 8, :]

        class Link:

            def __init__(self, eng, semaphore):
                self.eng, self.semaphore, self.n = eng, semaphore, 0

            def __call__(self, ins):
                self.n += 1
                ins.then_inc(self.semaphore, 1)
                self.eng.wait_ge(self.semaphore, self.n)

        def hold(eng, semaphore, count):
            eng.wait_ge(semaphore, count)
            eng.sem_inc(held, 1)

        def unit(it, k, per=1, add=0):
            return it * (SLOTS * per) + (per * k + add)

        def turn(it, k, n, per=1, add=0):
            return it * (SLOTS // n * per) + (per * (k // n) + add)

        def aux(it, k, a):
            n = 1 + AUX_TASKS * k + a
            return n % 2, it * (SLOTS * AUX_TASKS // 2) + n // 2

        def aux_index(task, last):
            return task - 1 if last and task > CA else task

        def silu_index(k, task):
            return 10 * (k // SLOTS) + 3 * (k % SLOTS) + (0 if k % SLOTS == 3 else {SA: 0, GU: 1, SB: 2}[task])

        def silu(it, k, task):
            return it * 10 + silu_index(k, task)

        def aux_done(it, k, task):
            if task == CB:
                return c_rows_ready, unit(it, k, 2, 2)
            if task == CA:
                return c_rows_ready, unit(it, k, 2, 3)
            if task == TR:
                return xet_ready, unit(it, k, 1, 1)
            if task == DN:
                return ye_ready, unit(it, k, 1, 1)
            if task != GU and k % SLOTS == 3:
                return shared_out, turn(it, k, SLOTS, 2, 1 if task == SA else 2)
            return silu_done, silu(it, k, task) + 1

        def phases(eng, phase):
            phase(0, 0, True, False)
            with eng.Fori(0, UNITS // SLOTS - 1) as it:
                for k in range(1, SLOTS + 1):
                    phase(it, k, False, False)
            for k in range(1, SLOTS):
                phase(UNITS // SLOTS - 1, k, False, k == SLOTS - 1)

        block = ctx.enter_context(nc.Block())

        @block.sync
        def _(sp):
            x_t = x.rearrange("b (t p) d -> p (b t) d", p=P)
            for g in range(4):
                sp.dma_start(XN[:, 4 * g:4 * g + 4, :], x_t[:, 4 * g:4 * g + 4, :]).then_inc(x_loaded[g], 16)
            sp.dma_start(INW, in_proj.rearrange("(a p) d -> p a d", p=P)).then_inc(w_loaded, 16)
            sp.dma_start(OW, out_w.rearrange("(a p) d -> p a d", p=P)).then_inc(w_loaded, 16)
            sp.dma_start(SL[:, :], slopes.rearrange("(h a) -> h a", a=1)).then_inc(slope_loaded, 16)
            sp.dma_start(RW[:, :, 0:E], w_router.rearrange("(a p) e -> p a e", p=P)).then_inc(rw_loaded, 16)
            sp.dma_start(RW[:, :, E:E + 1], w_sg.rearrange("(a p) e -> p a e", p=P),
                         allow_slow_non_contiguous=True).then_inc(rw_loaded, 16)
            for tile, row in ((WN, w_norm), (BV, in_b[2 * D:3 * D]), (OB, out_b)):
                sp.dma_start(tile[:, :], row.partition_broadcast(P)).then_inc(row_loaded, 16)
            sp.dma_start(BVR[:, 0:D], in_b[2 * D:3 * D].rearrange("(a d) -> a d", a=1)).then_inc(row_loaded, 16)
            sp.dma_start(BQK[:, :], in_b[0:2 * D].rearrange("(m p) -> p m", p=P),
                         allow_slow_non_contiguous=True).then_inc(row_loaded, 16)
            sp.dma_start(SWG[:, :, :], sw_gate.rearrange("(a p) f -> p a f", p=P)).then_inc(sw_loaded, 16)
            sp.dma_start(SWU[:, :, :], sw_up.rearrange("(a p) f -> p a f", p=P)).then_inc(sw_loaded, 16)
            sp.dma_start(SWD[:, 0:NF - 1, :], sw_down[0:P * (NF - 1), :].rearrange("(a p) d -> p a d", p=P))\
                .then_inc(sw_loaded, 16)
            sp.dma_start(SWD[0:FSZ[-1], NF - 1, :], sw_down[P * (NF - 1):FS, :]).then_inc(sw_loaded, 16)
            sp.wait_ge(table_tile, 1)
            sp.dma_start(slot_table.rearrange("(c e) w -> c (e w)", e=E), TI[:, :, :].rearrange("p e w -> p (e w)"))\
                .then_inc(table_cleared, 16)
            sp.wait_ge(slope_rows_ready, 1)
            sp.wait_ge(int_rows_ready, 6)
            for b in range(B):
                qa = q_alibi[b * H:(b + 1) * H, 3:15].rearrange("h (p r) s -> h p r s", r=4)
                ka = k_alibi[b * H:(b + 1) * H, 3:15].rearrange("h (p r) s -> h p r s", r=4)
                for dst, r, src in ((qa, 0, None), (qa, 2, None), (ka, 1, None), (ka, 3, None),
                                    (ka, 0, 0), (ka, 2, 1), (qa, 1, 2), (qa, 3, 3)):
                    source = SROW if src is None else \
                        IROW[:, src:src + 1, :].broadcast_to([H, 3, S])
                    sp.dma_start(dst[:, :, r, :], source).then_inc(alibi_stored, 16)
                sp.dma_start(k_alibi[b * H:(b + 1) * H, 0:3], ONER.unsqueeze(1).broadcast_to([H, 3, S]))\
                    .then_inc(alibi_stored, 16)
                sp.dma_start(q_alibi[b * H:(b + 1) * H, 0:3], ZROW.unsqueeze(1).broadcast_to([H, 3, S]))\
                    .then_inc(alibi_stored, 16)
            sp.wait_ge(xn_ready, NT)
            sp.dma_start(moe_rows[0:T].rearrange("(t p) d -> p t d", p=P), XN[:, :, :]).then_inc(moe_started, 16)
            sp.dma_start(moe_rows[T:T + CAP], XN[:, 0, :]).then_inc(moe_started, 16)
            sp.wait_ge(xf_ready, NT)
            sp.dma_start(xf_rows.rearrange("(t p) d -> p t d", p=P), XF).then_inc(xf_stored, 16)
            for n in range(16):
                b, tg, m = n // 8, n // 4 % 2, n % 4
                parts = (q_parts if m < 2 else k_parts)
                r0 = b * D + m % 2 * P
                sp.wait_ge(split_ready, n + 1)
                sp.dma_start(parts[:, r0:r0 + P, tg * 512:(tg + 1) * 512].rearrange("a p t -> p a t"), SPL[n % 3])\
                    .then_inc(split_stored[n % 3], 16)
            for r in range(3):
                sp.wait_ge(split_stored[r], 16 * len(range(r, 16, 3)))
            sp.wait_ge(alibi_stored, 16 * 10 * B)
            sp.wait_ge(xf_stored, 16)
            for n in range(XF0, XF0 + 8):
                sp.wait_ge(pro_free[n % 8], n // 8 + 1)

            def load_unit(u_head, u, slot):
                for dst, rows in ((QS, q_parts), (KS, k_parts)):
                    one = (rows[:, bass.ds(u_head, DH), :])
                    t = dst[slot]
                    if dst is QS:
                        plan = ((0, 0), (1, 1), (2, 2), (3, 0), (4, 1), (5, 0))
                    else:
                        plan = ((0, 0), (1, 0), (2, 0), (3, 1), (4, 1), (5, 2))
                    for r, part in plan:
                        sp.dma_start(t[r * DH:(r + 1) * DH, :], one[part]).then_inc(stack_loaded[slot], 16)
                sp.dma_start(QS[slot][SHIFT:ROWS, :], q_alibi[bass.ds(u, 1)].rearrange("a r s -> (a r) s"))\
                    .then_inc(stack_loaded[slot], 16)
                sp.dma_start(KS[slot][SHIFT:ROWS, :], k_alibi[bass.ds(u, 1)].rearrange("a r s -> (a r) s"))\
                    .then_inc(stack_loaded[slot], 16)
                sp.dma_start(WG[slot][:, :, :], w_gate[bass.ds(u, 1)].rearrange("o (a p) f -> p (o a) f", p=P))\
                    .then_inc(expert_loaded[slot], 16)
                sp.dma_start(WU[slot][:, :, :], w_up[bass.ds(u, 1)].rearrange("o (a p) f -> p (o a) f", p=P))\
                    .then_inc(expert_loaded[slot], 16)
                sp.dma_start(WD[slot][:, :, :], w_down[bass.ds(u, 1)].rearrange("o (a p) d -> p (o a) d", p=FE))\
                    .then_inc(expert_loaded[slot], 16)

            for u in range(3):
                load_unit(u * DH, u, u)

            def phase(it, k, first, last):
                if first or not isinstance(it, int):
                    if not first:
                        hold(sp, p2_ready, unit(it, k, NQ))
                        bank_, before = aux(it, k - 1, DN)
                        hold(sp, aux_ready[bank_], before + 1)
                    load_unit(unit(it, k, DH, 3 * DH), unit(it, k, 1, 3), (k + 3) % SLOTS)
                if not first:
                    store_heads(it, k - 1)

            def store_heads(it, k):
                hold(sp, o_evacuated, unit(it, k, 1, 1))
                rows = att_rows[bass.ds(unit(it, k, DH), DH), :].rearrange("d (t q) -> d t q", q=P)
                for c in range(4):
                    sp.dma_start(rows[:, c:NQ - c:NQ - 1 - 2 * c, :], OEV[32 * c:32 * c + DH, k % SLOTS, :, :])\
                        .then_inc(o_stored[k % SLOTS], 16)

            for r in range(SLOTS):
                sp.sem_inc(o_stored[r], 64)
            phases(sp, phase)
            store_heads(UNITS // SLOTS - 1, SLOTS - 1)
            for r in range(SLOTS):
                sp.wait_ge(o_stored[r], 64 * (UNITS // SLOTS + 1))
            sp.dma_start(ATTS, att_rows.rearrange("(b a p) t -> p b a t", b=B, p=P)).then_inc(fin_loaded, 16)
            sp.wait_ge(pv_done, UNITS * NQ)
            sp.dma_start(X, x_t).then_inc(fin_loaded, 16)
            sp.wait_ge(moe_added, 16 * UNITS)
            sp.dma_start(XN[:, :, :], moe_rows[0:T].rearrange("(t p) d -> p t d", p=P)).then_inc(fin_loaded, 16)
            out_t = out.rearrange("b (t p) d -> p (b t) d", p=P)
            for g in range(NT // 2):
                sp.wait_ge(fin_out, g + 1)
                sp.dma_start(out_t[:, 2 * g:2 * g + 2, :], X[:, 2 * g:2 * g + 2, :]).then_inc(stored, 16)
            sp.wait_ge(stored, 16 * (NT // 2))

        @block.tensor
        def _(pe):
            def begin(n):
                if n >= 8:
                    pe.wait_ge(pro_free[n % 8], n // 8)
                return bank(n)

            pe.wait_ge(w_loaded, 32)
            pe.wait_ge(mask_ready, 5)
            for m in range(4):
                o = begin(W0 + m)
                for a in range(2):
                    for c in range(KC):
                        src = INW[:, 2 * m + a, c * P:(c + 1) * P] if m < 3 else OW[:, a, c * P:(c + 1) * P]
                        ins = pe.transpose(o[:, (2 * a + c) * P:(2 * a + c + 1) * P], src, IDF[:, :])
                ins.then_inc(pro_ready[(W0 + m) % 8], 1)
            for base, src_t, ready in ((XN0, XN, xn_ready), (XF0, XF, xf_ready)):
                for g in range(8):
                    o = begin(base + g)
                    pe.wait_ge(ready, 2 * g + 2)
                    for a in range(2):
                        for c in range(KC):
                            ins = pe.transpose(o[:, (2 * a + c) * P:(2 * a + c + 1) * P],
                                               src_t[:, 2 * g + a, c * P:(c + 1) * P], IDF[:, :])
                    ins.then_inc(pro_ready[(base + g) % 8], 1)
            pe.wait_ge(rw_loaded, 32)
            for g in range(2):
                o = begin(R0 + g)
                pe.wait_ge(pro_free[(XF0 + 4 * g + 3) % 8], (XF0 + 4 * g + 3) // 8 + 1)
                for q in range(4):
                    n = XF0 + 4 * g + q
                    pe.wait_ge(pro_free[n % 8], n // 8 + 1)
                for a in range(8):
                    t = 8 * g + a
                    for c in range(KC):
                        ins = pe.matmul(o[:, 64 * a:64 * a + E + 1], XFT[:, c, t * P:(t + 1) * P], RW[:, c, :],
                                        start=(c == 0), stop=(c == KC - 1))
                ins.then_inc(pro_ready[(R0 + g) % 8], 1)
            for n in range(W0, XF0):
                pe.wait_ge(pro_free[n % 8], n // 8 + 1)

            def qk(b):
                for j in range(8):
                    n = (QK0 if b == 0 else QK1) + j
                    tg, m = 2 * b + j // 4, j % 4
                    o = begin(n)
                    for c in range(KC):
                        ins = pe.matmul(o, WIT[:, c, m * P:(m + 1) * P], XNT[:, c, tg * 512:(tg + 1) * 512],
                                        start=(c == 0), stop=(c == KC - 1))
                    ins.then_inc(pro_ready[n % 8], 1)

            qk(0)
            o = begin(POS0)
            pe.wait_ge(onehot_ready, 1)
            pe.matmul(o, LT[:, :], MB[:, :, :].rearrange("p t e -> p (t e)"), start=True, stop=False)
            pe.matmul(o, ONEB[:, :], MC[:, :, :].rearrange("p t e -> p (t e)"), start=False, stop=True)\
                .then_inc(pro_ready[POS0 % 8], 1)
            qk(1)
            for g in range(8):
                o = begin(V0 + g)
                for a in range(2):
                    t = 2 * g + a
                    for c in range(KC):
                        ins = pe.matmul(o[:, a * D:(a + 1) * D], XNT[:, c, t * P:(t + 1) * P],
                                        WIT[:, c, 2 * D:3 * D], start=(c == 0), stop=(c == KC - 1))
                ins.then_inc(pro_ready[(V0 + g) % 8], 1)
            o = begin(U0)
            pe.wait_ge(tsum_ready, 1)
            pe.wait_ge(row_loaded, 80)
            pe.wait_ge(const_ready, 3)
            pe.wait_ge(int_rows_ready, 6)
            for h in range(H):
                for c in range(4):
                    oo = o[32 * c:32 * c + 32, 4 * h:4 * h + 4]
                    v0 = 2 * D + DH * h
                    for a in range(KC):
                        pe.matmul(oo, WIT[:, a, v0:v0 + 2 * DH], XS2[:, a, :, c:NQ - c:NQ - 1 - 2 * c],
                                  start=(a == 0), stop=False)
                    ins = pe.matmul(oo, BVR[:, DH * h:DH * h + 2 * DH], CNT[:, :, c:NQ - c:NQ - 1 - 2 * c],
                                    start=False, stop=True)
            ins.then_inc(pro_ready[U0 % 8], 1)
            for b in range(8):
                pe.wait_ge(pro_free[b], PRO_TASKS // 8)

            def pass1(it, k, s, warm):
                i = step_tile(s)
                slot = (k + 1) % SLOTS
                base = P1_BANK[s] * 512
                if s == 0:
                    pe.wait_ge(stack_loaded[slot], turn(it, k + 1, SLOTS, 14 * 16, 14 * 16))
                if warm:
                    if s == 0:
                        pe.wait_ge(exp1_done, unit(it, k, NQ, 7))
                    if s == 1:
                        pe.wait_ge(exp1_done, unit(it, k, NQ, 8))
                        pe.wait_ge(exp2_done, unit(it, k, NQ))
                if s >= 2:
                    pe.wait_ge(exp1_done, unit(it, k, NQ, NQ + {2: 1, 3: 2, 4: 3, 5: 3, 6: 5, 7: 4}[s]))
                w = P * (i + 1)
                q = QS[slot][0:ROWS, i * P:(i + 1) * P]
                for c0 in range(0, w, 512):
                    c1 = min(c0 + 512, w)
                    pe.matmul(psf[:, base + c0:base + c1], q, KS[slot][0:ROWS, c0:c1],
                              start=True, stop=(c1 < w), skip_group_check=True)
                pe.matmul(psf[:, base + i * P:base + w], IDB[:, :], MQ[:, :],
                          start=False, stop=True, skip_group_check=True).then_inc(p1_ready, 1)

            def pass2(it, k, s, last):
                j = step_tile(s)
                slot = k % SLOTS
                base = P2_BANK[s] * 512
                if s == 0:
                    pe.wait_ge(c_rows_ready, unit(it, k, 2, 1))
                if s == 4:
                    pe.wait_ge(c_rows_ready, unit(it, k, 2, 2))
                    if not last:
                        pe.wait_ge(exp1_done, unit(it, k, NQ, NQ + 4))
                pe.wait_ge(exp2_done, unit(it, k, NQ, s))
                w = P * (NQ - j)
                key = KS[slot][0:ROWS, j * P:(j + 1) * P]
                for c0 in range(0, w, 512):
                    c1 = min(c0 + 512, w)
                    pe.matmul(psf[:, base + c0:base + c1], key, QS[slot][0:ROWS, j * P + c0:j * P + c1],
                              start=True, stop=(c0 > 0), skip_group_check=True)
                pe.matmul(psf[:, base:base + P], IDB[:, :], MK[:, :],
                          start=False, stop=True, skip_group_check=True).then_inc(p2_ready, 1)

            def values(it, k, s):
                j = step_tile(s)
                par = k % 2
                if s == 0:
                    pe.wait_ge(o_evacuated, unit(it, k))
                    pe.wait_ge(v_ready, unit(it, k, 1, 1))
                pe.wait_ge(clamp_done, unit(it, k, NQ, s + 1))
                probs = PB[:, par, prob_offset(s):prob_offset(s) + (s + 1) * P].rearrange("p (t q) -> p t q", q=P)
                for c in (3, 2, 1, 0):
                    far = NQ - 1 - c
                    if far < j:
                        continue
                    o = PSB[32 * c:32 * c + 32, O_BANK, 0:2 * P].rearrange("p (t q) -> p t q", q=P)
                    v = VH[:, par, j, :]
                    if c >= j:
                        ins = pe.matmul(o, v, probs[:, c - j:far - j + 1:far - c, :],
                                        start=False, stop=(j == 0), skip_group_check=True)
                    else:
                        ins = pe.matmul(o[:, 1, :], v, probs[:, far - j, :],
                                        start=(far == j), stop=False, skip_group_check=True)
                ins.then_inc(pv_done, 1)

            def aux_begin(it, k, task, last=False):
                order = [t for t in range(AUX_TASKS) if not (last and t == CA)]
                a = order.index(task)
                if a >= 2:
                    pe.wait_ge(*aux_done(it, k, order[a - 2]))
                elif k >= 1:
                    pe.wait_ge(*aux_done(it, k - 1, SB if a == 0 else DN))
                elif a == 1:
                    pe.wait_ge(c_rows_ready, 1)
                b, _ = aux(it, k, a)
                return PSB[:, AUX + b, :], aux_ready[b]

            def c_transpose(o, ready, half, parts_count):
                pe.wait_ge(c_parts_ready, parts_count)
                for i in range(4):
                    ins = pe.transpose(o[SHIFT:SHIFT + 3, i * P // 2:(i + 1) * P // 2].bitcast(BF16),
                                       C3[:, half, i, :], IDB[:, :])
                ins.then_inc(ready, 1)

            def expert_transpose(it, k, o, ready):
                pe.wait_ge(xe_loaded[k % 2], turn(it, k, 2, 16, 16))
                for c in range(KC):
                    ins = pe.transpose(o[:, c * P:(c + 1) * P], XE[:, k % 2, c * P:(c + 1) * P], IDF[:, :])
                ins.then_inc(ready, 1)

            def expert_up(it, k, o, ready):
                slot = k % SLOTS
                pe.wait_ge(expert_loaded[slot], turn(it, k, SLOTS, 48, 48))
                pe.wait_ge(xet_ready, unit(it, k, 1, 1))
                for n, w in enumerate((WG[slot], WU[slot])):
                    for f in range(2):
                        for c in range(KC):
                            ins = pe.matmul(o[0:FE, (2 * n + f) * P:(2 * n + f + 1) * P],
                                            w[:, c, f * FE:(f + 1) * FE], XET[:, c, :],
                                            start=(c == 0), stop=(c == KC - 1))
                ins.then_inc(ready, 1)

            def expert_down(it, k, o, ready):
                slot = k % SLOTS
                pe.wait_ge(silu_done, silu(it, k, GU) + 1)
                for f in range(2):
                    ins = pe.matmul(o[:, 0:D], HE[:, f, :], WD[slot][:, f, :], start=(f == 0), stop=(f == 1))
                ins.then_inc(ready, 1)

            def shared(it, k, o, ready, which):
                slot = k % SLOTS
                if slot < 3:
                    ch = 2 * slot + which
                    m = FSZ[ch]
                    if ch == 0:
                        pe.wait_ge(block_ready, turn(it, k, SLOTS, 2, 2))
                    for n, w in enumerate((SWG, SWU)):
                        for c in range(KC):
                            ins = pe.matmul(o[0:m, n * BLK:(n + 1) * BLK], w[:, c, ch * P:ch * P + m], XFB[:, c, :],
                                            start=(c == 0), stop=(c == KC - 1))
                else:
                    if which == 0:
                        pe.wait_ge(silu_done, silu(it, k, GU))
                    for ch in range(NF):
                        m = FSZ[ch]
                        ins = pe.matmul(o[:, 0:D], HS[0:m, ch, which * P:(which + 1) * P], SWD[0:m, ch, :],
                                        start=(ch == 0), stop=(ch == NF - 1))
                ins.then_inc(ready, 1)

            for s in range(NQ):
                pass1(0, -1, s, False)
            c_transpose(PSB[:, AUX, :], aux_ready[0], 0, 1)
            pe.wait_ge(sw_loaded, 64)

            def phase(it, k, first, last):
                for s in range(NQ):
                    if not last:
                        pass1(it, k, s, True)
                    pass2(it, k, s, last)
                    if s >= 2:
                        values(it, k, s - 2)
                    elif not first:
                        values(it, k - 1, s + 6)
                    if s == 1:
                        c_transpose(*aux_begin(it, k, CB), 1, unit(it, k, 2, 2))
                    if s == 2:
                        expert_transpose(it, k, *aux_begin(it, k, TR))
                    if s == 3:
                        shared(it, k, *aux_begin(it, k, SA), 0)
                    if s == 4:
                        expert_up(it, k, *aux_begin(it, k, GU))
                    if s == 5 and not last:
                        c_transpose(*aux_begin(it, k, CA), 0, unit(it, k, 2, 3))
                    if s == 6:
                        shared(it, k, *aux_begin(it, k, SB, last), 1)
                    if s == 7:
                        expert_down(it, k, *aux_begin(it, k, DN, last))

            phases(pe, phase)
            values(UNITS // SLOTS - 1, SLOTS - 1, 6)
            values(UNITS // SLOTS - 1, SLOTS - 1, 7)
            pe.wait_ge(fin_loaded, 48)
            pe.wait_ge(o_evacuated, UNITS)
            pe.wait_ge(exp2_done, UNITS * NQ)
            for g in range(NT // 2):
                for a in range(2):
                    t = 2 * g + a
                    b, tb = t // NQ, t % NQ
                    for c in range(KC):
                        ins = pe.matmul(PSB[:, g, a * D:(a + 1) * D], ATTS[:, b, c, tb * P:(tb + 1) * P],
                                        OWT[:, c, :], start=(c == 0), stop=(c == KC - 1))
                ins.then_inc(fin_mm, 1)

        @block.scalar
        def _(act):
            def task(n):
                act.wait_ge(pro_ready[n % 8], n // 8 + 1)
                return bank(n)

            def evacuate(n, dst, src):
                act.activation(dst, src, ACT.Copy).then_inc(pro_free[n % 8], 1)

            act.wait_ge(stat_ready, 1)
            act.activation(NRM[:, 1, :], NRM[:, 0, :], ACT.Sqrt).then_inc(sqrt_ready, 1)
            for m in range(3):
                n = W0 + m
                evacuate(n, WIT[:, :, 2 * m * P:(2 * m + 2) * P].rearrange("p c (a m) -> p a c m", a=2),
                         task(n).rearrange("p (a c m) -> p a c m", a=2, c=KC))
            evacuate(W0 + 3, OWT[:, :, :].rearrange("p c (a m) -> p a c m", a=2),
                     task(W0 + 3).rearrange("p (a c m) -> p a c m", a=2, c=KC))
            for t in range(NT):
                act.wait_ge(xn_ready, t + 1)
                if t >= 2:
                    act.wait_ge(ss_ready, t - 1)
                act.activation(SQJ[:, t % 2, :], XN[:, t, :], ACT.Square, accum_out=SS[:, t:t + 1])\
                    .then_inc(ss_ready, 1)
            act.wait_ge(stat_ready, 2)
            act.activation(NR2[:, 1, :], NR2[:, 0, :], ACT.Sqrt).then_inc(sqrt_ready, 1)
            act.preload_act_table_set("natural_log_exp_and_others")
            for base, dst in ((XN0, XNT), (XF0, XFT)):
                for g in range(8):
                    n = base + g
                    evacuate(n, dst[:, :, 2 * g * P:(2 * g + 2) * P].rearrange("p c (a m) -> p a c m", a=2),
                             task(n).rearrange("p (a c m) -> p a c m", a=2, c=KC))
            for g in range(2):
                n = R0 + g
                evacuate(n, LG[:, 8 * g:8 * g + 8, :],
                         task(n).rearrange("p (t e) -> p t e", e=64)[:, :, 0:E + 1])

            def qk(b):
                for j in range(8):
                    n, i, m = (QK0 if b == 0 else QK1) + j, 8 * b + j, j % 4
                    o = task(n)
                    if i >= 3:
                        act.wait_ge(split_ready, i - 2)
                    act.activation(QV[i % 3], o, ACT.Identity, bias=BQS[:, m:m + 1],
                                   scale=SCALE if m < 2 else 1.0).then_inc(pro_free[n % 8], 1)

            act.wait_ge(router_shifted, 1)
            act.activation(LE[:, :, :], LS0[:, :, :], ACT.Exp).then_inc(router_exp, 1)
            act.activation(W4E[:, :, :], W4[:, :, :], ACT.Exp).then_inc(router_exp, 1)
            act.activation(SGE[:, :], SGE[:, :], ACT.Exp, scale=-1.0).then_inc(router_exp, 1)
            qk(0)
            qk(1)
            o = task(U0)
            act.activation(UL[:, :, :].rearrange("p (b h) s -> p h b s", b=B),
                           o[:, 0:4 * H].rearrange("p (h b s) -> p h b s", h=H, b=B), ACT.Copy)\
                .then_inc(pro_free[U0 % 8], 1)

            def exp1(it, k, s):
                i, par = step_tile(s), (k + 1) % 2
                base = P1_BANK[s] * 512
                sc = psf[:, base:base + (i + 1) * P]
                act.wait_ge(max_ready, unit(it, k, NQ, NQ + s + 1))
                act.activation(sc, sc, ACT.Exp, bias=NEGM[:, par, i:i + 1],
                               accum_out=LSUM[:, par, i:i + 1]).then_inc(exp1_done, 1)

            def exp2(it, k, s):
                base = P2_BANK[s] * 512
                if s == 0 and k >= 1:
                    act.wait_ge(pv_done, unit(it, k, NQ, 1 - NQ))
                act.wait_ge(p2_ready, unit(it, k, NQ, s + 1))
                act.activation(PB[:, k % 2, prob_offset(s):prob_offset(s) + (s + 1) * P],
                               psf[:, base:base + (s + 1) * P], ACT.Exp).then_inc(exp2_done, 1)

            def ln_sum(it, k, half):
                par = (k + 1) % 2
                act.wait_ge(exp1_done, unit(it, k, NQ, NQ + 4 * half + 4))
                if k >= 0:
                    act.wait_ge(c_parts_ready, unit(it, k, 2, half + 1))
                i0 = 4 - 4 * half
                act.activation(LNL[:, half, :], LSUM[:, par, i0:i0 + 4], ACT.Ln).then_inc(ln_ready, 1)

            def aux_task(it, k, a):
                b, before = aux(it, k, a)
                act.wait_ge(aux_ready[b], before + 1)
                return PSB[:, AUX + b, :]

            def exp3(it, k, a, task_, rows):
                z = silu_index(k, task_)
                act.wait_ge(gate_ready, silu(it, k, task_) + 1)
                act.activation(ET[0:rows, z % 2, :], ET[0:rows, z % 2, :], ACT.Exp, scale=-1.0)\
                    .then_inc(exp3_ready, 1)

            def shared(it, k, a, task_):
                which = 0 if task_ == SA else 1
                slot = k % SLOTS
                if slot < 3:
                    exp3(it, k, a, task_, FSZ[2 * slot + which])
                else:
                    o = aux_task(it, k, a)
                    t = turn(it, k, SLOTS, 2, which)
                    act.wait_ge(block_ready, turn(it, k, SLOTS, 2, 2))
                    dst = SH[:, t, :] if isinstance(t, int) else SH[:, bass.ds(t, 1), :].rearrange("p o d -> p (o d)")
                    act.activation(dst, o[:, 0:D], ACT.Copy, scale=SGB[:, which:which + 1]).then_inc(shared_out, 1)

            for s in range(NQ):
                exp1(0, -1, s)
                if s == 3:
                    ln_sum(0, -1, 0)
            ln_sum(0, -1, 1)

            def phase(it, k, first, last):
                ix = lambda t: aux_index(t, last)
                for s in range(NQ):
                    exp2(it, k, s)
                    if not last:
                        exp1(it, k, s)
                    if s == 3:
                        if not last:
                            ln_sum(it, k, 0)
                        o = aux_task(it, k, ix(TR))
                        act.activation(XET[:, :, :].rearrange("p c m -> p (c m)"), o[:, 0:D], ACT.Copy)\
                            .then_inc(xet_ready, 1)
                    if s == 4:
                        shared(it, k, ix(SA), SA)
                    if s == 5:
                        exp3(it, k, ix(GU), GU, FE)
                    if s == 7:
                        shared(it, k, ix(SB), SB)
                        if not last:
                            ln_sum(it, k, 1)
                        o = aux_task(it, k, ix(DN))
                        act.wait_ge(idx_ready, unit(it, k, 1, 1))
                        if k >= 1:
                            act.wait_ge(ye_free, unit(it, k))
                        act.activation(YE[:, k % 2, :], o[:, 0:D], ACT.Copy,
                                       scale=IDX[:, k % SLOTS, 1:2].bitcast(F32)).then_inc(ye_ready, 1)

            phases(act, phase)
            for g in range(NT // 2):
                act.wait_ge(fin_z, g + 1)
                e = XFT[:, :, :].rearrange("p c n -> p (c n)")[:, 512 * g:512 * (g + 1)]
                act.activation(e, e, ACT.Exp, scale=-1.0).then_inc(fin_e, 1)

        @block.vector
        def _(dve):
            link = Link(dve, dve_self)

            def root(stats, n):
                dve.wait_ge(sqrt_ready, n)
                link(dve.reciprocal(stats[:, 2, :], stats[:, 1, :]))
                link(dve.tensor_tensor(stats[:, 3, :], stats[:, 2, :], stats[:, 2, :], ALU.mult))
                link(dve.tensor_tensor(stats[:, 4, :], stats[:, 3, :], stats[:, 0, :], ALU.mult))
                link(dve.tensor_scalar(stats[:, 3, :], stats[:, 4, :], -0.5, 1.5, ALU.mult, ALU.add))
                link(dve.tensor_tensor(stats[:, 5, :], stats[:, 3, :], stats[:, 2, :], ALU.mult))

            for t in range(NT):
                dve.wait_ge(x_loaded[t // 4], 16)
                ins = dve.bn_stats(BNS[:, t, :], XN[:, t, :])
                if t == NT - 1:
                    link(ins)
                else:
                    ins.then_inc(dve_self, 1)
                    link.n += 1
            for t in range(NT):
                ins = dve.bn_aggr(MV[:, t, :], BNS[:, t, :])
                ins.then_inc(dve_self, 1)
                link.n += 1
            dve.wait_ge(dve_self, link.n)
            dve.tensor_scalar(NRM[:, 0, :], MV[:, :, 1], LN_EPS, None, ALU.add).then_inc(stat_ready, 1)
            dve.wait_ge(slope_loaded, 16)
            dve.wait_ge(alibi_ready, 1)
            link(dve.tensor_copy(SLB[:, 0:1], SL[:, :]))
            link(dve.tensor_tensor(SLR[:, 0:1], SL[:, :], SLB[:, 0:1], ALU.subtract))
            link(dve.tensor_copy(SLB[:, 1:2], SLR[:, 0:1]))
            link(dve.tensor_tensor(SLR[:, 1:2], SLR[:, 0:1], SLB[:, 1:2], ALU.subtract))
            link(dve.tensor_copy(SLB[:, 2:3], SLR[:, 1:2]))
            link(dve.tensor_copy(SLP[:, :], SLB[:, :]))
            for p in range(3):
                ins = dve.tensor_scalar(SROW[:, p, :], ONER, SLP[:, p:p + 1], None, ALU.mult)
                if p < 2:
                    link(ins)
            ins.then_inc(slope_rows_ready, 1)
            root(NRM, 1)
            for t in range(NT):
                dve.tensor_scalar(XN[:, t, :], XN[:, t, :], MV[:, t, 0:1], NRM[:, 5, t:t + 1],
                                  ALU.subtract, ALU.mult).then_inc(xn_ready, 1)
            dve.wait_ge(row_loaded, 80)
            link(dve.tensor_scalar(BQS[:, 0:2], BQK[:, 0:2], SCALE, None, ALU.mult))
            link(dve.tensor_copy(BQS[:, 2:4], BQK[:, 2:4]))
            dve.wait_ge(ss_ready, NT)
            dve.tensor_scalar(NR2[:, 0, :], SS[:, :], 1.0 / D, RMS_EPS, ALU.mult, ALU.add).then_inc(stat_ready, 1)
            dve.wait_ge(stat_ready, 2)
            root(NR2, 2)
            dve.wait_ge(xn_ready, NT)
            for t in range(NT):
                dve.scalar_tensor_tensor(out=XF[:, t, :], in0=XN[:, t, :], scalar=NR2[:, 5, t:t + 1],
                                         in1=WN[:, :], op0=ALU.mult, op1=ALU.mult).then_inc(xf_ready, 1)
            for n in (R0, R0 + 1):
                dve.wait_ge(pro_free[n % 8], n // 8 + 1)
            for t in range(NT):
                dve.max(V8[:, t, :], LG[:, t, 0:E]).then_inc(dve_self, 1)
                link.n += 1
            dve.wait_ge(dve_self, link.n)
            link(dve.tensor_tensor(LS0[:, :, :], LG[:, :, 0:E], V8[:, :, 0:1].broadcast_to([P, NT, E]), ALU.subtract))
            link(dve.tensor_tensor(W4[:, :, :], V8[:, :, 0:TOPK], V8[:, :, 0:1].broadcast_to([P, NT, TOPK]),
                                   ALU.subtract))
            link(dve.tensor_scalar(SGE[:, :], LG[:, :, E], LEAST, None, ALU.max))
            for t in range(NT):
                ins = dve.max_index(I8[:, t, :], V8[:, t, :], LG[:, t, 0:E])
                if t == 0:
                    ins.then_inc(router_shifted, 1)
                else:
                    ins.then_inc(dve_self, 1)
                    link.n += 1
            dve.wait_ge(dve_self, link.n)
            dve.wait_ge(router_shifted, 1)
            link(dve.tensor_copy(IDXF[:, :, :], I8[:, :, 0:TOPK]))
            dve.wait_ge(const_ready, 3)
            for n in range(W0, W0 + 4):
                dve.wait_ge(pro_free[n % 8], 1)
            link(dve.tensor_tensor(OH, IO32[:, :].unsqueeze(1).unsqueeze(1).broadcast_to([P, NT, TOPK, E]),
                                   IDXF[:, :, :].unsqueeze(3).broadcast_to([P, NT, TOPK, E]), ALU.is_equal))
            link(dve.tensor_tensor(PROD[:, :, 0:2, :], OH[:, :, 0:2, :], OH[:, :, 2:4, :], ALU.add))
            link(dve.tensor_tensor(MB[:, :, :], PROD[:, :, 0, :], PROD[:, :, 1, :], ALU.add))
            link(dve.memset(MC[:, 0, :], 0.0))
            for t in range(1, NT):
                ins = dve.tensor_tensor(MC[:, t, :], MC[:, t - 1, :], MB[:, t - 1, :], ALU.add)
                if t < NT - 1:
                    link(ins)
            ins.then_inc(onehot_ready, 1)

            def qk_split(b):
                for j in range(8):
                    n, i = (QK0 if b == 0 else QK1) + j, 8 * b + j
                    r = i % 3
                    dve.wait_ge(pro_free[n % 8], n // 8 + 1)
                    if i >= 3:
                        dve.wait_ge(split_stored[r], 16 * (i // 3))
                    link(dve.tensor_copy(SPL[r][:, 0, :], QV[r]))
                    link(dve.tensor_tensor(QV[r], QV[r], SPL[r][:, 0, :], ALU.subtract))
                    link(dve.tensor_copy(SPL[r][:, 1, :], QV[r]))
                    dve.tensor_tensor(SPL[r][:, 2, :], QV[r], SPL[r][:, 1, :], ALU.subtract).then_inc(split_ready, 1)

            dve.wait_ge(router_exp, 3)
            link(dve.tensor_reduce(ZS[:, :], LE[:, :, :], AX_X, ALU.add))
            link(dve.reciprocal(ZR[:, :], ZS[:, :]))
            dve.wait_ge(token_ids, 3)
            link(dve.tensor_tensor(RWS[:, :, :, 1].bitcast(F32), W4E[:, :, :],
                                   ZR[:, :].unsqueeze(2).broadcast_to([P, NT, TOPK]), ALU.mult))
            link(dve.tensor_scalar(SG1[:, :], SGE[:, :], 1.0, None, ALU.add))
            link(dve.reciprocal(SG[:, :], SG1[:, :]))
            pos = bank(POS0).rearrange("p (t e) -> p t e", e=E)
            dve.wait_ge(pro_ready[POS0 % 8], POS0 // 8 + 1)
            dve.tensor_tensor(PROD, OH, pos.unsqueeze(2).broadcast_to([P, NT, TOPK, E]), ALU.mult)\
                .then_inc(pro_free[POS0 % 8], 1)
            dve.wait_ge(pro_free[POS0 % 8], POS0 // 8 + 1)
            link(dve.tensor_reduce(PK[:, :, :], PROD, AX_X, ALU.add))
            link(dve.tensor_scalar(BAD[:, :, :], PK[:, :, :], float(CAP), float(CAP * E), ALU.is_ge, ALU.mult))
            link(dve.scalar_tensor_tensor(out=DST[:, :, :], in0=PK[:, :, :], scalar=float(E), in1=IDXF[:, :, :],
                                          op0=ALU.mult, op1=ALU.add))
            link(dve.tensor_tensor(DST2[:, :, :], DST[:, :, :], BAD[:, :, :], ALU.add))
            dve.tensor_copy(DI[:, :, :], DST2[:, :, :].rearrange("p t k -> p k t")).then_inc(dest_ready, 1)
            qk_split(0)
            for n in range(XN0, XN0 + 8):
                dve.wait_ge(pro_free[n % 8], n // 8 + 1)
            link(dve.tensor_reduce(TS[:, :, :], XNT[:, :, :].rearrange("p c (t q) -> p c t q", q=P), AX_X, ALU.add))
            ts = TS[:, :, :].rearrange("p c (b t) -> p c b t", b=B)
            link(dve.memset(XS[:, :, :, NQ - 1], 0.0))
            for t in reversed(range(NQ - 1)):
                link(dve.tensor_tensor(XS[:, :, :, t], XS[:, :, :, t + 1], ts[:, :, :, t + 1], ALU.add))
            dve.tensor_scalar(XS2[:, :, :, :], XS[:, :, :, :], FLOOR, None, ALU.mult).then_inc(tsum_ready, 1)
            qk_split(1)
            dve.wait_ge(alibi_stored, 16 * 10 * B)
            for g in range(8):
                n = V0 + g
                dve.wait_ge(pro_ready[n % 8], n // 8 + 1)
                for a in range(2):
                    t = 2 * g + a
                    b = t // NQ
                    ins = dve.tensor_tensor(VS[:, b * H:(b + 1) * H, DH * (t % NQ):DH * (t % NQ + 1)],
                                            bank(n)[:, a * D:(a + 1) * D].rearrange("p (h d) -> p h d", d=DH),
                                            BV[:, :].rearrange("p (h d) -> p h d", d=DH), ALU.add)
                    if a == 0:
                        link(ins)
                ins.then_inc(pro_free[n % 8], 1)

            def row_max(it, k, s):
                i, par = step_tile(s), (k + 1) % 2
                base = P1_BANK[s] * 512
                dve.wait_ge(p1_ready, unit(it, k, NQ, NQ + s + 1))
                dve.tensor_reduce(NEGM[:, par, i:i + 1], psf[:, base:base + (i + 1) * P], AX_X, ALU.max,
                                  negate=True).then_inc(max_ready, 1)

            def clamp(it, k, s):
                dve.wait_ge(exp2_done, unit(it, k, NQ, s + 1))
                p = PB[:, k % 2, prob_offset(s):prob_offset(s) + (s + 1) * P]
                dve.tensor_scalar(p, p, FLOOR, None, ALU.max).then_inc(clamp_done, 1)

            def c_rows(it, k, a, half, slot):
                b, before = aux(it, k, a)
                c0 = 512 if half == 0 else 0
                dve.wait_ge(aux_ready[b], before + 1)
                dve.tensor_copy(QS[slot][SHIFT:SHIFT + 3, c0:c0 + 512],
                                PSB[SHIFT:SHIFT + 3, AUX + b, 0:256].bitcast(BF16)).then_inc(c_rows_ready, 1)

            def gate(it, k, a, task_, rows):
                b, before = aux(it, k, a)
                z, n = silu_index(k, task_), silu(it, k, task_)
                dve.wait_ge(aux_ready[b], before + 1)
                if z >= 2:
                    dve.wait_ge(silu_done, silu(it, k, task_) - 1)
                dve.tensor_scalar(ET[0:rows, z % 2, :], PSB[0:rows, AUX + b, 0:BLK], LEAST, None, ALU.max)\
                    .then_inc(gate_ready, 1)

            def silu_up(it, k, a, task_, dst, rows):
                b, _ = aux(it, k, a)
                z = silu_index(k, task_)
                n = silu(it, k, task_)
                psum = PSB[0:rows, AUX + b, :]
                dve.wait_ge(exp3_ready, n + 1)
                dve.tensor_scalar(RT[0:rows, 0, :], ET[0:rows, z % 2, :], 1.0, None, ALU.add).then_inc(silu_chain, 1)
                dve.wait_ge(silu_chain, n * 3 + 1)
                dve.reciprocal(RT[0:rows, 1, :], RT[0:rows, 0, :]).then_inc(silu_chain, 1)
                dve.wait_ge(silu_chain, n * 3 + 2)
                dve.tensor_tensor(RT[0:rows, 2, :], psum[:, 0:BLK], RT[0:rows, 1, :], ALU.mult)\
                    .then_inc(silu_chain, 1)
                dve.wait_ge(silu_chain, n * 3 + 3)
                dve.tensor_tensor(dst, psum[:, BLK:2 * BLK], RT[0:rows, 2, :], ALU.mult).then_inc(silu_done, 1)

            def shared_gate(it, k, a, task_):
                if k % SLOTS < 3:
                    gate(it, k, a, task_, FSZ[2 * (k % SLOTS) + (0 if task_ == SA else 1)])

            def shared(it, k, a, task_):
                slot = k % SLOTS
                if slot == 3:
                    return
                ch = 2 * slot + (0 if task_ == SA else 1)
                if ch == 0 and k >= SLOTS:
                    b, before = aux(it, k - 1, SB)
                    dve.wait_ge(aux_ready[b], before + 1)
                silu_up(it, k, a, task_, HS[0:FSZ[ch], ch, :], FSZ[ch])

            def evacuate_heads(it, k):
                slot = k % SLOTS
                dve.wait_ge(pv_done, unit(it, k, NQ, NQ))
                dve.wait_ge(o_stored[slot], turn(it, k, SLOTS, 64, 64))
                u = unit(it, k)
                ul = UL[:, u, :] if isinstance(u, int) else UL[:, bass.ds(u, 1), :].rearrange("p o s -> p (o s)")
                dve.tensor_tensor(OEV[:, slot, :, :], PSB[:, O_BANK, 0:2 * P].rearrange("p (t q) -> p t q", q=P),
                                  ul.unsqueeze(2).broadcast_to([P, 2, P]), ALU.add).then_inc(o_evacuated, 1)

            for s in range(NQ):
                row_max(0, -1, s)
            c_rows(0, -1, AUX_TASKS - 1, 0, 0)
            dve.wait_ge(pro_free[U0 % 8], U0 // 8 + 1)

            def phase(it, k, first, last):
                ix = lambda t: aux_index(t, last)
                for s in range(NQ):
                    if not last:
                        row_max(it, k, s)
                    if s == 2 and not first:
                        evacuate_heads(it, k - 1)
                    if s == 2:
                        c_rows(it, k, ix(CB), 1, k % SLOTS)
                    if s == 6 and not last:
                        c_rows(it, k, ix(CA), 0, (k + 1) % SLOTS)
                    if s == 7:
                        shared_gate(it, k, ix(SB), SB)
                    if s > 0:
                        clamp(it, k, s - 1)
                    elif not first:
                        clamp(it, k - 1, NQ - 1)
                    if s == 4:
                        shared_gate(it, k, ix(SA), SA)
                    if s == 5:
                        gate(it, k, ix(GU), GU, FE)
                        shared(it, k, ix(SA), SA)
                    if s == 6:
                        b, before = aux(it, k - 1, DN)
                        if not first:
                            dve.wait_ge(aux_ready[b], before + 1)
                        silu_up(it, k, ix(GU), GU, HE[:, :, :].rearrange("p f c -> p (f c)"), FE)
                    if s == 7:
                        shared(it, k, ix(SB), SB)

            phases(dve, phase)
            clamp(UNITS // SLOTS - 1, SLOTS - 1, NQ - 1)
            evacuate_heads(UNITS // SLOTS - 1, SLOTS - 1)
            dve.wait_ge(fin_loaded, 48)
            dve.wait_ge(ye_ready, UNITS)
            zf = XN[:, :, :].rearrange("p t d -> p (t d)")
            shf = SH.rearrange("p t d -> p (t d)")
            ef = XFT[:, :, :].rearrange("p c n -> p (c n)")
            vf = VS[:, :, :].rearrange("p u n -> p (u n)")
            xall = pbf[:, 0:T * D // P]
            fin = Link(dve, fin_chain)
            for g in range(NT // 2):
                c = slice(512 * g, 512 * (g + 1))
                fin(dve.tensor_tensor(zf[:, c], zf[:, c], shf[:, c], ALU.add))
                dve.tensor_scalar(ef[:, c], zf[:, c], LEAST, None, ALU.max).then_inc(fin_z, 1)
            for g in range(NT // 2):
                c = slice(512 * g, 512 * (g + 1))
                dve.wait_ge(fin_e, g + 1)
                dve.wait_ge(fin_mm, g + 1)
                fin(dve.tensor_scalar(ef[:, c], ef[:, c], 1.0, None, ALU.add))
                fin(dve.reciprocal(ef[:, c], ef[:, c]))
                fin(dve.tensor_tensor(zf[:, c], zf[:, c], ef[:, c], ALU.mult))
                fin(dve.tensor_tensor(vf[:, 0:512].rearrange("p (a d) -> p a d", a=2),
                                      PSB[:, g, :].rearrange("p (a d) -> p a d", a=2),
                                      OB[:, :].unsqueeze(1).broadcast_to([P, 2, D]), ALU.add))
                fin(dve.tensor_tensor(vf[:, 512:1024], vf[:, 0:512], zf[:, c], ALU.mult))
                dve.tensor_tensor(xall[:, c], xall[:, c], vf[:, 512:1024], ALU.add).then_inc(fin_out, 1)
                dve.wait_ge(fin_out, g + 1)

        @block.gpsimd
        def _(pool):
            link = Link(pool, pool_self)
            link(pool.memset(IDF[:, :], 0.0))
            link(pool.memset(IDB[:, :], 0.0))
            link(pool.memset(MQ[:, :], 0.0))
            link(pool.memset(MK[:, :], 0.0))
            link(pool.memset(ONEB[:, :], 1.0))
            link(pool.memset(LT[:, :], 1.0))
            link(pool.memset(WIT[:, :, 3 * D:3 * D + PAD], 0.0))
            pool.affine_select(out=IDF[:, :], in_=IDF[:, :], compare_op=ALU.not_equal, fill=1.0, base=0,
                               pattern=[[-1, P]], channel_multiplier=1).then_inc(mask_ready, 1)
            pool.affine_select(out=IDB[:, :], in_=IDB[:, :], compare_op=ALU.not_equal, fill=1.0, base=0,
                               pattern=[[-1, P]], channel_multiplier=1).then_inc(mask_ready, 1)
            pool.affine_select(out=MQ[:, :], in_=MQ[:, :], compare_op=ALU.is_ge, fill=MASK, base=0,
                               pattern=[[-1, P]], channel_multiplier=1).then_inc(mask_ready, 1)
            pool.affine_select(out=MK[:, :], in_=MK[:, :], compare_op=ALU.is_ge, fill=MASK, base=0,
                               pattern=[[1, P]], channel_multiplier=-1).then_inc(mask_ready, 1)
            pool.affine_select(out=LT[:, :], in_=LT[:, :], compare_op=ALU.is_gt, fill=0.0, base=0,
                               pattern=[[1, P]], channel_multiplier=-1).then_inc(mask_ready, 1)
            pool.memset(ONER, 1.0).then_inc(alibi_ready, 1)
            for r, pattern in enumerate(([[P, NQ], [0, P]], [[0, NQ], [1, P]], [[-P, NQ], [0, P]],
                                         [[0, NQ], [-1, P]])):
                pool.iota(IROW[:, r, :].rearrange("p (t q) -> p t q", q=P), pattern, base=0, channel_multiplier=0,
                          allow_small_or_imprecise_dtypes=True).then_inc(int_rows_ready, 1)
            pool.memset(ZROW, 0.0).then_inc(int_rows_ready, 1)
            pool.memset(BVR[:, D:D + PAD], 0.0).then_inc(int_rows_ready, 1)
            pool.iota(IO32[:, :], [[1, E]], base=0, channel_multiplier=0,
                      allow_small_or_imprecise_dtypes=True).then_inc(const_ready, 1)
            link(pool.iota(CNT[:, :, :], [[0, B], [-P, NQ]], base=P * (NQ - 1), channel_multiplier=0,
                           allow_small_or_imprecise_dtypes=True))
            pool.tensor_scalar(CNT[:, :, :], CNT[:, :, :], FLOOR, None, ALU.mult).then_inc(const_ready, 1)
            pool.memset(VH[:, :, :, :], 0.0).then_inc(const_ready, 1)
            link(pool.memset(TI[:, :, :], 0))
            pool.iota(TI[:, :, 2], [[0, E]], base=T, channel_multiplier=1).then_inc(table_tile, 1)
            link(pool.memset(RWS[:, :, :, 3], 0))
            pool.iota(RWS[:, :, :, 0], [[P, NT], [0, TOPK]], base=0, channel_multiplier=1).then_inc(token_ids, 1)
            pool.iota(RWS[:, :, :, 2], [[P, NT], [0, TOPK]], base=0, channel_multiplier=1).then_inc(token_ids, 1)
            pool.memset(RWS[:, :, :, 1], 0).then_inc(token_ids, 1)

            def chain(it, k, half):
                par, i0 = k % 2, 4 - 4 * half
                n = unit(it, k, 2, half)
                pool.wait_ge(ln_ready, n + 1)
                if not (isinstance(it, int) and unit(it, k) == 0):
                    pool.wait_ge(c_rows_ready, n - 1)
                pool.tensor_tensor(CC[:, half, :], NEGM[:, par, i0:i0 + 4], LNL[:, half, :], ALU.subtract)\
                    .then_inc(c_chain, 1)
                hold(pool, c_chain, n * 5 + 1)
                pool.tensor_copy(C3[:, half, :, 0], CC[:, half, :]).then_inc(c_chain, 1)
                pool.wait_ge(c_chain, n * 5 + 2)
                pool.tensor_tensor(CR[:, half, 0, :], CC[:, half, :], C3[:, half, :, 0], ALU.subtract)\
                    .then_inc(c_chain, 1)
                hold(pool, c_chain, n * 5 + 3)
                pool.tensor_copy(C3[:, half, :, 1], CR[:, half, 0, :]).then_inc(c_chain, 1)
                pool.wait_ge(c_chain, n * 5 + 4)
                pool.tensor_tensor(CR[:, half, 1, :], CR[:, half, 0, :], C3[:, half, :, 1], ALU.subtract)\
                    .then_inc(c_chain, 1)
                hold(pool, c_chain, n * 5 + 5)
                pool.tensor_copy(C3[:, half, :, 2], CR[:, half, 1, :]).then_inc(c_parts_ready, 1)

            pool.wait_ge(dest_ready, 1)
            pool.wait_ge(table_cleared, 16)
            for t in range(NT):
                for kk in range(TOPK):
                    pool.indirect_dma_start(
                        out=slot_table, out_offset=bass.IndirectOffsetOnAxis(ap=DI[:, kk, t:t + 1], axis=0),
                        in_=RWS[:, t, kk, :], in_offset=None, bounds_check=CAP * E - 1, oob_is_err=False)\
                        .then_inc(scattered, 16)
            pool.wait_ge(scattered, 16 * NT * TOPK)
            pool.dma_start(TABS[:, :], slot_table.rearrange("(c e) w -> c (e w)", e=E)).then_inc(table_loaded, 16)
            chain(0, 0, 0)
            chain(0, 0, 1)
            pool.wait_ge(table_loaded, 16)
            pool.wait_ge(xf_stored, 16)
            pool.wait_ge(moe_started, 32)
            for n in range(V0, V0 + 8):
                pool.wait_ge(pro_free[n % 8], n // 8 + 1)

            def sbuf_cols(tile, start, n):
                return tile[:, start:start + n] if isinstance(start, int) else tile[:, bass.ds(start, n)]

            def phase(it, k, first, last):
                slot, par = k % SLOTS, k % 2
                if k >= 1:
                    hold(pool, pv_done, unit(it, k, NQ, 1 - NQ))
                vflat = VS[:, :, :].rearrange("p u n -> p (u n)")
                pool.tensor_copy(VH[:, par, :, 0:DH],
                                 sbuf_cols(vflat, unit(it, k, NQ * DH), NQ * DH)
                                 .rearrange("p (t d) -> p t d", d=DH)).then_inc(v_ready, 1)
                pool.tensor_copy(IDX[:, slot, :], sbuf_cols(TABS, unit(it, k, 4), 4)).then_inc(idx_ready, 1)
                hold(pool, idx_ready, unit(it, k, 1, 1))
                if k >= 1:
                    hold(pool, xet_ready, unit(it, k))
                pool.indirect_dma_start(
                    out=XE[:, par, :], out_offset=None, in_=xf_rows,
                    in_offset=bass.IndirectOffsetOnAxis(ap=IDX[:, slot, 0:1].bitcast(U32), axis=0),
                    bounds_check=T - 1, oob_is_err=False).then_inc(xe_loaded[par], 16)
                if slot == 0:
                    if k >= SLOTS:
                        hold(pool, *aux_done(it, k - 1, SB))
                    c0 = turn(it, k, SLOTS, BLK)
                    src = XFT[:, :, c0:c0 + BLK] if isinstance(c0, int) else XFT[:, :, bass.ds(c0, BLK)]
                    pool.tensor_copy(XFB[:, :, :], src).then_inc(block_ready, 1)
                    pool.tensor_copy(SGB[:, :], sbuf_cols(SG, turn(it, k, SLOTS, 2), 2)).then_inc(block_ready, 1)
                if not last:
                    chain(it, k + 1, 0)
                    chain(it, k + 1, 1)
                hold(pool, ye_ready, unit(it, k, 1, 1))
                hold(pool, moe_added, unit(it, k, 16))
                pool.sem_inc(ye_free, 1)
                pool.indirect_dma_start(
                    out=moe_rows, out_offset=bass.IndirectOffsetOnAxis(ap=IDX[:, slot, 2:3].bitcast(U32), axis=0),
                    in_=YE[:, par, :], in_offset=None, bounds_check=T + CAP - 1, oob_is_err=True,
                    compute_op=ALU.add).then_inc(moe_added, 16)

            phases(pool, phase)


_INS = ['L0_attn_qkv', 'L0_attn_in_proj', 'L0_attn_in_proj_bias', 'L0_attn_out_w', 'L0_attn_out_b',
        'L0_attn_alibi_slopes', 'L0_ffn_w_norm', 'L0_ffn_w_router', 'L0_ffn_w_gate', 'L0_ffn_w_up',
        'L0_ffn_w_down', 'L0_ffn_sw_gate', 'L0_ffn_sw_up', 'L0_ffn_sw_down', 'L0_ffn_w_shared_gate']


def kernel(**inputs):
    import numpy as _np
    import concourse.bacc as _bacc
    from concourse import mybir as _mybir
    from concourse.bass_utils import run_bass_kernel_spmd as _run

    nc = _bacc.Bacc("TRN2", target_bir_lowering=False, num_devices=1)
    arrays, args = {}, []
    for name in _INS:
        a = _np.ascontiguousarray(inputs[name])
        arrays[f"in_{name}_dram"] = a
        args.append(nc.dram_tensor(f"in_{name}_dram", a.shape, _mybir.dt.from_np(a.dtype), kind="ExternalInput").ap())
    args.append(nc.dram_tensor("out_0_dram", (B, S, D), _mybir.dt.float32, kind="ExternalOutput").ap())
    build(nc, *args)
    r = _run(nc, [arrays], core_ids=[0])
    return r.results[0]["out_0_dram"]
```

```python
from contextlib import ExitStack

import concourse.bass as bass
from concourse import mybir

F32 = mybir.dt.float32
BF16 = mybir.dt.bfloat16
I32 = mybir.dt.int32
U32 = mybir.dt.uint32
ALU = mybir.AluOpType
ACT = mybir.ActivationFunctionType
AX_X = mybir.AxisListType.X

P = 128
B, S, D = 2, 1024, 256
T = B * S
NT = T // P
NQ = S // P
KC = D // P
H = 16
DH = D // H
E, TOPK, F, CAP = 32, 4, 176, 128
FE = F // 2
FS = 704
NF = -(-FS // P)
FSZ = [min(P, FS - P * c) for c in range(NF)]
SCALE = float(DH) ** -0.5
FLOOR = 1e-10
MASK = -1e30
LN_SLOPE = -0.6931471805599453 / (1 << 23)
LN_BASE = 0.6931471805599453 * (127 - 0.0430)
LN_EPS, RMS_EPS = 1e-5, 1e-6
UNITS = B * H
SLOTS = 4
SPLIT_ROWS = 6 * DH
SHIFT = SPLIT_ROWS
ROWS = SHIFT + 3 + 12
BLK = 256
O_BANK, AUX = 5, 6
PAD = 16

TR, SA, CB, GU, SB, CA, DN = range(7)
AUX_TASKS = 7
W0, XN0, XF0, R0, QK0, POS0, QK1, V0, U0 = 0, 4, 12, 20, 22, 30, 31, 39, 47
PRO_TASKS = 48


def step_tile(s):
    return NQ - 1 - s


AHEAD = NQ + NQ // 2

P1_BANK = [0, 2, 0, 2, 0, 1, 0, 2]
P2_BANK = [4, 4, 4, 4, 3, 3, 3, 3]


def prob_offset(s):
    return s * (s + 1) // 2 * P


def build(nc, x, in_proj, in_b, out_w, out_b, slopes, w_norm, w_router, w_gate, w_up, w_down,
          sw_gate, sw_up, sw_down, w_sg, out):
    ctx = ExitStack()
    with ctx:
        def sb(name, shape, dt=F32):
            return ctx.enter_context(nc.sbuf_tensor(name, shape, dt))

        def sem(name):
            return ctx.enter_context(nc.semaphore(name))

        def dram(name, shape, dt=F32):
            return nc.dram_tensor(name, shape, dt, kind="Internal").ap()

        xf_rows = dram("xf_rows", (T, D))
        moe_rows = dram("moe_rows", (T + CAP, D))
        slot_table = dram("slot_table", (CAP * E, 4), I32)
        q_parts = dram("q_parts", (3, B * D, S), BF16)
        k_parts = dram("k_parts", (3, B * D, S), BF16)
        q_alibi = dram("q_alibi", (UNITS, 15, S), BF16)
        k_alibi = dram("k_alibi", (UNITS, 15, S), BF16)
        att_rows = dram("att_rows", (B * D, S))

        XN = sb("XN", [P, NT, D])
        STACKS = sb("STACKS", [P, 2 * SLOTS, S], BF16)
        stf = STACKS[:, :, :].rearrange("p a s -> p (a s)").bitcast(F32)
        XF = stf.rearrange("p (t d) -> p t d", d=D)
        XNT = sb("XNT", [P, KC, T])
        XFT = sb("XFT", [P, KC, T])
        SH = XNT[:, :, :].rearrange("p a (t d) -> p (a t) d", d=D)
        ATTS = stf.rearrange("p (b a s) -> p b a s", b=B, a=KC)
        VS = sb("VS", [P, UNITS, NQ * DH])
        PB = sb("PB", [P, 2, 36 * P])
        pbf = PB[:, :, :].rearrange("p a n -> p (a n)")
        OH = pbf[:, 0:2048].rearrange("p (t k e) -> p t k e", t=NT, k=TOPK)
        PROD = pbf[:, 2048:4096].rearrange("p (t k e) -> p t k e", t=NT, k=TOPK)
        X = pbf[:, 0:T * D // P].rearrange("p (t d) -> p t d", d=D)
        INW = pbf[:, 0:1536].rearrange("p (a d) -> p a d", a=6)
        OW = pbf[:, 2048:2560].rearrange("p (a d) -> p a d", a=2)
        QV = [pbf[:, 4096 + 512 * r:4096 + 512 * (r + 1)] for r in range(3)]
        SPL = [pbf[:, 5632 + 768 * r:5632 + 768 * (r + 1)].bitcast(BF16).rearrange("p (a t) -> p a t", a=3)
               for r in range(3)]
        QS = [STACKS[:, r, :] for r in range(SLOTS)]
        KS = [STACKS[:, SLOTS + r, :] for r in range(SLOTS)]
        WG = [sb(f"WG{r}", [P, KC, F]) for r in range(SLOTS)]
        WU = [sb(f"WU{r}", [P, KC, F]) for r in range(SLOTS)]
        WD = [sb(f"WD{r}", [FE, 2, D]) for r in range(SLOTS)]
        SWG = sb("SWG", [P, KC, FS])
        SWU = sb("SWU", [P, KC, FS])
        SWD = sb("SWD", [P, NF, D])
        WIT = sb("WIT", [P, KC, 3 * D + PAD])
        OWT = sb("OWT", [P, KC, D])
        RW = sb("RW", [P, KC, E + 1])
        WN = sb("WN", [P, D])
        BV = sb("BV", [P, D])
        OB = sb("OB", [P, D])
        BQK = sb("BQK", [P, 4])
        BQS = sb("BQS", [P, 4])
        BVR = sb("BVR", [1, D + PAD])
        CNT = sb("CNT", [1, B, NQ])
        IDF = sb("IDF", [P, P])
        IDB = sb("IDB", [P, P], BF16)
        MQ = sb("MQ", [P, P], BF16)
        MK = sb("MK", [P, P], BF16)
        LT = sb("LT", [P, P], BF16)
        ONEB = sb("ONEB", [P, P], BF16)
        SL = sb("SL", [H, 1])
        SLR = sb("SLR", [H, 2])
        SLB = sb("SLB", [H, 3], BF16)
        SLP = sb("SLP", [H, 3])
        vsb = VS[0:H, :, :].rearrange("p u n -> p (u n)").bitcast(BF16).rearrange("p (a s) -> p a s", s=S)
        SROW, IROW, ONER = vsb[:, 0:3, :], vsb[:, 3:7, :], vsb[:, 7, :]
        BNS = sb("BNS", [P, NT, 6])
        MV = sb("MV", [P, NT, 2])
        SS = sb("SS", [P, NT])
        ET = sb("ET", [P, 2, BLK])
        SQJ = ET
        NRM = sb("NRM", [P, 6, NT])
        NR2 = sb("NR2", [P, 6, NT])
        LG = sb("LG", [P, NT, E + 1])
        V8 = sb("V8", [P, NT, 8])
        I8 = sb("I8", [P, NT, 8], U32)
        LS0 = pbf[:, 7936:8448].rearrange("p (t e) -> p t e", e=E)
        LE = pbf[:, 8448:8960].rearrange("p (t e) -> p t e", e=E)
        W4 = sb("W4", [P, NT, TOPK])
        W4E = sb("W4E", [P, NT, TOPK])
        ZS = sb("ZS", [P, NT])
        ZR = sb("ZR", [P, NT])
        SGE = sb("SGE", [P, NT])
        SG = sb("SG", [P, NT])
        IO32 = sb("IO32", [P, E])
        IDXF = sb("IDXF", [P, NT, TOPK])
        MB = sb("MB", [P, NT, E], BF16)
        MC = sb("MC", [P, NT, E], BF16)
        PK = sb("PK", [P, NT, TOPK])
        BAD = sb("BAD", [P, NT, TOPK])
        DST = sb("DST", [P, NT, TOPK])
        DST2 = sb("DST2", [P, NT, TOPK])
        DI = sb("DI", [P, TOPK, NT], I32)
        RWS = sb("RWS", [P, NT, TOPK, 4], I32)
        TI = sb("TI", [P, E, 4], I32)
        TABS = sb("TABS", [P, E * 4], I32)
        TS = sb("TS", [P, KC, NT])
        XS = sb("XS", [P, KC, B, NQ])
        XS2 = sb("XS2", [P, KC, B, NQ])
        UL = sb("UL", [P, UNITS, 2])
        NEGM = sb("NEGM", [P, 2, NQ])
        LSUM = sb("LSUM", [P, 2, NQ])
        LNS = sb("LNS", [P, 2, 4])
        LEX = sb("LEX", [P, 2, 4])
        CC = sb("CC", [P, 2, 4])
        CR = sb("CR", [P, 2, 2, 4])
        C3 = sb("C3", [P, 2, 4, 3], BF16)
        VH = sb("VH", [P, 2, NQ, 2 * DH])
        OEV = sb("OEV", [P, SLOTS, 2, P])
        XE = sb("XE", [P, 2, D])
        XET = sb("XET", [P, KC, P])
        IDX = sb("IDX", [P, SLOTS, 4], I32)
        RT = sb("RT", [P, BLK])
        HE = sb("HE", [FE, 2, CAP])
        HS = sb("HS", [P, NF, BLK])
        YE = sb("YE", [P, 2, D])
        ZROW = HS[0:H, 0:2, :].rearrange("p a n -> p (a n)").bitcast(BF16)
        XFB = sb("XFB", [P, KC, BLK])
        SGB = sb("SGB", [P, 2])

        PSB = ctx.enter_context(nc.psum_tensor("PSB", [P, 8, 512], F32))
        psf = PSB[:, :, :].rearrange("p a n -> p (a n)")

        x_loaded = [sem(f"x_loaded{g}") for g in range(4)]
        w_loaded = sem("w_loaded")
        rw_loaded = sem("rw_loaded")
        row_loaded = sem("row_loaded")
        sw_loaded = sem("sw_loaded")
        slope_loaded = sem("slope_loaded")
        const_ready = sem("const_ready")
        mask_ready = sem("mask_ready")
        pool_self = sem("pool_self")
        dve_self = sem("dve_self")
        xn_ready = sem("xn_ready")
        xf_ready = sem("xf_ready")
        stat_ready = sem("stat_ready")
        ss_ready = sem("ss_ready")
        sqrt_ready = sem("sqrt_ready")
        pro_ready = [sem(f"pro_ready{b}") for b in range(8)]
        pro_free = [sem(f"pro_free{b}") for b in range(8)]
        qv_ready = sem("qv_ready")
        split_ready = sem("split_ready")
        split_stored = [sem(f"split_stored{r}") for r in range(3)]
        alibi_ready = sem("alibi_ready")
        slope_rows_ready = sem("slope_rows_ready")
        int_rows_ready = sem("int_rows_ready")
        alibi_stored = sem("alibi_stored")
        router_shifted = sem("router_shifted")
        router_exp = sem("router_exp")
        onehot_ready = sem("onehot_ready")
        dest_ready = sem("dest_ready")
        table_tile = sem("table_tile")
        table_cleared = sem("table_cleared")
        token_ids = sem("token_ids")
        scattered = sem("scattered")
        table_loaded = sem("table_loaded")
        xf_stored = sem("xf_stored")
        moe_started = sem("moe_started")
        tsum_ready = sem("tsum_ready")
        held = sem("held")
        stack_loaded = [sem(f"stack_loaded{r}") for r in range(SLOTS)]
        expert_loaded = [sem(f"expert_loaded{r}") for r in range(SLOTS)]
        p1_ready = sem("p1_ready")
        max_ready = sem("max_ready")
        exp1_done = sem("exp1_done")
        p2_ready = sem("p2_ready")
        exp2_done = sem("exp2_done")
        clamp_done = sem("clamp_done")
        pv_done = sem("pv_done")
        v_ready = sem("v_ready")
        o_evacuated = sem("o_evacuated")
        o_stored = [sem(f"o_stored{r}") for r in range(SLOTS)]
        seed_ready = sem("seed_ready")
        seed_exp = sem("seed_exp")
        c_chain = sem("c_chain")
        c_parts_ready = sem("c_parts_ready")
        c_rows_ready = sem("c_rows_ready")
        aux_ready = [sem(f"aux_ready{b}") for b in range(2)]
        shared_out = sem("shared_out")
        tanh_ready = sem("tanh_ready")
        silu_chain = sem("silu_chain")
        silu_done = sem("silu_done")
        block_ready = sem("block_ready")
        scale_ready = sem("scale_ready")
        idx_ready = sem("idx_ready")
        xe_loaded = [sem(f"xe_loaded{r}") for r in range(2)]
        xet_ready = sem("xet_ready")
        ye_ready = sem("ye_ready")
        moe_added = sem("moe_added")
        ye_free = sem("ye_free")
        fin_loaded = sem("fin_loaded")
        fin_mm = sem("fin_mm")
        fin_z = sem("fin_z")
        fin_e = sem("fin_e")
        fin_chain = sem("fin_chain")
        fin_out = sem("fin_out")
        stored = sem("stored")

        def bank(n):
            return PSB[:, n % 8, :]

        class Link:

            def __init__(self, eng, semaphore):
                self.eng, self.semaphore, self.n = eng, semaphore, 0

            def __call__(self, ins):
                self.n += 1
                ins.then_inc(self.semaphore, 1)
                self.eng.wait_ge(self.semaphore, self.n)

        def hold(eng, semaphore, count):
            eng.wait_ge(semaphore, count)
            eng.sem_inc(held, 1)

        def unit(it, k, per=1, add=0):
            return it * (SLOTS * per) + (per * k + add)

        def turn(it, k, n, per=1, add=0):
            return it * (SLOTS // n * per) + (per * (k // n) + add)

        def aux(it, k, a):
            n = 2 + AUX_TASKS * k + a
            return n % 2, it * (SLOTS * AUX_TASKS // 2) + n // 2

        def aux_index(task, last):
            return task - (task > CB) - (task > CA) if last else task

        def silu_index(k, task):
            return 10 * (k // SLOTS) + 3 * (k % SLOTS) + (0 if k % SLOTS == 3 else {SA: 0, GU: 1, SB: 2}[task])

        def silu(it, k, task):
            return it * 10 + silu_index(k, task)

        def ahead_unit(n):
            return (n + NQ // 2) // NQ - 2

        def aux_done(it, k, task):
            if task == CB:
                return c_rows_ready, unit(it, k, 2, 3)
            if task == CA:
                return c_rows_ready, unit(it, k, 2, 4)
            if task == TR:
                return xet_ready, unit(it, k, 1, 1)
            if task == DN:
                return ye_ready, unit(it, k, 1, 1)
            if task != GU and k % SLOTS == 3:
                return shared_out, turn(it, k, SLOTS, 2, 1 if task == SA else 2)
            return silu_done, silu(it, k, task) + 1

        def phases(eng, phase):
            phase(0, 0, True, NQ)
            phase(0, 1, False, NQ)
            with eng.Fori(0, UNITS // SLOTS - 1) as it:
                for k in range(2, SLOTS + 2):
                    phase(it, k, False, NQ)
            phase(UNITS // SLOTS - 1, 2, False, NQ // 2)
            phase(UNITS // SLOTS - 1, 3, False, 0)

        block = ctx.enter_context(nc.Block())

        @block.sync
        def _(sp):
            x_t = x.rearrange("b (t p) d -> p (b t) d", p=P)
            for g in range(4):
                sp.dma_start(XN[:, 4 * g:4 * g + 4, :], x_t[:, 4 * g:4 * g + 4, :]).then_inc(x_loaded[g], 16)
            sp.dma_start(INW, in_proj.rearrange("(a p) d -> p a d", p=P)).then_inc(w_loaded, 16)
            sp.dma_start(OW, out_w.rearrange("(a p) d -> p a d", p=P)).then_inc(w_loaded, 16)
            sp.dma_start(SL[:, :], slopes.rearrange("(h a) -> h a", a=1)).then_inc(slope_loaded, 16)
            sp.dma_start(RW[:, :, 0:E], w_router.rearrange("(a p) e -> p a e", p=P)).then_inc(rw_loaded, 16)
            sp.dma_start(RW[:, :, E:E + 1], w_sg.rearrange("(a p) e -> p a e", p=P),
                         allow_slow_non_contiguous=True).then_inc(rw_loaded, 16)
            for tile, row in ((WN, w_norm), (BV, in_b[2 * D:3 * D]), (OB, out_b)):
                sp.dma_start(tile[:, :], row.partition_broadcast(P)).then_inc(row_loaded, 16)
            sp.dma_start(BVR[:, 0:D], in_b[2 * D:3 * D].rearrange("(a d) -> a d", a=1)).then_inc(row_loaded, 16)
            sp.dma_start(BQK[:, :], in_b[0:2 * D].rearrange("(m p) -> p m", p=P),
                         allow_slow_non_contiguous=True).then_inc(row_loaded, 16)
            sp.dma_start(SWG[:, :, :], sw_gate.rearrange("(a p) f -> p a f", p=P)).then_inc(sw_loaded, 16)
            sp.dma_start(SWU[:, :, :], sw_up.rearrange("(a p) f -> p a f", p=P)).then_inc(sw_loaded, 16)
            sp.dma_start(SWD[:, 0:NF - 1, :], sw_down[0:P * (NF - 1), :].rearrange("(a p) d -> p a d", p=P))\
                .then_inc(sw_loaded, 16)
            sp.dma_start(SWD[0:FSZ[-1], NF - 1, :], sw_down[P * (NF - 1):FS, :]).then_inc(sw_loaded, 16)
            sp.wait_ge(table_tile, 1)
            sp.dma_start(slot_table.rearrange("(c e) w -> c (e w)", e=E), TI[:, :, :].rearrange("p e w -> p (e w)"))\
                .then_inc(table_cleared, 16)
            sp.wait_ge(slope_rows_ready, 1)
            sp.wait_ge(int_rows_ready, 6)
            for b in range(B):
                qa = q_alibi[b * H:(b + 1) * H, 3:15].rearrange("h (p r) s -> h p r s", r=4)
                ka = k_alibi[b * H:(b + 1) * H, 3:15].rearrange("h (p r) s -> h p r s", r=4)
                for dst, r, src in ((qa, 0, None), (qa, 2, None), (ka, 1, None), (ka, 3, None),
                                    (ka, 0, 0), (ka, 2, 1), (qa, 1, 2), (qa, 3, 3)):
                    source = SROW if src is None else \
                        IROW[:, src:src + 1, :].broadcast_to([H, 3, S])
                    sp.dma_start(dst[:, :, r, :], source).then_inc(alibi_stored, 16)
                sp.dma_start(k_alibi[b * H:(b + 1) * H, 0:3], ONER.unsqueeze(1).broadcast_to([H, 3, S]))\
                    .then_inc(alibi_stored, 16)
                sp.dma_start(q_alibi[b * H:(b + 1) * H, 0:3], ZROW.unsqueeze(1).broadcast_to([H, 3, S]))\
                    .then_inc(alibi_stored, 16)
            sp.wait_ge(xn_ready, NT)
            sp.dma_start(moe_rows[0:T].rearrange("(t p) d -> p t d", p=P), XN[:, :, :]).then_inc(moe_started, 16)
            sp.dma_start(moe_rows[T:T + CAP], XN[:, 0, :]).then_inc(moe_started, 16)
            sp.wait_ge(xf_ready, NT)
            sp.dma_start(xf_rows.rearrange("(t p) d -> p t d", p=P), XF).then_inc(xf_stored, 16)
            for n in range(16):
                b, tg, m = n // 8, n // 4 % 2, n % 4
                parts = (q_parts if m < 2 else k_parts)
                r0 = b * D + m % 2 * P
                sp.wait_ge(split_ready, n + 1)
                sp.dma_start(parts[:, r0:r0 + P, tg * 512:(tg + 1) * 512].rearrange("a p t -> p a t"), SPL[n % 3])\
                    .then_inc(split_stored[n % 3], 16)
            for r in range(3):
                sp.wait_ge(split_stored[r], 16 * len(range(r, 16, 3)))
            sp.wait_ge(alibi_stored, 16 * 10 * B)
            sp.wait_ge(xf_stored, 16)
            for n in range(XF0, XF0 + 8):
                sp.wait_ge(pro_free[n % 8], n // 8 + 1)

            def load_unit(u_head, u, slot):
                for dst, rows in ((QS, q_parts), (KS, k_parts)):
                    one = (rows[:, bass.ds(u_head, DH), :])
                    t = dst[slot]
                    if dst is QS:
                        plan = ((0, 0), (1, 1), (2, 2), (3, 0), (4, 1), (5, 0))
                    else:
                        plan = ((0, 0), (1, 0), (2, 0), (3, 1), (4, 1), (5, 2))
                    for r, part in plan:
                        sp.dma_start(t[r * DH:(r + 1) * DH, :], one[part]).then_inc(stack_loaded[slot], 16)
                sp.dma_start(QS[slot][SHIFT:ROWS, :], q_alibi[bass.ds(u, 1)].rearrange("a r s -> (a r) s"))\
                    .then_inc(stack_loaded[slot], 16)
                sp.dma_start(KS[slot][SHIFT:ROWS, :], k_alibi[bass.ds(u, 1)].rearrange("a r s -> (a r) s"))\
                    .then_inc(stack_loaded[slot], 16)
                sp.dma_start(WG[slot][:, :, :], w_gate[bass.ds(u, 1)].rearrange("o (a p) f -> p (o a) f", p=P))\
                    .then_inc(expert_loaded[slot], 16)
                sp.dma_start(WU[slot][:, :, :], w_up[bass.ds(u, 1)].rearrange("o (a p) f -> p (o a) f", p=P))\
                    .then_inc(expert_loaded[slot], 16)
                sp.dma_start(WD[slot][:, :, :], w_down[bass.ds(u, 1)].rearrange("o (a p) d -> p (o a) d", p=FE))\
                    .then_inc(expert_loaded[slot], 16)

            for u in range(3):
                load_unit(u * DH, u, u)

            def phase(it, k):
                hold(sp, p2_ready, unit(it, k, NQ))
                bank_, before = aux(it, k - 1, DN)
                hold(sp, aux_ready[bank_], before + 1)
                load_unit(unit(it, k, DH, 3 * DH), unit(it, k, 1, 3), (k + 3) % SLOTS)
                store_heads(it, k - 1)

            def store_heads(it, k):
                hold(sp, o_evacuated, unit(it, k, 1, 1))
                rows = att_rows[bass.ds(unit(it, k, DH), DH), :].rearrange("d (t q) -> d t q", q=P)
                for c in range(4):
                    sp.dma_start(rows[:, c:NQ - c:NQ - 1 - 2 * c, :], OEV[32 * c:32 * c + DH, k % SLOTS, :, :])\
                        .then_inc(o_stored[k % SLOTS], 16)

            for r in range(SLOTS):
                sp.sem_inc(o_stored[r], 64)
            load_unit(3 * DH, 3, 3)
            with sp.Fori(0, UNITS // SLOTS - 1) as it:
                for k in range(1, SLOTS + 1):
                    phase(it, k)
            for k in range(SLOTS):
                store_heads(UNITS // SLOTS - 1, k)
            for r in range(SLOTS):
                sp.wait_ge(o_stored[r], 64 * (UNITS // SLOTS + 1))
            sp.dma_start(ATTS, att_rows.rearrange("(b a p) t -> p b a t", b=B, p=P)).then_inc(fin_loaded, 16)
            sp.wait_ge(pv_done, UNITS * NQ)
            sp.dma_start(X, x_t).then_inc(fin_loaded, 16)
            sp.wait_ge(moe_added, 16 * UNITS)
            sp.dma_start(XN[:, :, :], moe_rows[0:T].rearrange("(t p) d -> p t d", p=P)).then_inc(fin_loaded, 16)
            out_t = out.rearrange("b (t p) d -> p (b t) d", p=P)
            for g in range(NT // 2):
                sp.wait_ge(fin_out, g + 1)
                sp.dma_start(out_t[:, 2 * g:2 * g + 2, :], X[:, 2 * g:2 * g + 2, :]).then_inc(stored, 16)
            sp.wait_ge(stored, 16 * (NT // 2))

        @block.tensor
        def _(pe):
            def begin(n):
                if n >= 8:
                    pe.wait_ge(pro_free[n % 8], n // 8)
                return bank(n)

            pe.wait_ge(w_loaded, 32)
            pe.wait_ge(mask_ready, 5)
            for m in range(4):
                o = begin(W0 + m)
                for a in range(2):
                    for c in range(KC):
                        src = INW[:, 2 * m + a, c * P:(c + 1) * P] if m < 3 else OW[:, a, c * P:(c + 1) * P]
                        ins = pe.transpose(o[:, (2 * a + c) * P:(2 * a + c + 1) * P], src, IDF[:, :])
                ins.then_inc(pro_ready[(W0 + m) % 8], 1)
            for base, src_t, ready in ((XN0, XN, xn_ready), (XF0, XF, xf_ready)):
                for g in range(8):
                    o = begin(base + g)
                    pe.wait_ge(ready, 2 * g + 2)
                    for a in range(2):
                        for c in range(KC):
                            ins = pe.transpose(o[:, (2 * a + c) * P:(2 * a + c + 1) * P],
                                               src_t[:, 2 * g + a, c * P:(c + 1) * P], IDF[:, :])
                    ins.then_inc(pro_ready[(base + g) % 8], 1)
            pe.wait_ge(rw_loaded, 32)
            for g in range(2):
                o = begin(R0 + g)
                pe.wait_ge(pro_free[(XF0 + 4 * g + 3) % 8], (XF0 + 4 * g + 3) // 8 + 1)
                for q in range(4):
                    n = XF0 + 4 * g + q
                    pe.wait_ge(pro_free[n % 8], n // 8 + 1)
                for a in range(8):
                    t = 8 * g + a
                    for c in range(KC):
                        ins = pe.matmul(o[:, 64 * a:64 * a + E + 1], XFT[:, c, t * P:(t + 1) * P], RW[:, c, :],
                                        start=(c == 0), stop=(c == KC - 1))
                ins.then_inc(pro_ready[(R0 + g) % 8], 1)
            for n in range(W0, XF0):
                pe.wait_ge(pro_free[n % 8], n // 8 + 1)

            def qk(b):
                for j in range(8):
                    n = (QK0 if b == 0 else QK1) + j
                    tg, m = 2 * b + j // 4, j % 4
                    o = begin(n)
                    for c in range(KC):
                        ins = pe.matmul(o, WIT[:, c, m * P:(m + 1) * P], XNT[:, c, tg * 512:(tg + 1) * 512],
                                        start=(c == 0), stop=(c == KC - 1))
                    ins.then_inc(pro_ready[n % 8], 1)

            qk(0)
            o = begin(POS0)
            pe.wait_ge(onehot_ready, 1)
            pe.matmul(o, LT[:, :], MB[:, :, :].rearrange("p t e -> p (t e)"), start=True, stop=False)
            pe.matmul(o, ONEB[:, :], MC[:, :, :].rearrange("p t e -> p (t e)"), start=False, stop=True)\
                .then_inc(pro_ready[POS0 % 8], 1)
            qk(1)
            for g in range(8):
                o = begin(V0 + g)
                for a in range(2):
                    t = 2 * g + a
                    for c in range(KC):
                        ins = pe.matmul(o[:, a * D:(a + 1) * D], XNT[:, c, t * P:(t + 1) * P],
                                        WIT[:, c, 2 * D:3 * D], start=(c == 0), stop=(c == KC - 1))
                ins.then_inc(pro_ready[(V0 + g) % 8], 1)
            o = begin(U0)
            pe.wait_ge(tsum_ready, 1)
            pe.wait_ge(row_loaded, 80)
            pe.wait_ge(const_ready, 3)
            pe.wait_ge(int_rows_ready, 6)
            for h in range(H):
                for c in range(4):
                    oo = o[32 * c:32 * c + 32, 4 * h:4 * h + 4]
                    v0 = 2 * D + DH * h
                    for a in range(KC):
                        pe.matmul(oo, WIT[:, a, v0:v0 + 2 * DH], XS2[:, a, :, c:NQ - c:NQ - 1 - 2 * c],
                                  start=(a == 0), stop=False)
                    ins = pe.matmul(oo, BVR[:, DH * h:DH * h + 2 * DH], CNT[:, :, c:NQ - c:NQ - 1 - 2 * c],
                                    start=False, stop=True)
            ins.then_inc(pro_ready[U0 % 8], 1)
            for b in range(8):
                pe.wait_ge(pro_free[b], PRO_TASKS // 8)

            def pass1(it, k, s, n=None):
                i = step_tile(s)
                du = 1 if s < NQ // 2 else 2
                if n is not None:
                    k = ahead_unit(n)
                slot = (k + du) % SLOTS
                base = P1_BANK[s] * 512
                if s == NQ // 2:
                    pe.wait_ge(stack_loaded[slot], turn(it, k + 2, SLOTS, 14 * 16, 14 * 16))
                used = {0: -1, 1: 0, 2: 1, 3: 2, 4: 3, 5: 3, 6: 5, 7: 4}[s]
                if n is None or unit(0, k, NQ, AHEAD + used) > 0:
                    pe.wait_ge(exp1_done, unit(it, k, NQ, AHEAD + used))
                if n is None and s == 1:
                    pe.wait_ge(exp2_done, unit(it, k, NQ))
                w = P * (i + 1)
                q = QS[slot][0:ROWS, i * P:(i + 1) * P]
                for c0 in range(0, w, 512):
                    c1 = min(c0 + 512, w)
                    pe.matmul(psf[:, base + c0:base + c1], q, KS[slot][0:ROWS, c0:c1],
                              start=True, stop=(c1 < w), skip_group_check=True)
                pe.matmul(psf[:, base + i * P:base + w], IDB[:, :], MQ[:, :],
                          start=False, stop=True, skip_group_check=True).then_inc(p1_ready, 1)

            def pass2(it, k, s, last):
                j = step_tile(s)
                slot = k % SLOTS
                base = P2_BANK[s] * 512
                if s == 0:
                    pe.wait_ge(c_rows_ready, unit(it, k, 2, 2))
                if s == 4 and not last:
                    pe.wait_ge(exp1_done, unit(it, k, NQ, AHEAD + 4))
                pe.wait_ge(exp2_done, unit(it, k, NQ, s))
                w = P * (NQ - j)
                key = KS[slot][0:ROWS, j * P:(j + 1) * P]
                for c0 in range(0, w, 512):
                    c1 = min(c0 + 512, w)
                    pe.matmul(psf[:, base + c0:base + c1], key, QS[slot][0:ROWS, j * P + c0:j * P + c1],
                              start=True, stop=(c0 > 0), skip_group_check=True)
                pe.matmul(psf[:, base:base + P], IDB[:, :], MK[:, :],
                          start=False, stop=True, skip_group_check=True).then_inc(p2_ready, 1)

            def values(it, k, s):
                j = step_tile(s)
                par = k % 2
                if s == 0:
                    pe.wait_ge(o_evacuated, unit(it, k))
                    pe.wait_ge(v_ready, unit(it, k, 1, 1))
                pe.wait_ge(clamp_done, unit(it, k, NQ, s + 1))
                probs = PB[:, par, prob_offset(s):prob_offset(s) + (s + 1) * P].rearrange("p (t q) -> p t q", q=P)
                for c in (3, 2, 1, 0):
                    far = NQ - 1 - c
                    if far < j:
                        continue
                    o = PSB[32 * c:32 * c + 32, O_BANK, 0:2 * P].rearrange("p (t q) -> p t q", q=P)
                    v = VH[:, par, j, :]
                    if c >= j:
                        ins = pe.matmul(o, v, probs[:, c - j:far - j + 1:far - c, :],
                                        start=False, stop=(j == 0), skip_group_check=True)
                    else:
                        ins = pe.matmul(o[:, 1, :], v, probs[:, far - j, :],
                                        start=(far == j), stop=False, skip_group_check=True)
                ins.then_inc(pv_done, 1)

            def aux_begin(it, k, task, last=False):
                order = [t for t in range(AUX_TASKS) if not (last and t in (CB, CA))]
                a = order.index(task)
                if a >= 2:
                    pe.wait_ge(*aux_done(it, k, order[a - 2]))
                elif k >= 1:
                    pe.wait_ge(*aux_done(it, k - 1, CA if a == 0 else DN))
                else:
                    pe.wait_ge(c_rows_ready, a + 1)
                b, _ = aux(it, k, a)
                return PSB[:, AUX + b, :], aux_ready[b]

            def c_transpose(o, ready, half, parts_count):
                pe.wait_ge(c_parts_ready, parts_count)
                for i in range(4):
                    ins = pe.transpose(o[SHIFT:SHIFT + 3, i * P // 2:(i + 1) * P // 2].bitcast(BF16),
                                       C3[:, half, i, :], IDB[:, :])
                ins.then_inc(ready, 1)

            def expert_transpose(it, k, o, ready):
                pe.wait_ge(xe_loaded[k % 2], turn(it, k, 2, 16, 16))
                for c in range(KC):
                    ins = pe.transpose(o[:, c * P:(c + 1) * P], XE[:, k % 2, c * P:(c + 1) * P], IDF[:, :])
                ins.then_inc(ready, 1)

            def expert_up(it, k, o, ready):
                slot = k % SLOTS
                pe.wait_ge(expert_loaded[slot], turn(it, k, SLOTS, 48, 48))
                pe.wait_ge(xet_ready, unit(it, k, 1, 1))
                for n, w in enumerate((WG[slot], WU[slot])):
                    for f in range(2):
                        for c in range(KC):
                            ins = pe.matmul(o[0:FE, (2 * n + f) * P:(2 * n + f + 1) * P],
                                            w[:, c, f * FE:(f + 1) * FE], XET[:, c, :],
                                            start=(c == 0), stop=(c == KC - 1))
                ins.then_inc(ready, 1)

            def expert_down(it, k, o, ready):
                slot = k % SLOTS
                pe.wait_ge(silu_done, silu(it, k, GU) + 1)
                for f in range(2):
                    ins = pe.matmul(o[:, 0:D], HE[:, f, :], WD[slot][:, f, :], start=(f == 0), stop=(f == 1))
                ins.then_inc(ready, 1)

            def shared(it, k, task, part, last):
                slot, which = k % SLOTS, 0 if task == SA else 1
                b, _ = aux(it, k, aux_index(task, last))
                o, ready = PSB[:, AUX + b, :], aux_ready[b]
                if part == 0:
                    aux_begin(it, k, task, last)
                if slot < 3:
                    ch = 2 * slot + which
                    m = FSZ[ch]
                    if ch == 0 and part == 0:
                        pe.wait_ge(block_ready, turn(it, k, SLOTS, 1, 1))
                    w = SWU if part else SWG
                    for c in range(KC):
                        ins = pe.matmul(o[0:m, part * BLK:(part + 1) * BLK], w[:, c, ch * P:ch * P + m], XFB[:, c, :],
                                        start=(c == 0), stop=(c == KC - 1))
                else:
                    if which == 0 and part == 0:
                        pe.wait_ge(silu_done, silu(it, k, GU))
                    for ch in range(3 * part, 3 * part + 3):
                        m = FSZ[ch]
                        ins = pe.matmul(o[:, 0:D], HS[0:m, ch, which * P:(which + 1) * P], SWD[0:m, ch, :],
                                        start=(ch == 0), stop=(ch == NF - 1))
                if part:
                    ins.then_inc(ready, 1)

            for n in range(AHEAD):
                pass1(0, None, (n + NQ // 2) % NQ, n)
            for half in range(2):
                c_transpose(PSB[:, AUX + half, :], aux_ready[half], half, half + 1)
            pe.wait_ge(sw_loaded, 64)

            def phase(it, k, first, ahead):
                last = ahead == 0
                for s in range(NQ):
                    if s < ahead:
                        pass1(it, k, s)
                    pass2(it, k, s, last)
                    if s >= 2:
                        values(it, k, s - 2)
                    elif not first:
                        values(it, k - 1, s + 6)
                    if s == 0:
                        if not first:
                            expert_down(it, k - 1, *aux_begin(it, k - 1, DN))
                        expert_transpose(it, k, *aux_begin(it, k, TR))
                    if s in (1, 2):
                        shared(it, k, SA, s - 1, last)
                    if s == 3 and not last:
                        c_transpose(*aux_begin(it, k, CB), 0, unit(it, k, 2, 3))
                    if s == 4:
                        expert_up(it, k, *aux_begin(it, k, GU, last))
                    if s in (5, 6):
                        shared(it, k, SB, s - 5, last)
                    if s == 6 and not last:
                        c_transpose(*aux_begin(it, k, CA), 1, unit(it, k, 2, 4))

            phases(pe, phase)
            values(UNITS // SLOTS - 1, SLOTS - 1, 6)
            values(UNITS // SLOTS - 1, SLOTS - 1, 7)
            expert_down(UNITS // SLOTS - 1, SLOTS - 1, *aux_begin(UNITS // SLOTS - 1, SLOTS - 1, DN, True))
            pe.wait_ge(fin_loaded, 48)
            pe.wait_ge(o_evacuated, UNITS)
            pe.wait_ge(exp2_done, UNITS * NQ)
            for g in range(NT // 2):
                for a in range(2):
                    t = 2 * g + a
                    b, tb = t // NQ, t % NQ
                    for c in range(KC):
                        ins = pe.matmul(PSB[:, g, a * D:(a + 1) * D], ATTS[:, b, c, tb * P:(tb + 1) * P],
                                        OWT[:, c, :], start=(c == 0), stop=(c == KC - 1))
                ins.then_inc(fin_mm, 1)

        @block.scalar
        def _(act):
            def task(n):
                act.wait_ge(pro_ready[n % 8], n // 8 + 1)
                return bank(n)

            def evacuate(n, dst, src):
                act.activation(dst, src, ACT.Copy).then_inc(pro_free[n % 8], 1)

            act.wait_ge(stat_ready, 1)
            act.activation(NRM[:, 1, :], NRM[:, 0, :], ACT.Sqrt).then_inc(sqrt_ready, 1)
            for m in range(3):
                n = W0 + m
                evacuate(n, WIT[:, :, 2 * m * P:(2 * m + 2) * P].rearrange("p c (a m) -> p a c m", a=2),
                         task(n).rearrange("p (a c m) -> p a c m", a=2, c=KC))
            evacuate(W0 + 3, OWT[:, :, :].rearrange("p c (a m) -> p a c m", a=2),
                     task(W0 + 3).rearrange("p (a c m) -> p a c m", a=2, c=KC))
            for t in range(NT):
                act.wait_ge(xn_ready, t + 1)
                if t >= 2:
                    act.wait_ge(ss_ready, t - 1)
                act.activation(SQJ[:, t % 2, :], XN[:, t, :], ACT.Square, accum_out=SS[:, t:t + 1])\
                    .then_inc(ss_ready, 1)
            act.wait_ge(stat_ready, 2)
            act.activation(NR2[:, 1, :], NR2[:, 0, :], ACT.Sqrt).then_inc(sqrt_ready, 1)
            act.preload_act_table_set("exp_and_others")
            for base, dst in ((XN0, XNT), (XF0, XFT)):
                for g in range(8):
                    n = base + g
                    evacuate(n, dst[:, :, 2 * g * P:(2 * g + 2) * P].rearrange("p c (a m) -> p a c m", a=2),
                             task(n).rearrange("p (a c m) -> p a c m", a=2, c=KC))
            for g in range(2):
                n = R0 + g
                evacuate(n, LG[:, 8 * g:8 * g + 8, :],
                         task(n).rearrange("p (t e) -> p t e", e=64)[:, :, 0:E + 1])

            def qk(b):
                for j in range(8):
                    n, i, m = (QK0 if b == 0 else QK1) + j, 8 * b + j, j % 4
                    o = task(n)
                    if i >= 3:
                        act.wait_ge(split_ready, i - 2)
                    act.activation(QV[i % 3], o, ACT.Identity, bias=BQS[:, m:m + 1],
                                   scale=SCALE if m < 2 else 1.0).then_inc(pro_free[n % 8], 1)

            act.wait_ge(router_shifted, 1)
            act.activation(LE[:, :, :], LS0[:, :, :], ACT.Exp).then_inc(router_exp, 1)
            act.activation(W4E[:, :, :], W4[:, :, :], ACT.Exp).then_inc(router_exp, 1)
            act.activation(SGE[:, :], LG[:, :, E], ACT.Tanh, scale=0.5).then_inc(router_exp, 1)
            qk(0)
            qk(1)
            o = task(U0)
            act.activation(UL[:, :, :].rearrange("p (b h) s -> p h b s", b=B),
                           o[:, 0:4 * H].rearrange("p (h b s) -> p h b s", h=H, b=B), ACT.Copy)\
                .then_inc(pro_free[U0 % 8], 1)

            def exp1(it, k, s):
                i, par = step_tile(s), (k + 1 + (s >= NQ // 2)) % 2
                base = P1_BANK[s] * 512
                sc = psf[:, base:base + (i + 1) * P]
                act.wait_ge(max_ready, unit(it, k, NQ, AHEAD + s + 1))
                act.activation(sc, sc, ACT.Exp, bias=NEGM[:, par, i:i + 1],
                               accum_out=LSUM[:, par, i:i + 1]).then_inc(exp1_done, 1)

            def exp2(it, k, s):
                base = P2_BANK[s] * 512
                if s == 0 and k >= 1:
                    act.wait_ge(pv_done, unit(it, k, NQ, 1 - NQ))
                act.wait_ge(p2_ready, unit(it, k, NQ, s + 1))
                act.activation(PB[:, k % 2, prob_offset(s):prob_offset(s) + (s + 1) * P],
                               psf[:, base:base + (s + 1) * P], ACT.Exp).then_inc(exp2_done, 1)

            def exp_seed(it, k, half):
                n = unit(it, k, 2, half)
                act.wait_ge(seed_ready, n + 1)
                act.activation(LEX[:, half, :], LNS[:, half, :], ACT.Exp).then_inc(seed_exp, 1)

            def aux_task(it, k, a):
                b, before = aux(it, k, a)
                act.wait_ge(aux_ready[b], before + 1)
                return PSB[:, AUX + b, :]

            def tanh_gate(it, k, a, task_, rows):
                z = silu_index(k, task_)
                o = aux_task(it, k, a)
                if z >= 2:
                    act.wait_ge(silu_done, silu(it, k, task_) - 1)
                act.activation(ET[0:rows, z % 2, :], o[0:rows, 0:BLK], ACT.Tanh, scale=0.5)\
                    .then_inc(tanh_ready, 1)

            def shared(it, k, a, task_):
                which = 0 if task_ == SA else 1
                slot = k % SLOTS
                if slot < 3:
                    tanh_gate(it, k, a, task_, FSZ[2 * slot + which])
                else:
                    o = aux_task(it, k, a)
                    t = turn(it, k, SLOTS, 2, which)
                    act.wait_ge(scale_ready, turn(it, k, SLOTS, 1, 1))
                    dst = SH[:, t, :] if isinstance(t, int) else SH[:, bass.ds(t, 1), :].rearrange("p o d -> p (o d)")
                    act.activation(dst, o[:, 0:D], ACT.Copy, scale=SGB[:, which:which + 1]).then_inc(shared_out, 1)

            for n in range(AHEAD):
                exp1(0, ahead_unit(n), (n + NQ // 2) % NQ)
                if n in (5, 9):
                    exp_seed(0, 0, n // 8)

            def weigh(it, k, last):
                o = aux_task(it, k, aux_index(DN, last))
                act.wait_ge(idx_ready, unit(it, k, 1, 1))
                if k >= 1:
                    act.wait_ge(ye_free, unit(it, k))
                act.activation(YE[:, k % 2, :], o[:, 0:D], ACT.Copy,
                               scale=IDX[:, k % SLOTS, 1:2].bitcast(F32)).then_inc(ye_ready, 1)

            def phase(it, k, first, ahead):
                last = ahead == 0
                ix = lambda t: aux_index(t, last)
                for s in range(NQ):
                    exp2(it, k, s)
                    if s == 1:
                        if not first:
                            weigh(it, k - 1, False)
                        o = aux_task(it, k, ix(TR))
                        act.activation(XET[:, :, :].rearrange("p c m -> p (c m)"), o[:, 0:D], ACT.Copy)\
                            .then_inc(xet_ready, 1)
                        if not last:
                            exp_seed(it, k + 1, 0)
                    if s == 4 and not last:
                        exp_seed(it, k + 1, 1)
                    if s == 3:
                        shared(it, k, ix(SA), SA)
                    if s == 5:
                        tanh_gate(it, k, ix(GU), GU, FE)
                    if s == 7:
                        shared(it, k, ix(SB), SB)
                    if s < ahead:
                        exp1(it, k, s)

            phases(act, phase)
            weigh(UNITS // SLOTS - 1, SLOTS - 1, True)
            for g in range(NT // 2):
                act.wait_ge(fin_z, g + 1)
                e = XFT[:, :, :].rearrange("p c n -> p (c n)")[:, 512 * g:512 * (g + 1)]
                act.activation(e, XN[:, 2 * g:2 * g + 2, :].rearrange("p a d -> p (a d)"), ACT.Tanh, scale=0.5).then_inc(fin_e, 1)

        @block.vector
        def _(dve):
            link = Link(dve, dve_self)

            def root(stats, n):
                dve.wait_ge(sqrt_ready, n)
                link(dve.reciprocal(stats[:, 2, :], stats[:, 1, :]))
                link(dve.tensor_tensor(stats[:, 3, :], stats[:, 2, :], stats[:, 2, :], ALU.mult))
                link(dve.tensor_tensor(stats[:, 4, :], stats[:, 3, :], stats[:, 0, :], ALU.mult))
                link(dve.tensor_scalar(stats[:, 3, :], stats[:, 4, :], -0.5, 1.5, ALU.mult, ALU.add))
                link(dve.tensor_tensor(stats[:, 5, :], stats[:, 3, :], stats[:, 2, :], ALU.mult))

            for t in range(NT):
                dve.wait_ge(x_loaded[t // 4], 16)
                ins = dve.bn_stats(BNS[:, t, :], XN[:, t, :])
                if t == NT - 1:
                    link(ins)
                else:
                    ins.then_inc(dve_self, 1)
                    link.n += 1
            for t in range(NT):
                ins = dve.bn_aggr(MV[:, t, :], BNS[:, t, :])
                ins.then_inc(dve_self, 1)
                link.n += 1
            dve.wait_ge(dve_self, link.n)
            dve.tensor_scalar(NRM[:, 0, :], MV[:, :, 1], LN_EPS, None, ALU.add).then_inc(stat_ready, 1)
            dve.wait_ge(slope_loaded, 16)
            dve.wait_ge(alibi_ready, 1)
            link(dve.tensor_copy(SLB[:, 0:1], SL[:, :]))
            link(dve.tensor_tensor(SLR[:, 0:1], SL[:, :], SLB[:, 0:1], ALU.subtract))
            link(dve.tensor_copy(SLB[:, 1:2], SLR[:, 0:1]))
            link(dve.tensor_tensor(SLR[:, 1:2], SLR[:, 0:1], SLB[:, 1:2], ALU.subtract))
            link(dve.tensor_copy(SLB[:, 2:3], SLR[:, 1:2]))
            link(dve.tensor_copy(SLP[:, :], SLB[:, :]))
            for p in range(3):
                ins = dve.tensor_scalar(SROW[:, p, :], ONER, SLP[:, p:p + 1], None, ALU.mult)
                if p < 2:
                    link(ins)
            ins.then_inc(slope_rows_ready, 1)
            root(NRM, 1)
            for t in range(NT):
                dve.tensor_scalar(XN[:, t, :], XN[:, t, :], MV[:, t, 0:1], NRM[:, 5, t:t + 1],
                                  ALU.subtract, ALU.mult).then_inc(xn_ready, 1)
            dve.wait_ge(row_loaded, 80)
            link(dve.tensor_scalar(BQS[:, 0:2], BQK[:, 0:2], SCALE, None, ALU.mult))
            link(dve.tensor_copy(BQS[:, 2:4], BQK[:, 2:4]))
            dve.wait_ge(ss_ready, NT)
            dve.tensor_scalar(NR2[:, 0, :], SS[:, :], 1.0 / D, RMS_EPS, ALU.mult, ALU.add).then_inc(stat_ready, 1)
            dve.wait_ge(stat_ready, 2)
            root(NR2, 2)
            dve.wait_ge(xn_ready, NT)
            for t in range(NT):
                dve.scalar_tensor_tensor(out=XF[:, t, :], in0=XN[:, t, :], scalar=NR2[:, 5, t:t + 1],
                                         in1=WN[:, :], op0=ALU.mult, op1=ALU.mult).then_inc(xf_ready, 1)
            for n in (R0, R0 + 1):
                dve.wait_ge(pro_free[n % 8], n // 8 + 1)
            for t in range(NT):
                dve.max(V8[:, t, :], LG[:, t, 0:E]).then_inc(dve_self, 1)
                link.n += 1
            dve.wait_ge(dve_self, link.n)
            link(dve.tensor_tensor(LS0[:, :, :], LG[:, :, 0:E], V8[:, :, 0:1].broadcast_to([P, NT, E]), ALU.subtract))
            link(dve.tensor_tensor(W4[:, :, :], V8[:, :, 0:TOPK], V8[:, :, 0:1].broadcast_to([P, NT, TOPK]),
                                   ALU.subtract))
            for t in range(NT):
                ins = dve.max_index(I8[:, t, :], V8[:, t, :], LG[:, t, 0:E])
                if t == 0:
                    ins.then_inc(router_shifted, 1)
                else:
                    ins.then_inc(dve_self, 1)
                    link.n += 1
            dve.wait_ge(dve_self, link.n)
            dve.wait_ge(router_shifted, 1)
            link(dve.tensor_copy(IDXF[:, :, :], I8[:, :, 0:TOPK]))
            dve.wait_ge(const_ready, 3)
            for n in range(W0, W0 + 4):
                dve.wait_ge(pro_free[n % 8], 1)
            link(dve.tensor_tensor(OH, IO32[:, :].unsqueeze(1).unsqueeze(1).broadcast_to([P, NT, TOPK, E]),
                                   IDXF[:, :, :].unsqueeze(3).broadcast_to([P, NT, TOPK, E]), ALU.is_equal))
            link(dve.tensor_tensor(PROD[:, :, 0:2, :], OH[:, :, 0:2, :], OH[:, :, 2:4, :], ALU.add))
            link(dve.tensor_tensor(MB[:, :, :], PROD[:, :, 0, :], PROD[:, :, 1, :], ALU.add))
            link(dve.memset(MC[:, 0, :], 0.0))
            for t in range(1, NT):
                ins = dve.tensor_tensor(MC[:, t, :], MC[:, t - 1, :], MB[:, t - 1, :], ALU.add)
                if t < NT - 1:
                    link(ins)
            ins.then_inc(onehot_ready, 1)

            def qk_split(b):
                for j in range(8):
                    n, i = (QK0 if b == 0 else QK1) + j, 8 * b + j
                    r = i % 3
                    dve.wait_ge(pro_free[n % 8], n // 8 + 1)
                    if i >= 3:
                        dve.wait_ge(split_stored[r], 16 * (i // 3))
                    link(dve.tensor_copy(SPL[r][:, 0, :], QV[r]))
                    link(dve.tensor_tensor(QV[r], QV[r], SPL[r][:, 0, :], ALU.subtract))
                    link(dve.tensor_copy(SPL[r][:, 1, :], QV[r]))
                    dve.tensor_tensor(SPL[r][:, 2, :], QV[r], SPL[r][:, 1, :], ALU.subtract).then_inc(split_ready, 1)

            dve.wait_ge(router_exp, 3)
            link(dve.tensor_reduce(ZS[:, :], LE[:, :, :], AX_X, ALU.add))
            link(dve.reciprocal(ZR[:, :], ZS[:, :]))
            dve.wait_ge(token_ids, 3)
            link(dve.tensor_tensor(RWS[:, :, :, 1].bitcast(F32), W4E[:, :, :],
                                   ZR[:, :].unsqueeze(2).broadcast_to([P, NT, TOPK]), ALU.mult))
            link(dve.tensor_scalar(SG[:, :], SGE[:, :], 0.5, 0.5, ALU.mult, ALU.add))
            pos = bank(POS0).rearrange("p (t e) -> p t e", e=E)
            dve.wait_ge(pro_ready[POS0 % 8], POS0 // 8 + 1)
            dve.tensor_tensor(PROD, OH, pos.unsqueeze(2).broadcast_to([P, NT, TOPK, E]), ALU.mult)\
                .then_inc(pro_free[POS0 % 8], 1)
            dve.wait_ge(pro_free[POS0 % 8], POS0 // 8 + 1)
            link(dve.tensor_reduce(PK[:, :, :], PROD, AX_X, ALU.add))
            link(dve.tensor_scalar(BAD[:, :, :], PK[:, :, :], float(CAP), float(CAP * E), ALU.is_ge, ALU.mult))
            link(dve.scalar_tensor_tensor(out=DST[:, :, :], in0=PK[:, :, :], scalar=float(E), in1=IDXF[:, :, :],
                                          op0=ALU.mult, op1=ALU.add))
            link(dve.tensor_tensor(DST2[:, :, :], DST[:, :, :], BAD[:, :, :], ALU.add))
            dve.tensor_copy(DI[:, :, :], DST2[:, :, :].rearrange("p t k -> p k t")).then_inc(dest_ready, 1)
            qk_split(0)
            for n in range(XN0, XN0 + 8):
                dve.wait_ge(pro_free[n % 8], n // 8 + 1)
            link(dve.tensor_reduce(TS[:, :, :], XNT[:, :, :].rearrange("p c (t q) -> p c t q", q=P), AX_X, ALU.add))
            ts = TS[:, :, :].rearrange("p c (b t) -> p c b t", b=B)
            link(dve.memset(XS[:, :, :, NQ - 1], 0.0))
            for t in reversed(range(NQ - 1)):
                link(dve.tensor_tensor(XS[:, :, :, t], XS[:, :, :, t + 1], ts[:, :, :, t + 1], ALU.add))
            dve.tensor_scalar(XS2[:, :, :, :], XS[:, :, :, :], FLOOR, None, ALU.mult).then_inc(tsum_ready, 1)
            qk_split(1)
            dve.wait_ge(alibi_stored, 16 * 10 * B)
            for g in range(8):
                n = V0 + g
                dve.wait_ge(pro_ready[n % 8], n // 8 + 1)
                for a in range(2):
                    t = 2 * g + a
                    b = t // NQ
                    ins = dve.tensor_tensor(VS[:, b * H:(b + 1) * H, DH * (t % NQ):DH * (t % NQ + 1)],
                                            bank(n)[:, a * D:(a + 1) * D].rearrange("p (h d) -> p h d", d=DH),
                                            BV[:, :].rearrange("p (h d) -> p h d", d=DH), ALU.add)
                    if a == 0:
                        link(ins)
                ins.then_inc(pro_free[n % 8], 1)

            def row_max(it, k, s):
                i, par = step_tile(s), (k + 1 + (s >= NQ // 2)) % 2
                base = P1_BANK[s] * 512
                dve.wait_ge(p1_ready, unit(it, k, NQ, AHEAD + s + 1))
                dve.tensor_reduce(NEGM[:, par, i:i + 1], psf[:, base:base + (i + 1) * P], AX_X, ALU.max,
                                  negate=True).then_inc(max_ready, 1)

            def clamp(it, k, s):
                dve.wait_ge(exp2_done, unit(it, k, NQ, s + 1))
                p = PB[:, k % 2, prob_offset(s):prob_offset(s) + (s + 1) * P]
                dve.tensor_scalar(p, p, FLOOR, None, ALU.max).then_inc(clamp_done, 1)

            def c_rows(semaphore, count, b, half, slot):
                c0 = 512 * half
                dve.wait_ge(semaphore, count)
                dve.tensor_copy(QS[slot][SHIFT:SHIFT + 3, c0:c0 + 512],
                                PSB[SHIFT:SHIFT + 3, AUX + b, 0:256].bitcast(BF16)).then_inc(c_rows_ready, 1)

            def next_c_rows(it, k, task):
                b, before = aux(it, k, task)
                c_rows(aux_ready[b], before + 1, b, 0 if task == CB else 1, (k + 1) % SLOTS)

            def silu_up(it, k, a, task_, dst, rows):
                b, _ = aux(it, k, a)
                z = silu_index(k, task_)
                n = silu(it, k, task_)
                psum = PSB[0:rows, AUX + b, :]
                dve.wait_ge(tanh_ready, n + 1)
                dve.scalar_tensor_tensor(out=RT[0:rows, :], in0=ET[0:rows, z % 2, :], scalar=1.0,
                                         in1=psum[:, 0:BLK], op0=ALU.add, op1=ALU.mult).then_inc(silu_chain, 1)
                dve.wait_ge(silu_chain, n + 1)
                dve.scalar_tensor_tensor(out=dst, in0=RT[0:rows, :], scalar=0.5, in1=psum[:, BLK:2 * BLK],
                                         op0=ALU.mult, op1=ALU.mult).then_inc(silu_done, 1)

            def shared(it, k, a, task_):
                slot = k % SLOTS
                if slot == 3:
                    return
                ch = 2 * slot + (0 if task_ == SA else 1)
                if ch == 0 and k >= SLOTS:
                    b, before = aux(it, k - 1, SB)
                    dve.wait_ge(aux_ready[b], before + 1)
                silu_up(it, k, a, task_, HS[0:FSZ[ch], ch, :], FSZ[ch])

            def evacuate_heads(it, k):
                slot = k % SLOTS
                dve.wait_ge(pv_done, unit(it, k, NQ, NQ))
                dve.wait_ge(o_stored[slot], turn(it, k, SLOTS, 64, 64))
                u = unit(it, k)
                ul = UL[:, u, :] if isinstance(u, int) else UL[:, bass.ds(u, 1), :].rearrange("p o s -> p (o s)")
                dve.tensor_tensor(OEV[:, slot, :, :], PSB[:, O_BANK, 0:2 * P].rearrange("p (t q) -> p t q", q=P),
                                  ul.unsqueeze(2).broadcast_to([P, 2, P]), ALU.add).then_inc(o_evacuated, 1)

            for n in range(AHEAD):
                row_max(0, ahead_unit(n), (n + NQ // 2) % NQ)
            for half in range(2):
                c_rows(aux_ready[half], 1, half, half, 0)
            dve.wait_ge(pro_free[U0 % 8], U0 // 8 + 1)

            def phase(it, k, first, ahead):
                last = ahead == 0
                ix = lambda t: aux_index(t, last)
                for s in range(NQ):
                    if s > 0:
                        clamp(it, k, s - 1)
                    elif not first:
                        clamp(it, k - 1, NQ - 1)
                    if s < ahead:
                        row_max(it, k, s)
                    if s == 1 and not first:
                        evacuate_heads(it, k - 1)
                    if s == 3:
                        shared(it, k, ix(SA), SA)
                    if s == 4 and not last:
                        next_c_rows(it, k, CB)
                    if s == 5:
                        if not first:
                            b, before = aux(it, k - 1, DN)
                            dve.wait_ge(aux_ready[b], before + 1)
                        silu_up(it, k, ix(GU), GU, HE[:, :, :].rearrange("p f c -> p (f c)"), FE)
                    if s == 7:
                        if not last:
                            next_c_rows(it, k, CA)
                        shared(it, k, ix(SB), SB)

            phases(dve, phase)
            clamp(UNITS // SLOTS - 1, SLOTS - 1, NQ - 1)
            evacuate_heads(UNITS // SLOTS - 1, SLOTS - 1)
            dve.wait_ge(fin_loaded, 48)
            dve.wait_ge(ye_ready, UNITS)
            zf = XN[:, :, :].rearrange("p t d -> p (t d)")
            shf = SH.rearrange("p t d -> p (t d)")
            ef = XFT[:, :, :].rearrange("p c n -> p (c n)")
            vf = VS[:, :, :].rearrange("p u n -> p (u n)")
            xall = pbf[:, 0:T * D // P]
            fin = Link(dve, fin_chain)
            for g in range(NT // 2):
                c = slice(512 * g, 512 * (g + 1))
                dve.tensor_tensor(zf[:, c], zf[:, c], shf[:, c], ALU.add).then_inc(fin_z, 1)
            for g in range(NT // 2):
                c = slice(512 * g, 512 * (g + 1))
                dve.wait_ge(fin_e, g + 1)
                dve.wait_ge(fin_mm, g + 1)
                fin(dve.scalar_tensor_tensor(out=zf[:, c], in0=ef[:, c], scalar=1.0, in1=zf[:, c],
                                             op0=ALU.add, op1=ALU.mult))
                fin(dve.tensor_tensor(vf[:, 0:512].rearrange("p (a d) -> p a d", a=2),
                                      PSB[:, g, :].rearrange("p (a d) -> p a d", a=2),
                                      OB[:, :].unsqueeze(1).broadcast_to([P, 2, D]), ALU.add))
                fin(dve.scalar_tensor_tensor(out=vf[:, 512:1024], in0=vf[:, 0:512], scalar=0.5, in1=zf[:, c],
                                             op0=ALU.mult, op1=ALU.mult))
                dve.tensor_tensor(xall[:, c], xall[:, c], vf[:, 512:1024], ALU.add).then_inc(fin_out, 1)
                dve.wait_ge(fin_out, g + 1)

        @block.gpsimd
        def _(pool):
            link = Link(pool, pool_self)
            link(pool.memset(IDF[:, :], 0.0))
            link(pool.memset(IDB[:, :], 0.0))
            link(pool.memset(MQ[:, :], 0.0))
            link(pool.memset(MK[:, :], 0.0))
            link(pool.memset(ONEB[:, :], 1.0))
            link(pool.memset(LT[:, :], 1.0))
            link(pool.memset(WIT[:, :, 3 * D:3 * D + PAD], 0.0))
            pool.affine_select(out=IDF[:, :], in_=IDF[:, :], compare_op=ALU.not_equal, fill=1.0, base=0,
                               pattern=[[-1, P]], channel_multiplier=1).then_inc(mask_ready, 1)
            pool.affine_select(out=IDB[:, :], in_=IDB[:, :], compare_op=ALU.not_equal, fill=1.0, base=0,
                               pattern=[[-1, P]], channel_multiplier=1).then_inc(mask_ready, 1)
            pool.affine_select(out=MQ[:, :], in_=MQ[:, :], compare_op=ALU.is_ge, fill=MASK, base=0,
                               pattern=[[-1, P]], channel_multiplier=1).then_inc(mask_ready, 1)
            pool.affine_select(out=MK[:, :], in_=MK[:, :], compare_op=ALU.is_ge, fill=MASK, base=0,
                               pattern=[[1, P]], channel_multiplier=-1).then_inc(mask_ready, 1)
            pool.affine_select(out=LT[:, :], in_=LT[:, :], compare_op=ALU.is_gt, fill=0.0, base=0,
                               pattern=[[1, P]], channel_multiplier=-1).then_inc(mask_ready, 1)
            pool.memset(ONER, 1.0).then_inc(alibi_ready, 1)
            for r, pattern in enumerate(([[P, NQ], [0, P]], [[0, NQ], [1, P]], [[-P, NQ], [0, P]],
                                         [[0, NQ], [-1, P]])):
                pool.iota(IROW[:, r, :].rearrange("p (t q) -> p t q", q=P), pattern, base=0, channel_multiplier=0,
                          allow_small_or_imprecise_dtypes=True).then_inc(int_rows_ready, 1)
            pool.memset(ZROW, 0.0).then_inc(int_rows_ready, 1)
            pool.memset(BVR[:, D:D + PAD], 0.0).then_inc(int_rows_ready, 1)
            pool.iota(IO32[:, :], [[1, E]], base=0, channel_multiplier=0,
                      allow_small_or_imprecise_dtypes=True).then_inc(const_ready, 1)
            link(pool.iota(CNT[:, :, :], [[0, B], [-P, NQ]], base=P * (NQ - 1), channel_multiplier=0,
                           allow_small_or_imprecise_dtypes=True))
            pool.tensor_scalar(CNT[:, :, :], CNT[:, :, :], FLOOR, None, ALU.mult).then_inc(const_ready, 1)
            pool.memset(VH[:, :, :, :], 0.0).then_inc(const_ready, 1)
            link(pool.memset(TI[:, :, :], 0))
            pool.iota(TI[:, :, 2], [[0, E]], base=T, channel_multiplier=1).then_inc(table_tile, 1)
            link(pool.memset(RWS[:, :, :, 3], 0))
            pool.iota(RWS[:, :, :, 0], [[P, NT], [0, TOPK]], base=0, channel_multiplier=1).then_inc(token_ids, 1)
            pool.iota(RWS[:, :, :, 2], [[P, NT], [0, TOPK]], base=0, channel_multiplier=1).then_inc(token_ids, 1)
            pool.memset(RWS[:, :, :, 1], 0).then_inc(token_ids, 1)

            def chain(it, k, half):
                par, i0 = k % 2, 4 * half
                n = unit(it, k, 2, half)
                lsum, cc = LSUM[:, par, i0:i0 + 4], CC[:, half, :]
                t, a = CR[:, half, 0, :], CR[:, half, 1, :]
                hold(pool, exp1_done, unit(it, k, NQ, 4 * half + 4))
                pool.tensor_scalar(LNS[:, half, :], lsum.bitcast(I32), LN_SLOPE, LN_BASE, ALU.mult, ALU.add)\
                    .then_inc(seed_ready, 1)
                hold(pool, seed_ready, n + 1)
                if not (isinstance(it, int) and unit(it, k) == 0):
                    hold(pool, c_rows_ready, n - 1)
                pool.tensor_tensor(cc, NEGM[:, par, i0:i0 + 4], LNS[:, half, :], ALU.add).then_inc(c_chain, 1)
                hold(pool, seed_exp, n + 1)
                pool.tensor_tensor(t, lsum, LEX[:, half, :], ALU.mult).then_inc(c_chain, 1)
                hold(pool, c_chain, n * 11 + 2)
                pool.tensor_scalar(t, t, -1.0, None, ALU.add).then_inc(c_chain, 1)
                hold(pool, c_chain, n * 11 + 3)
                pool.tensor_scalar(a, t, -1 / 3, 0.5, ALU.mult, ALU.add).then_inc(c_chain, 1)
                hold(pool, c_chain, n * 11 + 4)
                pool.tensor_tensor(a, a, t, ALU.mult).then_inc(c_chain, 1)
                hold(pool, c_chain, n * 11 + 5)
                pool.tensor_scalar(a, a, -1.0, None, ALU.add).then_inc(c_chain, 1)
                hold(pool, c_chain, n * 11 + 6)
                pool.tensor_tensor(a, a, t, ALU.mult).then_inc(c_chain, 1)
                hold(pool, c_chain, n * 11 + 7)
                pool.tensor_tensor(cc, cc, a, ALU.add).then_inc(c_chain, 1)
                hold(pool, c_chain, n * 11 + 8)
                pool.tensor_copy(C3[:, half, :, 0], cc).then_inc(c_chain, 1)
                hold(pool, c_chain, n * 11 + 9)
                pool.tensor_tensor(t, cc, C3[:, half, :, 0], ALU.subtract).then_inc(c_chain, 1)
                hold(pool, c_chain, n * 11 + 10)
                pool.tensor_copy(C3[:, half, :, 1], t).then_inc(c_chain, 1)
                hold(pool, c_chain, n * 11 + 11)
                pool.tensor_tensor(C3[:, half, :, 2], t, C3[:, half, :, 1], ALU.subtract).then_inc(c_parts_ready, 1)

            pool.wait_ge(dest_ready, 1)
            pool.wait_ge(table_cleared, 16)
            for t in range(NT):
                for kk in range(TOPK):
                    pool.indirect_dma_start(
                        out=slot_table, out_offset=bass.IndirectOffsetOnAxis(ap=DI[:, kk, t:t + 1], axis=0),
                        in_=RWS[:, t, kk, :], in_offset=None, bounds_check=CAP * E - 1, oob_is_err=False)\
                        .then_inc(scattered, 16)
            pool.wait_ge(scattered, 16 * NT * TOPK)
            pool.dma_start(TABS[:, :], slot_table.rearrange("(c e) w -> c (e w)", e=E)).then_inc(table_loaded, 16)
            chain(0, 0, 0)
            chain(0, 0, 1)
            pool.wait_ge(table_loaded, 16)
            pool.wait_ge(xf_stored, 16)
            pool.wait_ge(moe_started, 32)
            for n in range(V0, V0 + 8):
                pool.wait_ge(pro_free[n % 8], n // 8 + 1)

            def sbuf_cols(tile, start, n):
                return tile[:, start:start + n] if isinstance(start, int) else tile[:, bass.ds(start, n)]

            def prepare(it, k):
                slot, par = k % SLOTS, k % 2
                if k >= 2:
                    hold(pool, pv_done, unit(it, k, NQ, -NQ))
                vflat = VS[:, :, :].rearrange("p u n -> p (u n)")
                pool.tensor_copy(VH[:, par, :, 0:DH],
                                 sbuf_cols(vflat, unit(it, k, NQ * DH), NQ * DH)
                                 .rearrange("p (t d) -> p t d", d=DH)).then_inc(v_ready, 1)
                pool.tensor_copy(IDX[:, slot, :], sbuf_cols(TABS, unit(it, k, 4), 4)).then_inc(idx_ready, 1)
                hold(pool, idx_ready, unit(it, k, 1, 1))
                if k >= 2:
                    hold(pool, xet_ready, unit(it, k, 1, -1))
                pool.indirect_dma_start(
                    out=XE[:, par, :], out_offset=None, in_=xf_rows,
                    in_offset=bass.IndirectOffsetOnAxis(ap=IDX[:, slot, 0:1].bitcast(U32), axis=0),
                    bounds_check=T - 1, oob_is_err=False).then_inc(xe_loaded[par], 16)

            def copy_block(it, k):
                c0 = turn(it, k, SLOTS, BLK)
                src = XFT[:, :, c0:c0 + BLK] if isinstance(c0, int) else XFT[:, :, bass.ds(c0, BLK)]
                pool.tensor_copy(XFB[:, :, :], src).then_inc(block_ready, 1)

            def copy_scales(it, k):
                if k >= SLOTS:
                    hold(pool, *aux_done(it, k - 1, SB))
                pool.tensor_copy(SGB[:, :], sbuf_cols(SG, turn(it, k, SLOTS, 2), 2)).then_inc(scale_ready, 1)

            def scatter(it, k):
                slot, par = k % SLOTS, k % 2
                hold(pool, ye_ready, unit(it, k, 1, 1))
                if k >= 1:
                    hold(pool, moe_added, unit(it, k, 16))
                pool.sem_inc(ye_free, 1)
                pool.indirect_dma_start(
                    out=moe_rows, out_offset=bass.IndirectOffsetOnAxis(ap=IDX[:, slot, 2:3].bitcast(U32), axis=0),
                    in_=YE[:, par, :], in_offset=None, bounds_check=T + CAP - 1, oob_is_err=True,
                    compute_op=ALU.add).then_inc(moe_added, 16)

            prepare(0, 0)
            copy_block(0, 0)

            def phase(it, k, first, ahead):
                if ahead:
                    chain(it, k + 1, 0)
                    prepare(it, k + 1)
                if not first:
                    scatter(it, k - 1)
                if k % SLOTS == 0:
                    copy_scales(it, k)
                if k % SLOTS == SLOTS - 1 and ahead:
                    b, before = aux(it, k - 1, SB)
                    hold(pool, aux_ready[b], before + 1)
                    copy_block(it, k + 1)
                if ahead:
                    chain(it, k + 1, 1)

            phases(pool, phase)
            scatter(UNITS // SLOTS - 1, SLOTS - 1)


_INS = ['L0_attn_qkv', 'L0_attn_in_proj', 'L0_attn_in_proj_bias', 'L0_attn_out_w', 'L0_attn_out_b',
        'L0_attn_alibi_slopes', 'L0_ffn_w_norm', 'L0_ffn_w_router', 'L0_ffn_w_gate', 'L0_ffn_w_up',
        'L0_ffn_w_down', 'L0_ffn_sw_gate', 'L0_ffn_sw_up', 'L0_ffn_sw_down', 'L0_ffn_w_shared_gate']


def kernel(**inputs):
    import numpy as _np
    import concourse.bacc as _bacc
    from concourse import mybir as _mybir
    from concourse.bass_utils import run_bass_kernel_spmd as _run

    nc = _bacc.Bacc("TRN2", target_bir_lowering=False, num_devices=1)
    arrays, args = {}, []
    for name in _INS:
        a = _np.ascontiguousarray(inputs[name])
        arrays[f"in_{name}_dram"] = a
        args.append(nc.dram_tensor(f"in_{name}_dram", a.shape, _mybir.dt.from_np(a.dtype), kind="ExternalInput").ap())
    args.append(nc.dram_tensor("out_0_dram", (B, S, D), _mybir.dt.float32, kind="ExternalOutput").ap())
    build(nc, *args)
    r = _run(nc, [arrays], core_ids=[0])
    return r.results[0]["out_0_dram"]
```

```python
from contextlib import ExitStack

import concourse.bass as bass
from concourse import mybir


F32 = mybir.dt.float32
F32R = mybir.dt.float32r
BF16 = mybir.dt.bfloat16
I32 = mybir.dt.int32
U32 = mybir.dt.uint32
ALU = mybir.AluOpType
ACT = mybir.ActivationFunctionType
AX_X = mybir.AxisListType.X

P = 128
B, S, D = 2, 1024, 256
T = B * S
NT = T // P
NQ = S // P
KC = D // P
H = 16
DH = D // H
E, TOPK, F, CAP = 32, 4, 176, 128
FE = F // 2
FS = 704
NF = -(-FS // P)
FSZ = [min(P, FS - P * c) for c in range(NF)]
SCALE = float(DH) ** -0.5
FLOOR = 1e-10
MASK = -1e30
LN_SLOPE = -0.6931471805599453 / (1 << 23)
LN_BASE = 0.6931471805599453 * (127 - 0.0430)
LN_EPS, RMS_EPS = 1e-5, 1e-6
UNITS = B * H
SLOTS = 4
SPLIT_ROWS = 6 * DH
SHIFT = SPLIT_ROWS
ROWS = SHIFT + 3 + 12
BLK = 256
O_BANK, AUX = 5, 6
PAD = 16

TR, SA, GU, SB, C, DN = range(6)
AUX_TASKS = 6
W0, XF0, R0, XN0, QK0, POS0, QK1, V0, U0 = 0, 4, 12, 14, 22, 26, 31, 39, 47
PRO_TASKS = 48


def qk_task(b, j):
    return QK1 + j if b else QK0 + j + (j >= 4)


def step_tile(s):
    return NQ - 1 - s


AHEAD = 2 * NQ

P1_BANK = [0, 2, 0, 2, 0, 1, 0, 2]
P2_BANK = [4, 4, 4, 4, 3, 3, 3, 3]
P2_LATE = [4, 0, 4, 0, 3, 0, 3, 0]


def prob_offset(s):
    return s * (s + 1) // 2 * P


def build(nc, x, in_proj, in_b, out_w, out_b, slopes, w_norm, w_router, w_gate, w_up, w_down,
          sw_gate, sw_up, sw_down, w_sg, out):
    ctx = ExitStack()
    with ctx:
        def sb(name, shape, dt=F32):
            return ctx.enter_context(nc.sbuf_tensor(name, shape, dt))

        def sem(name):
            return ctx.enter_context(nc.semaphore(name))

        def dram(name, shape, dt=F32):
            return nc.dram_tensor(name, shape, dt, kind="Internal").ap()

        xf_rows = dram("xf_rows", (T, D))
        moe_rows = dram("moe_rows", (T + CAP, D))
        slot_table = dram("slot_table", (CAP * E, 4), I32)
        q_parts = dram("q_parts", (3, B * D, S), BF16)
        k_parts = dram("k_parts", (3, B * D, S), BF16)
        q_alibi = dram("q_alibi", (UNITS, 15, S), BF16)
        k_alibi = dram("k_alibi", (UNITS, 15, S), BF16)
        att_rows = dram("att_rows", (B * D, S))

        XN = sb("XN", [P, NT, D])
        STACKS = sb("STACKS", [P, 2 * SLOTS, S], BF16)
        stf = STACKS[:, :, :].rearrange("p a s -> p (a s)").bitcast(F32)
        XF = stf.rearrange("p (t d) -> p t d", d=D)
        XNT = sb("XNT", [P, KC, T])
        XFT = sb("XFT", [P, KC, T])
        SH = XNT[:, :, :].rearrange("p a (t d) -> p (a t) d", d=D)
        ATTS = stf.rearrange("p (a b s) -> p a b s", b=B, a=KC)
        VS = sb("VS", [P, UNITS, NQ * DH])
        PB = sb("PB", [P, 2, 36 * P])
        pbf = PB[:, :, :].rearrange("p a n -> p (a n)")
        OH = pbf[:, 0:2048].rearrange("p (t k e) -> p t k e", t=NT, k=TOPK)
        PROD = pbf[:, 2048:4096].rearrange("p (t k e) -> p t k e", t=NT, k=TOPK)
        xagain = VS[:, :, :].rearrange("p u n -> p (u n)")
        X = xagain.rearrange("p (t d) -> p t d", d=D)
        INW = pbf[:, 0:1536].rearrange("p (a d) -> p a d", a=6)
        OW = pbf[:, 2048:2560].rearrange("p (a d) -> p a d", a=2)
        QV = [pbf[:, o:o + 512] for o in (4096, 4608, 5120, 0)]
        SPL = [pbf[:, o:o + 768].bitcast(BF16).rearrange("p (a t) -> p a t", a=3) for o in (5632, 6400, 7168, 512)]
        RING = len(SPL)
        QS = [STACKS[:, r, :] for r in range(SLOTS)]
        KS = [STACKS[:, SLOTS + r, :] for r in range(SLOTS)]
        WG = [sb(f"WG{r}", [P, KC, F]) for r in range(SLOTS)]
        WU = [sb(f"WU{r}", [P, KC, F]) for r in range(SLOTS)]
        WD = [sb(f"WD{r}", [FE, 2, D]) for r in range(SLOTS)]
        SWGH = sb("SWGH", [P, KC, FS], F32R)
        SWUH = sb("SWUH", [P, KC, FS], F32R)
        SWGL = sb("SWGL", [P, KC, FS], F32R)
        SWUL = sb("SWUL", [P, KC, FS], F32R)
        SWD = sb("SWD", [P, NF, D])
        WIT = sb("WIT", [P, KC, 3 * D + PAD])
        OWT = sb("OWT", [P, KC, D])
        RW = sb("RW", [P, KC, E + 1])
        OBR = sb("OBR", [1, D])
        ONEF = sb("ONEF", [1, P])
        BQK = sb("BQK", [P, 4])
        BQS = sb("BQS", [P, 4])
        BVR = sb("BVR", [1, D + PAD])
        CNT = sb("CNT", [1, B, NQ])
        IDF = sb("IDF", [P, P])
        IDB = sb("IDB", [P, P], BF16)
        MQ = sb("MQ", [P, P], BF16)
        MK = sb("MK", [P, P], BF16)
        LT = sb("LT", [P, P], BF16)
        ONEB = sb("ONEB", [P, P], BF16)
        SL = sb("SL", [H, 1])
        SLR = sb("SLR", [H, 2])
        SLB = sb("SLB", [H, 3], BF16)
        SLP = sb("SLP", [H, 3])
        vsb = VS[0:H, :, :].rearrange("p u n -> p (u n)").bitcast(BF16).rearrange("p (a s) -> p a s", s=S)
        SROW, IROW, ONER = vsb[:, 0:3, :], vsb[:, 3:7, :], vsb[:, 7, :]
        BNS = sb("BNS", [P, NT, 6])
        MV = sb("MV", [P, NT, 2])
        SS = sb("SS", [P, NT])
        ET = sb("ET", [P, 2, BLK])
        SQJ = ET
        NRM = sb("NRM", [P, 6, NT])
        NR2 = sb("NR2", [P, 6, NT])
        V8 = sb("V8", [P, NT, 8])
        I8 = sb("I8", [P, NT, 8], U32)
        LS0 = pbf[:, 7936:8448].rearrange("p (t e) -> p t e", e=E)
        LE = pbf[:, 8448:8960].rearrange("p (t e) -> p t e", e=E)
        W4 = sb("W4", [P, NT, TOPK])
        W4E = sb("W4E", [P, NT, TOPK])
        ZS = sb("ZS", [P, NT])
        ZR = sb("ZR", [P, NT])
        SGE = sb("SGE", [P, NT])
        SG = sb("SG", [P, NT])
        IO32 = sb("IO32", [P, E])
        IDXF = sb("IDXF", [P, NT, TOPK])
        PK = sb("PK", [P, NT, TOPK])
        BAD = sb("BAD", [P, NT, TOPK])
        DST = sb("DST", [P, NT, TOPK])
        DST2 = sb("DST2", [P, NT, TOPK])
        DI = sb("DI", [P, TOPK, NT], I32)
        TI = sb("TI", [P, E, 4], I32)
        TABS = sb("TABS", [P, E * 4], I32)
        TS = sb("TS", [P, KC, NT])
        XS = sb("XS", [P, KC, B, NQ])
        XS2 = sb("XS2", [P, KC, B, NQ])
        UL = sb("UL", [P, UNITS, 2])
        NEGM = sb("NEGM", [P, 2, NQ])
        LSUM = sb("LSUM", [P, 2, NQ])
        LNS = sb("LNS", [P, NQ])
        LEX = sb("LEX", [P, NQ])
        CC = sb("CC", [P, NQ])
        CR = sb("CR", [P, 2, NQ])
        C3 = sb("C3", [P, NQ, 3], BF16)
        VH = sb("VH", [P, 2, NQ, 2 * DH])
        OEV = sb("OEV", [P, SLOTS, 2, P])
        XE = sb("XE", [P, 2, D])
        XET = sb("XET", [P, KC, P])
        IDX = sb("IDX", [P, SLOTS, 4], I32)
        RT = sb("RT", [P, BLK])
        HE = sb("HE", [FE, 2, CAP])
        HS = sb("HS", [P, NF, BLK])
        YE = sb("YE", [P, 2, D])
        ZROW = HS[0:H, 0:2, :].rearrange("p a n -> p (a n)").bitcast(BF16)
        hsf = HS[:, :, :].rearrange("p a n -> p (a n)")
        WN = hsf[:, 512:512 + D]
        LG = hsf[:, 768:768 + NT * (E + 1)].rearrange("p (t e) -> p t e", e=E + 1)
        MB = XET[:, :, :].rearrange("p c n -> p (c n)").bitcast(BF16).rearrange("p (t e) -> p t e", e=E)
        MC = RT[:, :].bitcast(BF16).rearrange("p (t e) -> p t e", e=E)
        RWS = XE[:, 1, :].bitcast(I32).rearrange("p (t k w) -> p t k w", t=NT, k=TOPK)
        XFH = sb("XFH", [P, KC, BLK], F32R)
        XFL = sb("XFL", [P, KC, BLK], F32R)
        SGB = sb("SGB", [P, 2])

        PSB = ctx.enter_context(nc.psum_tensor("PSB", [P, 8, 512], F32))
        psf = PSB[:, :, :].rearrange("p a n -> p (a n)")

        x_loaded = [sem(f"x_loaded{g}") for g in range(4)]
        w_loaded = sem("w_loaded")
        rw_loaded = sem("rw_loaded")
        row_loaded = sem("row_loaded")
        sw_loaded = sem("sw_loaded")
        sw_split = sem("sw_split")
        slope_loaded = sem("slope_loaded")
        const_ready = sem("const_ready")
        mask_ready = sem("mask_ready")
        pool_self = sem("pool_self")
        dve_self = sem("dve_self")
        xn_ready = sem("xn_ready")
        xf_ready = sem("xf_ready")
        stat_ready = sem("stat_ready")
        ss_ready = sem("ss_ready")
        sqrt_ready = sem("sqrt_ready")
        pro_ready = [sem(f"pro_ready{b}") for b in range(8)]
        pro_free = [sem(f"pro_free{b}") for b in range(8)]
        qv_ready = sem("qv_ready")
        rest_ready = sem("rest_ready")
        second_ready = sem("second_ready")
        split_ready = sem("split_ready")
        split_stored = [sem(f"split_stored{r}") for r in range(4)]
        alibi_ready = sem("alibi_ready")
        slope_rows_ready = sem("slope_rows_ready")
        int_rows_ready = sem("int_rows_ready")
        alibi_stored = sem("alibi_stored")
        router_shifted = sem("router_shifted")
        router_exp = sem("router_exp")
        onehot_ready = sem("onehot_ready")
        dest_ready = sem("dest_ready")
        table_tile = sem("table_tile")
        table_cleared = sem("table_cleared")
        token_ids = sem("token_ids")
        scattered = sem("scattered")
        table_loaded = sem("table_loaded")
        xf_stored = sem("xf_stored")
        moe_started = sem("moe_started")
        tsum_ready = sem("tsum_ready")
        held = sem("held")
        stack_loaded = [sem(f"stack_loaded{r}") for r in range(SLOTS)]
        expert_loaded = [sem(f"expert_loaded{r}") for r in range(SLOTS)]
        p1_ready = sem("p1_ready")
        max_ready = sem("max_ready")
        exp1_done = sem("exp1_done")
        p2_ready = sem("p2_ready")
        exp2_done = sem("exp2_done")
        clamp_done = sem("clamp_done")
        pv_done = sem("pv_done")
        v_ready = sem("v_ready")
        o_evacuated = sem("o_evacuated")
        o_stored = [sem(f"o_stored{r}") for r in range(SLOTS)]
        seed_ready = sem("seed_ready")
        seed_exp = sem("seed_exp")
        c_chain = sem("c_chain")
        c_parts_ready = sem("c_parts_ready")
        c_rows_ready = sem("c_rows_ready")
        aux_ready = [sem(f"aux_ready{b}") for b in range(2)]
        shared_out = sem("shared_out")
        tanh_ready = sem("tanh_ready")
        silu_chain = sem("silu_chain")
        silu_done = sem("silu_done")
        block_ready = sem("block_ready")
        scale_ready = sem("scale_ready")
        idx_ready = sem("idx_ready")
        xe_loaded = [sem(f"xe_loaded{r}") for r in range(2)]
        xet_ready = sem("xet_ready")
        ye_ready = sem("ye_ready")
        moe_added = sem("moe_added")
        ye_free = sem("ye_free")
        att_loaded = [sem(f"att_loaded{b}") for b in range(B)]
        x_again = sem("x_again")
        moe_loaded = [sem(f"moe_loaded{g}") for g in range(NT // 2)]
        fin_gate = sem("fin_gate")
        fin_product = sem("fin_product")
        fin_mm = sem("fin_mm")
        fin_z = sem("fin_z")
        fin_e = sem("fin_e")
        fin_out = sem("fin_out")
        stored = sem("stored")

        def bank(n):
            return PSB[:, n % 8, :]

        class Link:

            def __init__(self, eng, semaphore):
                self.eng, self.semaphore, self.n = eng, semaphore, 0

            def __call__(self, ins):
                self.n += 1
                ins.then_inc(self.semaphore, 1)
                self.eng.wait_ge(self.semaphore, self.n)

        def values_of(g):
            b, t = 2 * g // NQ, 2 * g % NQ
            return VS[:, b * H:(b + 1) * H, DH * t:DH * (t + 2)].rearrange("p h (a d) -> p a h d", a=2)

        def products_of(n):
            return bank(n).rearrange("p (a h d) -> p a h d", a=2, d=DH)

        def hold(eng, semaphore, count):
            eng.wait_ge(semaphore, count)
            eng.sem_inc(held, 1)

        def unit(it, k, per=1, add=0):
            return it * (SLOTS * per) + (per * k + add)

        def turn(it, k, n, per=1, add=0):
            return it * (SLOTS // n * per) + (per * (k // n) + add)

        def aux(it, k, a):
            n = 1 + AUX_TASKS * k + a
            return n % 2, it * (SLOTS * AUX_TASKS // 2) + n // 2

        def aux_index(task, last):
            return task - (task > C) if last else task

        def silu_index(k, task):
            return 10 * (k // SLOTS) + 3 * (k % SLOTS) + (0 if k % SLOTS == 3 else {SA: 0, GU: 1, SB: 2}[task])

        def silu(it, k, task):
            return it * 10 + silu_index(k, task)

        def aux_done(it, k, task):
            if task == C:
                return c_rows_ready, unit(it, k, 1, 2)
            if task == TR:
                return xet_ready, unit(it, k, 1, 1)
            if task == DN:
                return ye_ready, unit(it, k, 1, 1)
            if task != GU and k % SLOTS == 3:
                return shared_out, turn(it, k, SLOTS, 2, 1 if task == SA else 2)
            return silu_done, silu(it, k, task) + 1

        def phases(eng, phase):
            phase(0, 0, True, True)
            phase(0, 1, False, True)
            with eng.Fori(0, UNITS // SLOTS - 1) as it:
                for k in range(2, SLOTS + 2):
                    phase(it, k, False, True)
            phase(UNITS // SLOTS - 1, 2, False, False)
            phase(UNITS // SLOTS - 1, 3, False, False)

        def is_last(it, k):
            return isinstance(it, int) and unit(it, k) == UNITS - 1

        block = ctx.enter_context(nc.Block())

        @block.sync
        def _(sp):
            x_t = x.rearrange("b (t p) d -> p (b t) d", p=P)
            for g in range(4):
                sp.dma_start(XN[:, 4 * g:4 * g + 4, :], x_t[:, 4 * g:4 * g + 4, :]).then_inc(x_loaded[g], 16)
            sp.dma_start(INW, in_proj.rearrange("(a p) d -> p a d", p=P)).then_inc(w_loaded, 16)
            sp.dma_start(OW, out_w.rearrange("(a p) d -> p a d", p=P)).then_inc(w_loaded, 16)
            sp.dma_start(SL[:, :], slopes.rearrange("(h a) -> h a", a=1)).then_inc(slope_loaded, 16)
            sp.dma_start(RW[:, :, 0:E], w_router.rearrange("(a p) e -> p a e", p=P)).then_inc(rw_loaded, 16)
            sp.dma_start(RW[:, :, E:E + 1], w_sg.rearrange("(a p) e -> p a e", p=P),
                         allow_slow_non_contiguous=True).then_inc(rw_loaded, 16)
            for tile, row in ((WN, w_norm),):
                sp.dma_start(tile[:, :], row.partition_broadcast(P)).then_inc(row_loaded, 16)
            sp.dma_start(OBR[:, :], out_b.rearrange("(a d) -> a d", a=1)).then_inc(row_loaded, 16)
            sp.dma_start(BVR[:, 0:D], in_b[2 * D:3 * D].rearrange("(a d) -> a d", a=1)).then_inc(row_loaded, 16)
            sp.dma_start(BQK[:, :], in_b[0:2 * D].rearrange("(m p) -> p m", p=P),
                         allow_slow_non_contiguous=True).then_inc(row_loaded, 16)
            for w, places in ((sw_gate, WG), (sw_up, WU)):
                for r in range(SLOTS):
                    a, f0 = r // 2, r % 2 * (FS // 2)
                    sp.dma_start(places[r][:, :, :].rearrange("p a f -> p (a f)"),
                                 w[a * P:(a + 1) * P, f0:f0 + FS // 2]).then_inc(sw_loaded, 16)
            sp.dma_start(SWD[:, 0:NF - 1, :], sw_down[0:P * (NF - 1), :].rearrange("(a p) d -> p a d", p=P))\
                .then_inc(sw_loaded, 16)
            sp.dma_start(SWD[0:FSZ[-1], NF - 1, :], sw_down[P * (NF - 1):FS, :]).then_inc(sw_loaded, 16)
            sp.wait_ge(table_tile, 1)
            sp.dma_start(slot_table.rearrange("(c e) w -> c (e w)", e=E), TI[:, :, :].rearrange("p e w -> p (e w)"))\
                .then_inc(table_cleared, 16)
            sp.wait_ge(slope_rows_ready, 1)
            sp.wait_ge(int_rows_ready, 6)
            for b in range(B):
                qa = q_alibi[b * H:(b + 1) * H, 3:15].rearrange("h (p r) s -> h p r s", r=4)
                ka = k_alibi[b * H:(b + 1) * H, 3:15].rearrange("h (p r) s -> h p r s", r=4)
                for dst, r, src in ((qa, 0, None), (qa, 2, None), (ka, 1, None), (ka, 3, None),
                                    (ka, 0, 0), (ka, 2, 1), (qa, 1, 2), (qa, 3, 3)):
                    source = SROW if src is None else \
                        IROW[:, src:src + 1, :].broadcast_to([H, 3, S])
                    sp.dma_start(dst[:, :, r, :], source).then_inc(alibi_stored, 16)
                sp.dma_start(k_alibi[b * H:(b + 1) * H, 0:3], ONER.unsqueeze(1).broadcast_to([H, 3, S]))\
                    .then_inc(alibi_stored, 16)
                sp.dma_start(q_alibi[b * H:(b + 1) * H, 0:3], ZROW.unsqueeze(1).broadcast_to([H, 3, S]))\
                    .then_inc(alibi_stored, 16)
            sp.wait_ge(xn_ready, NT)
            sp.dma_start(moe_rows[0:T].rearrange("(t p) d -> p t d", p=P), XN[:, :, :]).then_inc(moe_started, 16)
            sp.dma_start(moe_rows[T:T + CAP], XN[:, 0, :]).then_inc(moe_started, 16)
            sp.wait_ge(xf_ready, NT)
            sp.dma_start(xf_rows.rearrange("(t p) d -> p t d", p=P), XF).then_inc(xf_stored, 16)
            def store_parts(n):
                b, tg, m = n // 8, n // 4 % 2, n % 4
                parts = (q_parts if m < 2 else k_parts)
                r0 = b * D + m % 2 * P
                sp.wait_ge(split_ready, n + 1)
                sp.dma_start(parts[:, r0:r0 + P, tg * 512:(tg + 1) * 512].rearrange("a p t -> p a t"), SPL[n % RING])\
                    .then_inc(split_stored[n % RING], 16)

            for n in range(8):
                store_parts(n)
            sp.wait_ge(alibi_stored, 16 * 10 * B)
            sp.wait_ge(xf_stored, 16)
            for n in range(XF0, XF0 + 8):
                sp.wait_ge(pro_free[n % 8], n // 8 + 1)

            def load_operand(t, rows, plan, alibi, u_head, u, semaphore):
                one = rows[:, bass.ds(u_head, DH), :]
                for r, part in enumerate(plan):
                    sp.dma_start(t[r * DH:(r + 1) * DH, :], one[part]).then_inc(semaphore, 16)
                sp.dma_start(t[SHIFT:ROWS, :], alibi[bass.ds(u, 1)].rearrange("a r s -> (a r) s"))\
                    .then_inc(semaphore, 16)

            def load_queries(u_head, u, slot):
                load_operand(QS[slot], q_parts, (0, 1, 2, 0, 1, 0), q_alibi, u_head, u, stack_loaded[slot])

            def load_keys(u_head, u, slot):
                load_operand(KS[slot], k_parts, (0, 0, 0, 1, 1, 2), k_alibi, u_head, u, stack_loaded[slot])

            def load_stack(u_head, u, slot):
                load_queries(u_head, u, slot)
                load_keys(u_head, u, slot)

            def load_expert(u, slot):
                sp.dma_start(WG[slot][:, :, :], w_gate[bass.ds(u, 1)].rearrange("o (a p) f -> p (o a) f", p=P))\
                    .then_inc(expert_loaded[slot], 16)
                sp.dma_start(WU[slot][:, :, :], w_up[bass.ds(u, 1)].rearrange("o (a p) f -> p (o a) f", p=P))\
                    .then_inc(expert_loaded[slot], 16)
                sp.dma_start(WD[slot][:, :, :], w_down[bass.ds(u, 1)].rearrange("o (a p) d -> p (o a) d", p=FE))\
                    .then_inc(expert_loaded[slot], 16)

            for r in range(RING):
                sp.wait_ge(split_stored[r], 16 * len(range(r, 8, RING)))
            store_parts(8)
            load_queries(0, 0, 0)
            store_parts(9)
            load_keys(0, 0, 0)
            store_parts(10)
            load_queries(DH, 1, 1)
            store_parts(11)
            load_keys(DH, 1, 1)
            for n in range(12, 16):
                store_parts(n)
            for u in (2, 3):
                load_stack(u * DH, u, u)
            sp.wait_ge(sw_split, 2 * SLOTS)
            for u in range(4):
                load_expert(u, u)
            for r in range(RING):
                sp.wait_ge(split_stored[r], 16 * len(range(r, 16, RING)))

            def phase(it, k):
                hold(sp, p2_ready, unit(it, k, NQ))
                bank_, before = aux(it, k - 1, DN)
                hold(sp, aux_ready[bank_], before + 1)
                load_stack(unit(it, k, DH, 3 * DH), unit(it, k, 1, 3), (k + 3) % SLOTS)
                load_expert(unit(it, k, 1, 3), (k + 3) % SLOTS)
                store_heads(it, k - 1)

            def store_heads(it, k):
                hold(sp, o_evacuated, unit(it, k, 1, 1))
                rows = att_rows[bass.ds(unit(it, k, DH), DH), :].rearrange("d (t q) -> d t q", q=P)
                for c in range(4):
                    sp.dma_start(rows[:, c:NQ - c:NQ - 1 - 2 * c, :], OEV[32 * c:32 * c + DH, k % SLOTS, :, :])\
                        .then_inc(o_stored[k % SLOTS], 16)

            for r in range(SLOTS):
                sp.sem_inc(o_stored[r], 64)
            with sp.Fori(0, UNITS // SLOTS - 1) as it:
                for k in range(1, SLOTS + 1):
                    phase(it, k)
            def load_attended(b):
                rows = att_rows[b * D:(b + 1) * D].rearrange("(a p) t -> p a t", p=P)
                sp.dma_start(ATTS[:, :, b, :], rows).then_inc(att_loaded[b], 16)

            store_heads(UNITS // SLOTS - 1, 0)
            store_heads(UNITS // SLOTS - 1, 1)
            for r in range(SLOTS):
                sp.wait_ge(o_stored[r], 64 * (H // SLOTS + 1))
            sp.wait_ge(p2_ready, (UNITS - 2) * NQ)
            sp.wait_ge(xe_loaded[(UNITS - 1) % 2], 16 * (UNITS // 2))
            load_attended(0)
            sp.wait_ge(v_ready, UNITS)
            sp.dma_start(X, x_t).then_inc(x_again, 16)
            store_heads(UNITS // SLOTS - 1, 2)
            store_heads(UNITS // SLOTS - 1, 3)
            for r in range(SLOTS):
                sp.wait_ge(o_stored[r], 64 * (UNITS // SLOTS + 1))
            load_attended(1)
            sp.wait_ge(moe_added, 16 * UNITS)
            moe_t = moe_rows[0:T].rearrange("(t p) d -> p t d", p=P)
            for g in range(NT // 2):
                sp.dma_start(XN[:, 2 * g:2 * g + 2, :], moe_t[:, 2 * g:2 * g + 2, :]).then_inc(moe_loaded[g], 16)
            out_t = out.rearrange("b (t p) d -> p (b t) d", p=P)
            for g in range(NT // 2):
                sp.wait_ge(fin_out, g + 1)
                sp.dma_start(out_t[:, 2 * g:2 * g + 2, :], X[:, 2 * g:2 * g + 2, :]).then_inc(stored, 16)
            sp.wait_ge(stored, 16 * (NT // 2))

        @block.tensor
        def _(pe):
            def begin(n):
                if n >= 8:
                    pe.wait_ge(pro_free[n % 8], n // 8)
                return bank(n)

            pe.wait_ge(w_loaded, 32)
            pe.wait_ge(mask_ready, 5)
            for m in range(4):
                o = begin(W0 + m)
                for a in range(2):
                    for c in range(KC):
                        src = INW[:, 2 * m + a, c * P:(c + 1) * P] if m < 3 else OW[:, a, c * P:(c + 1) * P]
                        ins = pe.transpose(o[:, (2 * a + c) * P:(2 * a + c + 1) * P], src, IDF[:, :])
                ins.then_inc(pro_ready[(W0 + m) % 8], 1)
            def transpose_rows(base, src_t, ready):
                for g in range(8):
                    o = begin(base + g)
                    pe.wait_ge(ready, 2 * g + 2)
                    for a in range(2):
                        for c in range(KC):
                            ins = pe.transpose(o[:, (2 * a + c) * P:(2 * a + c + 1) * P],
                                               src_t[:, 2 * g + a, c * P:(c + 1) * P], IDF[:, :])
                    ins.then_inc(pro_ready[(base + g) % 8], 1)

            transpose_rows(XF0, XF, xf_ready)
            pe.wait_ge(rw_loaded, 32)
            for g in range(2):
                o = begin(R0 + g)
                for q in range(4):
                    n = XF0 + 4 * g + q
                    pe.wait_ge(pro_free[n % 8], n // 8 + 1)
                for a in range(8):
                    t = 8 * g + a
                    for c in range(KC):
                        ins = pe.matmul(o[:, 64 * a:64 * a + E + 1], XFT[:, c, t * P:(t + 1) * P], RW[:, c, :],
                                        start=(c == 0), stop=(c == KC - 1))
                ins.then_inc(pro_ready[(R0 + g) % 8], 1)
            transpose_rows(XN0, XN, xn_ready)
            for n in (*range(W0, W0 + 4), *range(XN0, XN0 + 8)):
                pe.wait_ge(pro_free[n % 8], n // 8 + 1)

            def count_choices():
                o = begin(POS0)
                pe.wait_ge(onehot_ready, 1)
                pe.matmul(o, LT[:, :], MB[:, :, :].rearrange("p t e -> p (t e)"), start=True, stop=False)
                pe.matmul(o, ONEB[:, :], MC[:, :, :].rearrange("p t e -> p (t e)"), start=False, stop=True)\
                    .then_inc(pro_ready[POS0 % 8], 1)

            def qk(b):
                for j in range(8):
                    n = qk_task(b, j)
                    tg, m = 2 * b + j // 4, j % 4
                    if n == POS0 + 1:
                        count_choices()
                    o = begin(n)
                    for c in range(KC):
                        ins = pe.matmul(o, WIT[:, c, m * P:(m + 1) * P], XNT[:, c, tg * 512:(tg + 1) * 512],
                                        start=(c == 0), stop=(c == KC - 1))
                    ins.then_inc(pro_ready[n % 8], 1)

            qk(0)
            qk(1)
            pe.wait_ge(row_loaded, 64)
            for g in range(8):
                o = begin(V0 + g)
                for a in range(2):
                    t = 2 * g + a
                    for c in range(KC):
                        ins = pe.matmul(o[:, a * D:(a + 1) * D], XNT[:, c, t * P:(t + 1) * P],
                                        WIT[:, c, 2 * D:3 * D], start=(c == 0), stop=False)
                    ins = pe.matmul(o[:, a * D:(a + 1) * D], ONEF[:, :], BVR[:, 0:D], start=False, stop=True)
                ins.then_inc(pro_ready[(V0 + g) % 8], 1)
            o = begin(U0)
            pe.wait_ge(tsum_ready, 1)
            pe.wait_ge(row_loaded, 64)
            pe.wait_ge(const_ready, 3)
            pe.wait_ge(int_rows_ready, 6)
            for h in range(H):
                for c in range(4):
                    oo = o[32 * c:32 * c + 32, 4 * h:4 * h + 4]
                    v0 = 2 * D + DH * h
                    for a in range(KC):
                        pe.matmul(oo, WIT[:, a, v0:v0 + 2 * DH], XS2[:, a, :, c:NQ - c:NQ - 1 - 2 * c],
                                  start=(a == 0), stop=False)
                    ins = pe.matmul(oo, BVR[:, DH * h:DH * h + 2 * DH], CNT[:, :, c:NQ - c:NQ - 1 - 2 * c],
                                    start=False, stop=True)
            ins.then_inc(pro_ready[U0 % 8], 1)
            for b in range(8):
                pe.wait_ge(pro_free[b], PRO_TASKS // 8)

            def pass1(it, k, s):
                i = step_tile(s)
                slot = k % SLOTS
                base = P1_BANK[s] * 512
                if s == 0:
                    pe.wait_ge(stack_loaded[slot], turn(it, k, SLOTS, 14 * 16, 14 * 16))
                used = {0: -1, 1: 0, 2: 1, 3: 2, 4: 3, 5: 3, 6: 5, 7: 4}[s]
                if k > 0 or used > 0:
                    pe.wait_ge(exp1_done, unit(it, k, NQ, used))
                if k >= 2 and s == 1:
                    pe.wait_ge(exp2_done, unit(it, k, NQ, -2 * NQ))
                w = P * (i + 1)
                q = QS[slot][0:ROWS, i * P:(i + 1) * P]
                for c0 in range(0, w, 512):
                    c1 = min(c0 + 512, w)
                    pe.matmul(psf[:, base + c0:base + c1], q, KS[slot][0:ROWS, c0:c1],
                              start=True, stop=(c1 < w), skip_group_check=True)
                pe.matmul(psf[:, base + i * P:base + w], IDB[:, :], MQ[:, :],
                          start=False, stop=True, skip_group_check=True).then_inc(p1_ready, 1)

            def pass2(it, k, s, ahead):
                j = step_tile(s)
                slot = k % SLOTS
                base = (P2_BANK if ahead else P2_LATE)[s] * 512
                if s == 0:
                    pe.wait_ge(c_rows_ready, unit(it, k, 1, 1))
                if s == 4 and ahead:
                    pe.wait_ge(exp1_done, unit(it, k, NQ, AHEAD + 4))
                if ahead or (s == 0 and not is_last(it, k)):
                    pe.wait_ge(exp2_done, unit(it, k, NQ, s))
                else:
                    pe.wait_ge(exp1_done, UNITS * NQ)
                    pe.wait_ge(exp2_done, unit(it, k, NQ, s - 1))
                w = P * (NQ - j)
                key = KS[slot][0:ROWS, j * P:(j + 1) * P]
                for c0 in range(0, w, 512):
                    c1 = min(c0 + 512, w)
                    pe.matmul(psf[:, base + c0:base + c1], key, QS[slot][0:ROWS, j * P + c0:j * P + c1],
                              start=True, stop=(c0 > 0), skip_group_check=True)
                pe.matmul(psf[:, base:base + P], IDB[:, :], MK[:, :],
                          start=False, stop=True, skip_group_check=True).then_inc(p2_ready, 1)

            def values(it, k, s):
                j = step_tile(s)
                par = k % 2
                if s == 0:
                    pe.wait_ge(o_evacuated, unit(it, k))
                    pe.wait_ge(v_ready, unit(it, k, 1, 1))
                pe.wait_ge(clamp_done, unit(it, k, NQ, s + 1))
                probs = PB[:, par, prob_offset(s):prob_offset(s) + (s + 1) * P].rearrange("p (t q) -> p t q", q=P)
                for c in (3, 2, 1, 0):
                    far = NQ - 1 - c
                    if far < j:
                        continue
                    o = PSB[32 * c:32 * c + 32, O_BANK, 0:2 * P].rearrange("p (t q) -> p t q", q=P)
                    v = VH[:, par, j, :]
                    if c >= j:
                        ins = pe.matmul(o, v, probs[:, c - j:far - j + 1:far - c, :],
                                        start=False, stop=(j == 0), skip_group_check=True)
                    else:
                        ins = pe.matmul(o[:, 1, :], v, probs[:, far - j, :],
                                        start=(far == j), stop=False, skip_group_check=True)
                ins.then_inc(pv_done, 1)

            def aux_begin(it, k, task, last=False):
                order = [t for t in range(AUX_TASKS) if not (last and t == C)]
                a = order.index(task)
                if a >= 2:
                    pe.wait_ge(*aux_done(it, k, order[a - 2]))
                elif k >= 1:
                    pe.wait_ge(*aux_done(it, k - 1, C if a == 0 else DN))
                elif a == 1:
                    pe.wait_ge(c_rows_ready, 1)
                b, _ = aux(it, k, a)
                return PSB[:, AUX + b, :], aux_ready[b]

            def c_transpose(o, ready, parts_count):
                pe.wait_ge(c_parts_ready, parts_count)
                for i in range(NQ):
                    ins = pe.transpose(o[SHIFT:SHIFT + 3, i * P // 2:(i + 1) * P // 2].bitcast(BF16),
                                       C3[:, i, :], IDB[:, :])
                ins.then_inc(ready, 1)

            def expert_transpose(it, k, o, ready):
                pe.wait_ge(xe_loaded[k % 2], turn(it, k, 2, 16, 16))
                for c in range(KC):
                    ins = pe.transpose(o[:, c * P:(c + 1) * P], XE[:, k % 2, c * P:(c + 1) * P], IDF[:, :])
                ins.then_inc(ready, 1)

            def expert_up(it, k, part, last):
                slot = k % SLOTS
                b, _ = aux(it, k, aux_index(GU, last))
                o, ready = PSB[:, AUX + b, :], aux_ready[b]
                if part == 0:
                    aux_begin(it, k, GU, last)
                    pe.wait_ge(expert_loaded[slot], turn(it, k, SLOTS, 48, 48))
                    pe.wait_ge(xet_ready, unit(it, k, 1, 1))
                w = WU[slot] if part else WG[slot]
                for f in range(2):
                    for c in range(KC):
                        ins = pe.matmul(o[0:FE, (2 * part + f) * P:(2 * part + f + 1) * P],
                                        w[:, c, f * FE:(f + 1) * FE], XET[:, c, :],
                                        start=(c == 0), stop=(c == KC - 1))
                if part:
                    ins.then_inc(ready, 1)

            def expert_down(it, k, o, ready):
                slot = k % SLOTS
                pe.wait_ge(silu_done, silu(it, k, GU) + 1)
                for f in range(2):
                    ins = pe.matmul(o[:, 0:D], HE[:, f, :], WD[slot][:, f, :], start=(f == 0), stop=(f == 1))
                ins.then_inc(ready, 1)

            def shared(it, k, task, part, last):
                slot, which = k % SLOTS, 0 if task == SA else 1
                b, _ = aux(it, k, aux_index(task, last))
                o, ready = PSB[:, AUX + b, :], aux_ready[b]
                if part == 0:
                    aux_begin(it, k, task, last)
                if slot < 3:
                    ch = 2 * slot + which
                    m = FSZ[ch]
                    if ch == 0 and part == 0:
                        pe.wait_ge(block_ready, turn(it, k, SLOTS, 2, 2))
                    high, left = (SWUH, SWUL) if part else (SWGH, SWGL)
                    for c in range(KC):
                        for w, v in ((high, XFH), (high, XFL), (left, XFH)):
                            ins = pe.matmul(o[0:m, part * BLK:(part + 1) * BLK], w[:, c, ch * P:ch * P + m],
                                            v[:, c, :], start=(c == 0 and v is XFH and w is high),
                                            stop=(c == KC - 1 and w is left))
                else:
                    if which == 0 and part == 0:
                        pe.wait_ge(silu_done, silu(it, k, GU))
                    for ch in range(3 * part, 3 * part + 3):
                        m = FSZ[ch]
                        ins = pe.matmul(o[:, 0:D], HS[0:m, ch, which * P:(which + 1) * P], SWD[0:m, ch, :],
                                        start=(ch == 0), stop=(ch == NF - 1))
                if part:
                    ins.then_inc(ready, 1)

            for u in range(2):
                for s in range(NQ):
                    pass1(0, u, s)
            c_transpose(PSB[:, AUX, :], aux_ready[0], 1)
            pe.wait_ge(sw_loaded, 16 * 10)
            pe.wait_ge(sw_split, 2 * SLOTS)

            def phase(it, k, first, ahead):
                last = is_last(it, k)
                for s in range(NQ):
                    if ahead:
                        pass1(it, k + 2, s)
                    if s == 0 and not first:
                        shared(it, k - 1, SB, 1, False)
                    pass2(it, k, s, ahead)
                    if s >= 3:
                        values(it, k, s - 3)
                    elif not first:
                        values(it, k - 1, s + 5)
                    if s == 1:
                        if not first:
                            expert_down(it, k - 1, *aux_begin(it, k - 1, DN))
                        expert_transpose(it, k, *aux_begin(it, k, TR))
                    if s == 7 and not last:
                        c_transpose(*aux_begin(it, k, C), unit(it, k, 1, 2))
                    if s in (2, 3):
                        shared(it, k, SA, s - 2, last)
                    if s in (4, 5):
                        expert_up(it, k, s - 4, last)
                    if s == 6:
                        shared(it, k, SB, 0, last)

            phases(pe, phase)
            shared(UNITS // SLOTS - 1, SLOTS - 1, SB, 1, True)
            values(UNITS // SLOTS - 1, SLOTS - 1, 5)
            values(UNITS // SLOTS - 1, SLOTS - 1, 6)
            values(UNITS // SLOTS - 1, SLOTS - 1, 7)
            expert_down(UNITS // SLOTS - 1, SLOTS - 1, *aux_begin(UNITS // SLOTS - 1, SLOTS - 1, DN, True))
            pe.wait_ge(o_evacuated, UNITS)
            pe.wait_ge(exp2_done, UNITS * NQ)
            for g in range(NT // 2):
                pe.wait_ge(att_loaded[2 * g // NQ], 16)
                if g == AUX:
                    pe.wait_ge(ye_ready, UNITS)
                    pe.wait_ge(shared_out, 2 * (UNITS // SLOTS))
                for a in range(2):
                    t = 2 * g + a
                    b, tb = t // NQ, t % NQ
                    for c in range(KC):
                        ins = pe.matmul(PSB[:, g, a * D:(a + 1) * D], ATTS[:, c, b, tb * P:(tb + 1) * P],
                                        OWT[:, c, :], start=(c == 0), stop=False)
                    ins = pe.matmul(PSB[:, g, a * D:(a + 1) * D], ONEF[:, :], OBR[:, :], start=False, stop=True)
                ins.then_inc(fin_mm, 1)

        @block.scalar
        def _(act):
            def task(n):
                act.wait_ge(pro_ready[n % 8], n // 8 + 1)
                return bank(n)

            def evacuate(n, dst, src):
                act.activation(dst, src, ACT.Copy).then_inc(pro_free[n % 8], 1)

            act.wait_ge(stat_ready, 1)
            act.activation(NRM[:, 1, :], NRM[:, 0, :], ACT.Sqrt).then_inc(sqrt_ready, 1)
            for m in range(3):
                n = W0 + m
                evacuate(n, WIT[:, :, 2 * m * P:(2 * m + 2) * P].rearrange("p c (a m) -> p a c m", a=2),
                         task(n).rearrange("p (a c m) -> p a c m", a=2, c=KC))
            evacuate(W0 + 3, OWT[:, :, :].rearrange("p c (a m) -> p a c m", a=2),
                     task(W0 + 3).rearrange("p (a c m) -> p a c m", a=2, c=KC))
            for t in range(NT):
                act.wait_ge(xn_ready, t + 1)
                if t >= 2:
                    act.wait_ge(ss_ready, t - 1)
                act.activation(SQJ[:, t % 2, :], XN[:, t, :], ACT.Square, accum_out=SS[:, t:t + 1])\
                    .then_inc(ss_ready, 1)
            act.wait_ge(stat_ready, 2)
            act.activation(NR2[:, 1, :], NR2[:, 0, :], ACT.Sqrt).then_inc(sqrt_ready, 1)
            act.preload_act_table_set("exp_and_others")
            def evacuate_rows(base, dst):
                for g in range(8):
                    n = base + g
                    evacuate(n, dst[:, :, 2 * g * P:(2 * g + 2) * P].rearrange("p c (a m) -> p a c m", a=2),
                             task(n).rearrange("p (a c m) -> p a c m", a=2, c=KC))

            evacuate_rows(XF0, XFT)
            for g in range(2):
                n = R0 + g
                evacuate(n, LG[:, 8 * g:8 * g + 8, :],
                         task(n).rearrange("p (t e) -> p t e", e=64)[:, :, 0:E + 1])
            evacuate_rows(XN0, XNT)

            def router_exponentials():
                act.wait_ge(router_shifted, 2)
                act.activation(LE[:, :, :], LS0[:, :, :], ACT.Exp).then_inc(router_exp, 1)
                act.activation(W4E[:, :, :], W4[:, :, :], ACT.Exp).then_inc(router_exp, 1)
                act.activation(SGE[:, :], LG[:, :, E], ACT.Tanh, scale=0.5).then_inc(router_exp, 1)

            def second_part(i):
                act.wait_ge(rest_ready, i + 1)
                act.activation(SPL[i % RING][:, 1, :], QV[i % RING], ACT.Copy).then_inc(second_ready, 1)

            def qk(b):
                for j in range(8):
                    n, i, m = qk_task(b, j), 8 * b + j, j % 4
                    scale = SCALE if m < 2 else 1.0
                    o = task(n)
                    if i == RING - 1:
                        act.wait_ge(dest_ready, 1)
                    if i >= RING:
                        act.wait_ge(split_ready, i - RING + 1)
                        act.wait_ge(split_stored[i % RING], 16 * (i // RING))
                    act.activation(QV[i % RING], o, ACT.Identity, bias=BQS[:, m:m + 1], scale=scale).then_inc(qv_ready, 1)
                    act.activation(SPL[i % RING][:, 0, :], o, ACT.Identity, bias=BQS[:, m:m + 1], scale=scale)\
                        .then_inc(pro_free[n % 8], 1)
                    if i == 1:
                        router_exponentials()
                    if i >= 1:
                        second_part(i - 1)

            qk(0)
            qk(1)
            second_part(15)
            act.wait_ge(alibi_stored, 16 * 10 * B)
            for g in range(0, 8, 2):
                task(V0 + g)
                evacuate(V0 + g, values_of(g), products_of(V0 + g))
            o = task(U0)
            act.activation(UL[:, :, :].rearrange("p (b h) s -> p h b s", b=B),
                           o[:, 0:4 * H].rearrange("p (h b s) -> p h b s", h=H, b=B), ACT.Copy)\
                .then_inc(pro_free[U0 % 8], 1)

            def exp1(it, k, s):
                i, par = step_tile(s), k % 2
                base = P1_BANK[s] * 512
                sc = psf[:, base:base + (i + 1) * P]
                act.wait_ge(max_ready, unit(it, k, NQ, s + 1))
                if s == 0 and k >= 2:
                    act.wait_ge(c_parts_ready, unit(it, k, 1, -1))
                act.activation(sc, sc, ACT.Exp, bias=NEGM[:, par, i:i + 1],
                               accum_out=LSUM[:, par, i:i + 1]).then_inc(exp1_done, 1)

            def exp2(it, k, s, ahead):
                base = (P2_BANK if ahead else P2_LATE)[s] * 512
                if s == 0 and k >= 1:
                    act.wait_ge(pv_done, unit(it, k, NQ, 1 - NQ))
                act.wait_ge(p2_ready, unit(it, k, NQ, s + 1))
                act.activation(PB[:, k % 2, prob_offset(s):prob_offset(s) + (s + 1) * P],
                               psf[:, base:base + (s + 1) * P], ACT.Exp).then_inc(exp2_done, 1)

            def exp_seed(it, k):
                act.wait_ge(seed_ready, unit(it, k, 1, 1))
                act.activation(LEX[:, :], LNS[:, :], ACT.Exp).then_inc(seed_exp, 1)

            def aux_task(it, k, a):
                b, before = aux(it, k, a)
                act.wait_ge(aux_ready[b], before + 1)
                return PSB[:, AUX + b, :]

            def tanh_gate(it, k, a, task_, rows):
                z = silu_index(k, task_)
                o = aux_task(it, k, a)
                if z >= 2:
                    act.wait_ge(silu_done, silu(it, k, task_) - 1)
                act.activation(ET[0:rows, z % 2, :], o[0:rows, 0:BLK], ACT.Tanh, scale=0.5)\
                    .then_inc(tanh_ready, 1)

            def shared(it, k, a, task_):
                which = 0 if task_ == SA else 1
                slot = k % SLOTS
                if slot < 3:
                    tanh_gate(it, k, a, task_, FSZ[2 * slot + which])
                else:
                    o = aux_task(it, k, a)
                    t = turn(it, k, SLOTS, 2, which)
                    act.wait_ge(scale_ready, turn(it, k, SLOTS, 1, 1))
                    dst = SH[:, t, :] if isinstance(t, int) else SH[:, bass.ds(t, 1), :].rearrange("p o d -> p (o d)")
                    act.activation(dst, o[:, 0:D], ACT.Copy, scale=SGB[:, which:which + 1]).then_inc(shared_out, 1)

            for u in range(2):
                for s in range(NQ):
                    exp1(0, u, s)
                    if u == 1 and s == 1:
                        exp_seed(0, 0)

            def weigh(it, k, last):
                o = aux_task(it, k, aux_index(DN, last))
                act.wait_ge(idx_ready, unit(it, k, 1, 1))
                if k >= 1:
                    act.wait_ge(ye_free, unit(it, k))
                act.activation(YE[:, k % 2, :], o[:, 0:D], ACT.Copy,
                               scale=IDX[:, k % SLOTS, 1:2].bitcast(F32)).then_inc(ye_ready, 1)

            def phase(it, k, first, ahead):
                last = is_last(it, k)
                ix = lambda t: aux_index(t, last)
                for s in range(NQ):
                    if s == 0 and not first:
                        shared(it, k - 1, SB, SB)
                    if s == 2:
                        o = aux_task(it, k, ix(TR))
                        act.activation(XET[:, :, :].rearrange("p c m -> p (c m)"), o[:, 0:D], ACT.Copy)\
                            .then_inc(xet_ready, 1)
                    if s == 4:
                        shared(it, k, ix(SA), SA)
                    if s == 6:
                        tanh_gate(it, k, ix(GU), GU, FE)
                    exp2(it, k, s, ahead)
                    if s == 1:
                        if not first:
                            weigh(it, k - 1, False)
                        if not last:
                            exp_seed(it, k + 1)
                    if ahead:
                        exp1(it, k + 2, s)

            phases(act, phase)
            shared(UNITS // SLOTS - 1, SLOTS - 1, aux_index(SB, True), SB)
            weigh(UNITS // SLOTS - 1, SLOTS - 1, True)
            for g in range(NT // 2):
                act.wait_ge(fin_z, g + 1)
                e = XFT[:, :, :].rearrange("p c n -> p (c n)")[:, 512 * g:512 * (g + 1)]
                act.activation(e, XN[:, 2 * g:2 * g + 2, :].rearrange("p a d -> p (a d)"), ACT.Tanh, scale=0.5).then_inc(fin_e, 1)

        @block.vector
        def _(dve):
            link = Link(dve, dve_self)

            def root(stats, n):
                dve.wait_ge(sqrt_ready, n)
                link(dve.reciprocal(stats[:, 2, :], stats[:, 1, :]))
                link(dve.tensor_tensor(stats[:, 3, :], stats[:, 2, :], stats[:, 2, :], ALU.mult))
                link(dve.tensor_tensor(stats[:, 4, :], stats[:, 3, :], stats[:, 0, :], ALU.mult))
                link(dve.tensor_scalar(stats[:, 3, :], stats[:, 4, :], -0.5, 1.5, ALU.mult, ALU.add))
                link(dve.tensor_tensor(stats[:, 5, :], stats[:, 3, :], stats[:, 2, :], ALU.mult))

            for t in range(NT):
                dve.wait_ge(x_loaded[t // 4], 16)
                ins = dve.bn_stats(BNS[:, t, :], XN[:, t, :])
                if t == NT - 1:
                    link(ins)
                else:
                    ins.then_inc(dve_self, 1)
                    link.n += 1
            for t in range(NT):
                ins = dve.bn_aggr(MV[:, t, :], BNS[:, t, :])
                ins.then_inc(dve_self, 1)
                link.n += 1
            dve.wait_ge(dve_self, link.n)
            dve.tensor_scalar(NRM[:, 0, :], MV[:, :, 1], LN_EPS, None, ALU.add).then_inc(stat_ready, 1)
            dve.wait_ge(slope_loaded, 16)
            dve.wait_ge(alibi_ready, 1)
            link(dve.tensor_copy(SLB[:, 0:1], SL[:, :]))
            link(dve.tensor_tensor(SLR[:, 0:1], SL[:, :], SLB[:, 0:1], ALU.subtract))
            link(dve.tensor_copy(SLB[:, 1:2], SLR[:, 0:1]))
            link(dve.tensor_tensor(SLR[:, 1:2], SLR[:, 0:1], SLB[:, 1:2], ALU.subtract))
            link(dve.tensor_copy(SLB[:, 2:3], SLR[:, 1:2]))
            link(dve.tensor_copy(SLP[:, :], SLB[:, :]))
            for p in range(3):
                ins = dve.tensor_scalar(SROW[:, p, :], ONER, SLP[:, p:p + 1], None, ALU.mult)
                if p < 2:
                    link(ins)
            ins.then_inc(slope_rows_ready, 1)
            root(NRM, 1)
            for t in range(NT):
                dve.tensor_scalar(XN[:, t, :], XN[:, t, :], MV[:, t, 0:1], NRM[:, 5, t:t + 1],
                                  ALU.subtract, ALU.mult).then_inc(xn_ready, 1)
            dve.wait_ge(row_loaded, 64)
            link(dve.tensor_scalar(BQS[:, 0:2], BQK[:, 0:2], SCALE, None, ALU.mult))
            link(dve.tensor_copy(BQS[:, 2:4], BQK[:, 2:4]))
            dve.wait_ge(ss_ready, NT)
            dve.tensor_scalar(NR2[:, 0, :], SS[:, :], 1.0 / D, RMS_EPS, ALU.mult, ALU.add).then_inc(stat_ready, 1)
            dve.wait_ge(stat_ready, 2)
            root(NR2, 2)
            dve.wait_ge(xn_ready, NT)
            for t in range(NT):
                dve.scalar_tensor_tensor(out=XF[:, t, :], in0=XN[:, t, :], scalar=NR2[:, 5, t:t + 1],
                                         in1=WN[:, :], op0=ALU.mult, op1=ALU.mult).then_inc(xf_ready, 1)
            for n in (R0, R0 + 1):
                dve.wait_ge(pro_free[n % 8], n // 8 + 1)
            for t in range(NT):
                dve.max(V8[:, t, :], LG[:, t, 0:E]).then_inc(dve_self, 1)
                link.n += 1
            dve.wait_ge(dve_self, link.n)
            for t in range(NT):
                dve.max_index(I8[:, t, :], V8[:, t, :], LG[:, t, 0:E]).then_inc(dve_self, 1)
                link.n += 1
            dve.wait_ge(dve_self, link.n)
            link(dve.tensor_copy(IDXF[:, :, :], I8[:, :, 0:TOPK]))
            dve.wait_ge(const_ready, 3)
            for n in range(W0, W0 + 4):
                dve.wait_ge(pro_free[n % 8], 1)
            link(dve.tensor_tensor(OH, IO32[:, :].unsqueeze(1).unsqueeze(1).broadcast_to([P, NT, TOPK, E]),
                                   IDXF[:, :, :].unsqueeze(3).broadcast_to([P, NT, TOPK, E]), ALU.is_equal))
            link(dve.tensor_tensor(PROD[:, :, 0:2, :], OH[:, :, 0:2, :], OH[:, :, 2:4, :], ALU.add))
            link(dve.tensor_tensor(MB[:, :, :], PROD[:, :, 0, :], PROD[:, :, 1, :], ALU.add))
            link(dve.memset(MC[:, 0, :], 0.0))
            for t in range(1, NT):
                ins = dve.tensor_tensor(MC[:, t, :], MC[:, t - 1, :], MB[:, t - 1, :], ALU.add)
                if t < NT - 1:
                    link(ins)
            ins.then_inc(onehot_ready, 1)
            dve.tensor_tensor(LS0[:, :, :], LG[:, :, 0:E], V8[:, :, 0:1].broadcast_to([P, NT, E]), ALU.subtract)\
                .then_inc(router_shifted, 1)
            dve.tensor_tensor(W4[:, :, :], V8[:, :, 0:TOPK], V8[:, :, 0:1].broadcast_to([P, NT, TOPK]),
                              ALU.subtract).then_inc(router_shifted, 1)
            for n in range(XN0, XN0 + 8):
                dve.wait_ge(pro_free[n % 8], n // 8 + 1)
            link(dve.tensor_reduce(TS[:, :, :], XNT[:, :, :].rearrange("p c (t q) -> p c t q", q=P), AX_X, ALU.add))

            def third_part(i):
                dve.wait_ge(second_ready, i + 1)
                dve.tensor_tensor(SPL[i % RING][:, 2, :], QV[i % RING], SPL[i % RING][:, 1, :], ALU.subtract)\
                    .then_inc(split_ready, 1)

            def qk_split(b):
                for j in range(8):
                    n, i = qk_task(b, j), 8 * b + j
                    dve.wait_ge(qv_ready, i + 1)
                    dve.wait_ge(pro_free[n % 8], n // 8 + 1)
                    dve.tensor_tensor(QV[i % RING], QV[i % RING], SPL[i % RING][:, 0, :], ALU.subtract).then_inc(rest_ready, 1)
                    if i >= 1:
                        third_part(i - 1)

            dve.wait_ge(router_exp, 3)
            link(dve.tensor_reduce(ZS[:, :], LE[:, :, :], AX_X, ALU.add))
            link(dve.reciprocal(ZR[:, :], ZS[:, :]))
            dve.wait_ge(token_ids, 3)
            link(dve.tensor_tensor(RWS[:, :, :, 1].bitcast(F32), W4E[:, :, :],
                                   ZR[:, :].unsqueeze(2).broadcast_to([P, NT, TOPK]), ALU.mult))
            link(dve.tensor_scalar(SG[:, :], SGE[:, :], 0.5, 0.5, ALU.mult, ALU.add))
            pos = bank(POS0).rearrange("p (t e) -> p t e", e=E)
            dve.wait_ge(pro_ready[POS0 % 8], POS0 // 8 + 1)
            dve.tensor_tensor(PROD, OH, pos.unsqueeze(2).broadcast_to([P, NT, TOPK, E]), ALU.mult)\
                .then_inc(pro_free[POS0 % 8], 1)
            dve.wait_ge(pro_free[POS0 % 8], POS0 // 8 + 1)
            link(dve.tensor_reduce(PK[:, :, :], PROD, AX_X, ALU.add))
            link(dve.tensor_scalar(BAD[:, :, :], PK[:, :, :], float(CAP), float(CAP * E), ALU.is_ge, ALU.mult))
            link(dve.scalar_tensor_tensor(out=DST[:, :, :], in0=PK[:, :, :], scalar=float(E), in1=IDXF[:, :, :],
                                          op0=ALU.mult, op1=ALU.add))
            link(dve.tensor_tensor(DST2[:, :, :], DST[:, :, :], BAD[:, :, :], ALU.add))
            dve.tensor_copy(DI[:, :, :], DST2[:, :, :].rearrange("p t k -> p k t")).then_inc(dest_ready, 1)
            ts = TS[:, :, :].rearrange("p c (b t) -> p c b t", b=B)
            link(dve.memset(XS[:, :, :, NQ - 1], 0.0))
            for t in reversed(range(NQ - 1)):
                link(dve.tensor_tensor(XS[:, :, :, t], XS[:, :, :, t + 1], ts[:, :, :, t + 1], ALU.add))
            dve.tensor_scalar(XS2[:, :, :, :], XS[:, :, :, :], FLOOR, None, ALU.mult).then_inc(tsum_ready, 1)
            qk_split(0)
            qk_split(1)
            third_part(15)
            dve.wait_ge(alibi_stored, 16 * 10 * B)
            for g in range(1, 8, 2):
                n = V0 + g
                dve.wait_ge(pro_ready[n % 8], n // 8 + 1)
                dve.tensor_copy(values_of(g), products_of(n)).then_inc(pro_free[n % 8], 1)

            def row_max(it, k, s):
                i, par = step_tile(s), k % 2
                base = P1_BANK[s] * 512
                dve.wait_ge(p1_ready, unit(it, k, NQ, s + 1))
                if s == 0 and k >= 2:
                    dve.wait_ge(c_parts_ready, unit(it, k, 1, -1))
                dve.tensor_reduce(NEGM[:, par, i:i + 1], psf[:, base:base + (i + 1) * P], AX_X, ALU.max,
                                  negate=True).then_inc(max_ready, 1)

            def clamp(it, k, s):
                dve.wait_ge(exp2_done, unit(it, k, NQ, s + 1))
                p = PB[:, k % 2, prob_offset(s):prob_offset(s) + (s + 1) * P]
                dve.tensor_scalar(p, p, FLOOR, None, ALU.max).then_inc(clamp_done, 1)

            def c_rows(it, k, b, count):
                dve.wait_ge(aux_ready[b], count)
                dve.tensor_copy(QS[k % SLOTS][SHIFT:SHIFT + 3, :], PSB[SHIFT:SHIFT + 3, AUX + b, :].bitcast(BF16))\
                    .then_inc(c_rows_ready, 1)

            def silu_up(it, k, a, task_, dst, rows):
                b, _ = aux(it, k, a)
                z = silu_index(k, task_)
                n = silu(it, k, task_)
                psum = PSB[0:rows, AUX + b, :]
                if not (isinstance(n, int) and n == 0):
                    dve.wait_ge(silu_done, n)
                dve.wait_ge(tanh_ready, n + 1)
                dve.scalar_tensor_tensor(out=RT[0:rows, :], in0=ET[0:rows, z % 2, :], scalar=1.0,
                                         in1=psum[:, 0:BLK], op0=ALU.add, op1=ALU.mult).then_inc(silu_chain, 1)
                dve.wait_ge(silu_chain, n + 1)
                dve.scalar_tensor_tensor(out=dst, in0=RT[0:rows, :], scalar=0.5, in1=psum[:, BLK:2 * BLK],
                                         op0=ALU.mult, op1=ALU.mult).then_inc(silu_done, 1)

            def shared(it, k, a, task_):
                slot = k % SLOTS
                if slot == 3:
                    return
                ch = 2 * slot + (0 if task_ == SA else 1)
                if ch == 0 and k >= SLOTS:
                    b, before = aux(it, k - 1, SB)
                    dve.wait_ge(aux_ready[b], before + 1)
                silu_up(it, k, a, task_, HS[0:FSZ[ch], ch, :], FSZ[ch])

            def evacuate_heads(it, k):
                slot = k % SLOTS
                dve.wait_ge(pv_done, unit(it, k, NQ, NQ))
                dve.wait_ge(o_stored[slot], turn(it, k, SLOTS, 64, 64))
                u = unit(it, k)
                ul = UL[:, u, :] if isinstance(u, int) else UL[:, bass.ds(u, 1), :].rearrange("p o s -> p (o s)")
                dve.tensor_tensor(OEV[:, slot, :, :], PSB[:, O_BANK, 0:2 * P].rearrange("p (t q) -> p t q", q=P),
                                  ul.unsqueeze(2).broadcast_to([P, 2, P]), ALU.add).then_inc(o_evacuated, 1)

            for u in range(2):
                for s in range(NQ):
                    row_max(0, u, s)
            c_rows(0, 0, 0, 1)
            dve.wait_ge(pro_free[U0 % 8], U0 // 8 + 1)

            def phase(it, k, first, ahead):
                last = is_last(it, k)
                ix = lambda t: aux_index(t, last)
                for s in range(NQ):
                    if s > 0:
                        clamp(it, k, s - 1)
                    if ahead:
                        row_max(it, k + 2, s)
                    if s == 0 and not first:
                        shared(it, k - 1, SB, SB)
                        clamp(it, k - 1, NQ - 1)
                    if s == 2 and not first:
                        evacuate_heads(it, k - 1)
                    if s == 4:
                        shared(it, k, ix(SA), SA)
                    if s == 6:
                        if not first:
                            b, before = aux(it, k - 1, DN)
                            dve.wait_ge(aux_ready[b], before + 1)
                        silu_up(it, k, ix(GU), GU, HE[:, :, :].rearrange("p f c -> p (f c)"), FE)
                    if s == 7 and not last:
                        b, before = aux(it, k, C)
                        c_rows(it, k + 1, b, before + 1)

            def gated_output(g):
                c = slice(512 * g, 512 * (g + 1))
                dve.wait_ge(fin_e, g + 1)
                dve.scalar_tensor_tensor(out=zf[:, c], in0=ef[:, c], scalar=1.0, in1=zf[:, c],
                                         op0=ALU.add, op1=ALU.mult).then_inc(fin_gate, 1)
                dve.wait_ge(fin_mm, g + 1)
                dve.wait_ge(fin_gate, g + 1)
                dve.scalar_tensor_tensor(out=ef[:, c], in0=PSB[:, g, :], scalar=0.5, in1=zf[:, c],
                                         op0=ALU.mult, op1=ALU.mult).then_inc(fin_product, 1)

            phases(dve, phase)
            clamp(UNITS // SLOTS - 1, SLOTS - 1, NQ - 1)
            evacuate_heads(UNITS // SLOTS - 1, SLOTS - 1)
            dve.wait_ge(ye_ready, UNITS)
            zf = XN[:, :, :].rearrange("p t d -> p (t d)")
            shf = SH.rearrange("p t d -> p (t d)")
            ef = XFT[:, :, :].rearrange("p c n -> p (c n)")
            for g in range(NT // 2):
                c = slice(512 * g, 512 * (g + 1))
                dve.wait_ge(moe_loaded[g], 16)
                dve.tensor_tensor(zf[:, c], zf[:, c], shf[:, c], ALU.add).then_inc(fin_z, 1)
                if g >= 1:
                    gated_output(g - 1)
            gated_output(NT // 2 - 1)

        @block.gpsimd
        def _(pool):
            link = Link(pool, pool_self)
            link(pool.memset(IDF[:, :], 0.0))
            link(pool.memset(IDB[:, :], 0.0))
            link(pool.memset(MQ[:, :], 0.0))
            link(pool.memset(MK[:, :], 0.0))
            link(pool.memset(ONEB[:, :], 1.0))
            link(pool.memset(LT[:, :], 1.0))
            link(pool.memset(ONEF[:, :], 1.0))
            link(pool.memset(WIT[:, :, 3 * D:3 * D + PAD], 0.0))
            pool.affine_select(out=IDF[:, :], in_=IDF[:, :], compare_op=ALU.not_equal, fill=1.0, base=0,
                               pattern=[[-1, P]], channel_multiplier=1).then_inc(mask_ready, 1)
            pool.affine_select(out=IDB[:, :], in_=IDB[:, :], compare_op=ALU.not_equal, fill=1.0, base=0,
                               pattern=[[-1, P]], channel_multiplier=1).then_inc(mask_ready, 1)
            pool.affine_select(out=MQ[:, :], in_=MQ[:, :], compare_op=ALU.is_ge, fill=MASK, base=0,
                               pattern=[[-1, P]], channel_multiplier=1).then_inc(mask_ready, 1)
            pool.affine_select(out=MK[:, :], in_=MK[:, :], compare_op=ALU.is_ge, fill=MASK, base=0,
                               pattern=[[1, P]], channel_multiplier=-1).then_inc(mask_ready, 1)
            pool.affine_select(out=LT[:, :], in_=LT[:, :], compare_op=ALU.is_gt, fill=0.0, base=0,
                               pattern=[[1, P]], channel_multiplier=-1).then_inc(mask_ready, 1)
            pool.memset(ONER, 1.0).then_inc(alibi_ready, 1)
            for r, pattern in enumerate(([[P, NQ], [0, P]], [[0, NQ], [1, P]], [[-P, NQ], [0, P]],
                                         [[0, NQ], [-1, P]])):
                pool.iota(IROW[:, r, :].rearrange("p (t q) -> p t q", q=P), pattern, base=0, channel_multiplier=0,
                          allow_small_or_imprecise_dtypes=True).then_inc(int_rows_ready, 1)
            pool.memset(ZROW, 0.0).then_inc(int_rows_ready, 1)
            pool.memset(BVR[:, D:D + PAD], 0.0).then_inc(int_rows_ready, 1)
            pool.iota(IO32[:, :], [[1, E]], base=0, channel_multiplier=0,
                      allow_small_or_imprecise_dtypes=True).then_inc(const_ready, 1)
            link(pool.iota(CNT[:, :, :], [[0, B], [-P, NQ]], base=P * (NQ - 1), channel_multiplier=0,
                           allow_small_or_imprecise_dtypes=True))
            pool.tensor_scalar(CNT[:, :, :], CNT[:, :, :], FLOOR, None, ALU.mult).then_inc(const_ready, 1)
            pool.memset(VH[:, :, :, :], 0.0).then_inc(const_ready, 1)
            link(pool.memset(TI[:, :, :], 0))
            pool.iota(TI[:, :, 2], [[0, E]], base=T, channel_multiplier=1).then_inc(table_tile, 1)
            link(pool.memset(RWS[:, :, :, 3], 0))
            pool.iota(RWS[:, :, :, 0], [[P, NT], [0, TOPK]], base=0, channel_multiplier=1).then_inc(token_ids, 1)
            pool.iota(RWS[:, :, :, 2], [[P, NT], [0, TOPK]], base=0, channel_multiplier=1).then_inc(token_ids, 1)
            pool.memset(RWS[:, :, :, 1], 0).then_inc(token_ids, 1)

            def chain(it, k):
                par = k % 2
                n = unit(it, k)
                lsum, cc = LSUM[:, par, :], CC[:, :]
                t, a = CR[:, 0, :], CR[:, 1, :]
                hold(pool, exp1_done, unit(it, k, NQ, NQ))
                pool.tensor_scalar(LNS[:, :], lsum.bitcast(I32), LN_SLOPE, LN_BASE, ALU.mult, ALU.add)\
                    .then_inc(seed_ready, 1)
                hold(pool, seed_ready, n + 1)
                if not (isinstance(it, int) and unit(it, k) == 0):
                    hold(pool, c_rows_ready, n)
                pool.tensor_tensor(cc, NEGM[:, par, :], LNS[:, :], ALU.add).then_inc(c_chain, 1)
                hold(pool, seed_exp, n + 1)
                pool.tensor_tensor(t, lsum, LEX[:, :], ALU.mult).then_inc(c_chain, 1)
                hold(pool, c_chain, unit(it, k, 11, 2))
                pool.tensor_scalar(t, t, -1.0, None, ALU.add).then_inc(c_chain, 1)
                hold(pool, c_chain, unit(it, k, 11, 3))
                pool.tensor_scalar(a, t, -1 / 3, 0.5, ALU.mult, ALU.add).then_inc(c_chain, 1)
                hold(pool, c_chain, unit(it, k, 11, 4))
                pool.tensor_tensor(a, a, t, ALU.mult).then_inc(c_chain, 1)
                hold(pool, c_chain, unit(it, k, 11, 5))
                pool.tensor_scalar(a, a, -1.0, None, ALU.add).then_inc(c_chain, 1)
                hold(pool, c_chain, unit(it, k, 11, 6))
                pool.tensor_tensor(a, a, t, ALU.mult).then_inc(c_chain, 1)
                hold(pool, c_chain, unit(it, k, 11, 7))
                pool.tensor_tensor(cc, cc, a, ALU.add).then_inc(c_chain, 1)
                hold(pool, c_chain, unit(it, k, 11, 8))
                pool.tensor_copy(C3[:, :, 0], cc).then_inc(c_chain, 1)
                hold(pool, c_chain, unit(it, k, 11, 9))
                pool.tensor_tensor(t, cc, C3[:, :, 0], ALU.subtract).then_inc(c_chain, 1)
                hold(pool, c_chain, unit(it, k, 11, 10))
                pool.tensor_copy(C3[:, :, 1], t).then_inc(c_chain, 1)
                hold(pool, c_chain, unit(it, k, 11, 11))
                pool.tensor_tensor(C3[:, :, 2], t, C3[:, :, 1], ALU.subtract).then_inc(c_parts_ready, 1)

            pool.wait_ge(sw_loaded, 16 * 10)
            for places, high, left in ((WG, SWGH, SWGL), (WU, SWUH, SWUL)):
                for r in range(SLOTS):
                    a, f0 = r // 2, r % 2 * (FS // 2)
                    w = places[r][:, :, :].rearrange("p a f -> p (a f)")
                    h = high[:, a, f0:f0 + FS // 2]
                    link(pool.tensor_copy(h, w))
                    pool.tensor_tensor(left[:, a, f0:f0 + FS // 2], w, h.bitcast(F32), ALU.subtract)\
                        .then_inc(sw_split, 1)
            pool.wait_ge(dest_ready, 1)
            pool.wait_ge(table_cleared, 16)
            for t in range(NT):
                for kk in range(TOPK):
                    pool.indirect_dma_start(
                        out=slot_table, out_offset=bass.IndirectOffsetOnAxis(ap=DI[:, kk, t:t + 1], axis=0),
                        in_=RWS[:, t, kk, :], in_offset=None, bounds_check=CAP * E - 1, oob_is_err=False)\
                        .then_inc(scattered, 16)
            pool.wait_ge(scattered, 16 * NT * TOPK)
            pool.dma_start(TABS[:, :], slot_table.rearrange("(c e) w -> c (e w)", e=E)).then_inc(table_loaded, 16)
            chain(0, 0)
            pool.wait_ge(table_loaded, 16)
            pool.wait_ge(xf_stored, 16)
            pool.wait_ge(moe_started, 32)
            for n in range(V0, V0 + 8):
                pool.wait_ge(pro_free[n % 8], n // 8 + 1)

            def sbuf_cols(tile, start, n):
                return tile[:, start:start + n] if isinstance(start, int) else tile[:, bass.ds(start, n)]

            def prepare(it, k):
                slot, par = k % SLOTS, k % 2
                if k >= 2:
                    hold(pool, pv_done, unit(it, k, NQ, -NQ))
                vflat = VS[:, :, :].rearrange("p u n -> p (u n)")
                pool.tensor_copy(VH[:, par, :, 0:DH],
                                 sbuf_cols(vflat, unit(it, k, NQ * DH), NQ * DH)
                                 .rearrange("p (t d) -> p t d", d=DH)).then_inc(v_ready, 1)
                pool.tensor_copy(IDX[:, slot, :], sbuf_cols(TABS, unit(it, k, 4), 4)).then_inc(idx_ready, 1)
                hold(pool, idx_ready, unit(it, k, 1, 1))
                if k >= 2:
                    hold(pool, xet_ready, unit(it, k, 1, -1))
                pool.indirect_dma_start(
                    out=XE[:, par, :], out_offset=None, in_=xf_rows,
                    in_offset=bass.IndirectOffsetOnAxis(ap=IDX[:, slot, 0:1].bitcast(U32), axis=0),
                    bounds_check=T - 1, oob_is_err=False).then_inc(xe_loaded[par], 16)

            def copy_block(it, k):
                c0 = turn(it, k, SLOTS, BLK)
                src = XFT[:, :, c0:c0 + BLK] if isinstance(c0, int) else XFT[:, :, bass.ds(c0, BLK)]
                pool.tensor_copy(XFH[:, :, :], src).then_inc(block_ready, 1)
                hold(pool, block_ready, turn(it, k, SLOTS, 2, 1))
                pool.tensor_tensor(XFL[:, :, :], src, XFH[:, :, :].bitcast(F32), ALU.subtract).then_inc(block_ready, 1)

            def copy_scales(it, k):
                if k >= SLOTS:
                    hold(pool, *aux_done(it, k - 1, SB))
                pool.tensor_copy(SGB[:, :], sbuf_cols(SG, turn(it, k, SLOTS, 2), 2)).then_inc(scale_ready, 1)

            def scatter(it, k):
                slot, par = k % SLOTS, k % 2
                hold(pool, ye_ready, unit(it, k, 1, 1))
                if k >= 1:
                    hold(pool, moe_added, unit(it, k, 16))
                pool.sem_inc(ye_free, 1)
                pool.indirect_dma_start(
                    out=moe_rows, out_offset=bass.IndirectOffsetOnAxis(ap=IDX[:, slot, 2:3].bitcast(U32), axis=0),
                    in_=YE[:, par, :], in_offset=None, bounds_check=T + CAP - 1, oob_is_err=True,
                    compute_op=ALU.add).then_inc(moe_added, 16)

            prepare(0, 0)
            copy_block(0, 0)

            def phase(it, k, first, ahead):
                last = is_last(it, k)
                if not last:
                    chain(it, k + 1)
                if not first:
                    scatter(it, k - 1)
                if not last:
                    prepare(it, k + 1)
                if k % SLOTS == 0:
                    copy_scales(it, k)
                if k % SLOTS == SLOTS - 1 and not last:
                    b, before = aux(it, k - 1, SB)
                    hold(pool, aux_ready[b], before + 1)
                    copy_block(it, k + 1)

            phases(pool, phase)
            scatter(UNITS // SLOTS - 1, SLOTS - 1)
            pool.wait_ge(x_again, 16)
            ef = XFT[:, :, :].rearrange("p c n -> p (c n)")
            for g in range(NT // 2):
                c = slice(512 * g, 512 * (g + 1))
                pool.wait_ge(fin_product, g + 1)
                pool.tensor_tensor(xagain[:, c], xagain[:, c], ef[:, c], ALU.add).then_inc(fin_out, 1)


_INS = ['L0_attn_qkv', 'L0_attn_in_proj', 'L0_attn_in_proj_bias', 'L0_attn_out_w', 'L0_attn_out_b',
        'L0_attn_alibi_slopes', 'L0_ffn_w_norm', 'L0_ffn_w_router', 'L0_ffn_w_gate', 'L0_ffn_w_up',
        'L0_ffn_w_down', 'L0_ffn_sw_gate', 'L0_ffn_sw_up', 'L0_ffn_sw_down', 'L0_ffn_w_shared_gate']


def kernel(**inputs):
    import numpy as _np
    import concourse.bacc as _bacc
    from concourse import mybir as _mybir
    from concourse.bass_utils import run_bass_kernel_spmd as _run

    nc = _bacc.Bacc("TRN2", target_bir_lowering=False, num_devices=1)
    arrays, args = {}, []
    for name in _INS:
        a = _np.ascontiguousarray(inputs[name])
        arrays[f"in_{name}_dram"] = a
        args.append(nc.dram_tensor(f"in_{name}_dram", a.shape, _mybir.dt.from_np(a.dtype), kind="ExternalInput").ap())
    args.append(nc.dram_tensor("out_0_dram", (B, S, D), _mybir.dt.float32, kind="ExternalOutput").ap())
    build(nc, *args)
    r = _run(nc, [arrays], core_ids=[0])
    return r.results[0]["out_0_dram"]
```
